# Optimizing a Trainium2 kernel written in Bass

```python
import numpy as np
import jax
import jax.numpy as jnp

def _softmax(x, axis=-1):
    return jax.nn.softmax(x, axis=axis)

def _gelu(x):
    return jax.nn.gelu(x, approximate=True)

def _silu(x):
    return jax.nn.silu(x)

def _sigmoid(x):
    return jax.nn.sigmoid(x)

def _layernorm(x, axis=-1, eps=1e-05):
    m = jnp.mean(x, axis=axis, keepdims=True)
    v = jnp.var(x, axis=axis, keepdims=True)
    return (x - m) / jnp.sqrt(v + eps)

def _scatter_add(tgt, idx, src, axis=0):
    return tgt.at[idx].add(src)

def _segment_sum(src, seg, n):
    return jax.ops.segment_sum(src, seg, n)
kernel_name = 'mk_lm_tower_d2_tok_ids512_r4_9b88ed'

def setup_inputs(seed: int=0):
    np.random.seed(seed)
    _w = jnp.asarray

    def _rec_inputs():
        import jax
        import jax.numpy as jnp
        _rk = jax.random.key(seed)
        x = jax.random.randint(jax.random.fold_in(_rk, 1), (4, 512), 0, 668, jnp.int32)
        return x
    x = _rec_inputs()

    def _L0_tok_setup():
        import jax, jax.numpy as jnp
        import numpy as np
        import math
        D = 128
        CAT_VOCAB = 128
        TIME_START, TIME_STEPS = (128, 250)
        NOTE_START, NOTE_RANGE = (378, 128)
        VEL_START, VEL_BINS = (410, 32)
        DUR_START, DUR_STEPS = (418, 250)
        VOCAB = 668

        def _time2vec(t, max_steps, lin_w, lin_b, w, b):
            tn = t.astype(jnp.float32)[..., None] / max_steps
            linear = tn * lin_w + lin_b
            periodic = jnp.sin(tn * w + b)
            return jnp.concatenate([linear, periodic], axis=-1)

        def _pitch_embed(p):
            pf = p.astype(jnp.float32)
            octave = jnp.floor(pf / 12.0)
            semitone = jnp.mod(pf, 12.0)
            i = jnp.arange(D // 4, dtype=jnp.float32)
            div = 2.0 ** i
            ph_oct = octave[..., None] / div
            ph_sem = semitone[..., None] * (math.pi / 6.0) * (i + 1.0)
            emb = jnp.stack([jnp.sin(ph_oct), jnp.cos(ph_oct), jnp.sin(ph_sem), jnp.cos(ph_sem)], axis=-1)
            return emb.reshape(*p.shape, D)

        def _vel_embed(v, w1, b1, w2, b2, g, beta):
            vn = v.astype(jnp.float32)[..., None] / VEL_BINS
            h = jax.nn.gelu(vn * w1 + b1, approximate=False)
            e = jnp.einsum('bsh,dh->bsd', h, w2) + b2
            mu = e.mean(-1, keepdims=True)
            var = ((e - mu) ** 2).mean(-1, keepdims=True)
            return g * (e - mu) / jnp.sqrt(var + 1e-05) + beta
        key = jax.random.key(seed)
        ks = jax.random.split(key, 16)
        tokens = jax.random.randint(ks[0], (8, 2048), 0, VOCAB)
        token_emb = jax.random.normal(ks[1], (CAT_VOCAB, D), jnp.float32) * 0.02
        token_emb = token_emb.at[0].set(0.0)
        return {'tokens': tokens, 'token_emb': token_emb, 'time_lin_w': jax.random.normal(ks[2], (D // 2,), jnp.float32), 'time_lin_b': jax.random.normal(ks[3], (D // 2,), jnp.float32), 'time_w': jax.random.normal(ks[4], (D // 2,), jnp.float32), 'time_b': jax.random.normal(ks[5], (D // 2,), jnp.float32), 'vel_w1': jax.random.normal(ks[6], (D // 2,), jnp.float32), 'vel_b1': jax.random.normal(ks[7], (D // 2,), jnp.float32), 'vel_w2': jax.random.normal(ks[8], (D, D // 2), jnp.float32) * 0.05, 'vel_b2': jax.random.normal(ks[9], (D,), jnp.float32), 'vel_ln_g': jnp.ones((D,), jnp.float32), 'vel_ln_b': jnp.zeros((D,), jnp.float32), 'dur_lin_w': jax.random.normal(ks[10], (D // 2,), jnp.float32), 'dur_lin_b': jax.random.normal(ks[11], (D // 2,), jnp.float32), 'dur_w': jax.random.normal(ks[12], (D // 2,), jnp.float32), 'dur_b': jax.random.normal(ks[13], (D // 2,), jnp.float32)}
    _L0_tok_all = _L0_tok_setup()
    _L0_tok_in = {k: v for k, v in _L0_tok_all.items() if k in ('token_emb', 'time_lin_w', 'time_lin_b', 'time_w', 'time_b', 'vel_w1', 'vel_b1', 'vel_w2', 'vel_b2', 'vel_ln_g', 'vel_ln_b', 'dur_lin_w', 'dur_lin_b', 'dur_w', 'dur_b')}
    del _L0_tok_all

    def _L0_attn_setup():
        import jax, jax.numpy as jnp
        import numpy as np
        K = 128
        H = 8
        key = jax.random.key(seed)
        k1, k2, k3, k4, k5 = jax.random.split(key, 5)
        b, s = (2, 512)
        x = jax.random.normal(k1, (b, s, K), dtype=jnp.float32)
        scale = 0.02
        Wq = jax.random.normal(k2, (H * K, K), dtype=jnp.float32) * scale
        Wk = jax.random.normal(k3, (H * K, K), dtype=jnp.float32) * scale
        Wv = jax.random.normal(k4, (H * K, K), dtype=jnp.float32) * scale
        Wu = jax.random.normal(k5, (K, H * K), dtype=jnp.float32) * scale
        return {'x': x, 'Wq': Wq, 'Wk': Wk, 'Wv': Wv, 'Wu': Wu}
    _L0_attn_all = _L0_attn_setup()
    _L0_attn_in = {k: v for k, v in _L0_attn_all.items() if k in ('Wq', 'Wk', 'Wv', 'Wu')}
    del _L0_attn_all

    def _L0_ffn_setup():
        import jax, jax.numpy as jnp
        import numpy as np
        B, S, D, F, E = (8, 1024, 128, 512, 8)
        INIT_LAMBDA = 0.2
        LN_EPS = 1e-05
        LN_MERGE = 0.03
        key = jax.random.key(seed)
        ks = jax.random.split(key, 12)
        n = lambda k, shp, s=1.0: jax.random.normal(k, shp, dtype=jnp.float32) * s
        return {'hidden_states': n(ks[0], (B, S, D)), 'gfc1_w': n(ks[1], (D, D), 0.01), 'gfc1_b': jnp.zeros((D,), jnp.float32), 'gfc2_w': n(ks[2], (E, D), 0.01), 'gfc2_b': jnp.full((E,), INIT_LAMBDA, dtype=jnp.float32), 'W1': n(ks[3], (F, D), 0.02), 'b1': jnp.zeros((F,), jnp.float32), 'W2': n(ks[4], (D, F), 0.02), 'b2': jnp.zeros((D,), jnp.float32), 'ln_g': jnp.ones((D,), jnp.float32), 'ln_b': jnp.zeros((D,), jnp.float32), 'tv_W1': n(ks[5], (E, F, D), 0.02), 'tv_b1': n(ks[6], (E, F), 0.02), 'tv_W2': n(ks[7], (E, D, F), 0.02), 'tv_b2': n(ks[8], (E, D), 0.02), 'tv_ln_g': n(ks[9], (E, D), 0.02), 'tv_ln_b': n(ks[10], (E, D), 0.02)}
    _L0_ffn_all = _L0_ffn_setup()
    _L0_ffn_in = {k: v for k, v in _L0_ffn_all.items() if k in ('gfc1_w', 'gfc1_b', 'gfc2_w', 'gfc2_b', 'W1', 'b1', 'W2', 'b2', 'ln_g', 'ln_b', 'tv_W1', 'tv_b1', 'tv_W2', 'tv_b2', 'tv_ln_g', 'tv_ln_b')}
    del _L0_ffn_all

    def _L1_attn_setup():
        import jax, jax.numpy as jnp
        import numpy as np
        HIGHEST = jax.lax.Precision.HIGHEST
        KEY_CHUNK_SIZE = 1024 * 4
        HEADS = 8
        DIM_HEAD = 64

        def _query_chunk_size(num_q: int) -> int:
            if num_q % 64 == 0:
                return num_q // 64
            if num_q % 16 == 0:
                return num_q // 16
            if num_q % 4 == 0:
                return num_q // 4
            return num_q

        def _me_attention(q, k, v, q_chunk: int, k_chunk: int):
            S, H, D = q.shape
            num_kv = k.shape[0]
            k_chunk = min(k_chunk, num_kv)
            q = q / jnp.sqrt(jnp.asarray(D, q.dtype))
            kc = k.reshape(-1, k_chunk, H, D)
            vc = v.reshape(-1, k_chunk, H, v.shape[-1])

            def per_qchunk(qch):

                def summarize(args):
                    kch, vch = args
                    s = jnp.einsum('qhd,khd->qhk', qch, kch, precision=HIGHEST)
                    m = jax.lax.stop_gradient(jnp.max(s, axis=-1, keepdims=True))
                    e = jnp.exp(s - m)
                    ev = jnp.einsum('khf,qhk->qhf', vch, e, precision=HIGHEST)
                    return (ev, e.sum(axis=-1), m[..., 0])
                evs, ews, ms = jax.lax.map(summarize, (kc, vc))
                gm = jnp.max(ms, axis=0)
                sc = jnp.exp(ms - gm)
                num = (evs * sc[..., None]).sum(axis=0)
                den = (ews * sc).sum(axis=0)
                return num / den[..., None]
            qs = q.reshape(-1, q_chunk, H, D)
            out = jax.lax.map(per_qchunk, qs)
            return out.reshape(S, H, -1)

        def _forward(hidden_states, w_q, w_k, w_v, w_out, b_out):
            B, S, Dm = hidden_states.shape
            H, dh = (HEADS, DIM_HEAD)
            q = hidden_states @ w_q
            k = hidden_states @ w_k
            v = hidden_states @ w_v

            def to_heads(t):
                return t.reshape(B, S, H, dh).transpose(0, 2, 1, 3).reshape(B * H, S, dh)
            qs, ks, vs = (to_heads(q), to_heads(k), to_heads(v))
            qcs = _query_chunk_size(S)
            attn = _me_attention(qs.transpose(1, 0, 2), ks.transpose(1, 0, 2), vs.transpose(1, 0, 2), qcs, KEY_CHUNK_SIZE)
            attn = attn.transpose(1, 0, 2)
            attn = attn.reshape(B, H, S, dh).transpose(0, 2, 1, 3).reshape(B, S, H * dh)
            return attn @ w_out + b_out
        key = jax.random.key(seed)
        ks = jax.random.split(key, 6)
        B, S, Dm = (2, 2048, 128)
        inner = HEADS * DIM_HEAD
        return {'hidden_states': jax.random.normal(ks[0], (B, S, Dm), dtype=jnp.float32), 'w_q': jax.random.normal(ks[1], (Dm, inner), dtype=jnp.float32) * 0.02, 'w_k': jax.random.normal(ks[2], (Dm, inner), dtype=jnp.float32) * 0.02, 'w_v': jax.random.normal(ks[3], (Dm, inner), dtype=jnp.float32) * 0.02, 'w_out': jax.random.normal(ks[4], (inner, Dm), dtype=jnp.float32) * 0.02, 'b_out': jnp.zeros((Dm,), dtype=jnp.float32)}
    _L1_attn_all = _L1_attn_setup()
    _L1_attn_in = {k: v for k, v in _L1_attn_all.items() if k in ('w_q', 'w_k', 'w_v', 'w_out', 'b_out')}
    del _L1_attn_all

    def _L1_ffn_setup():
        import jax, jax.numpy as jnp
        import numpy as np
        B, T, DIM = (2, 64, 128)
        E, H, K = (64, 256, 42)
        key = jax.random.key(seed)
        ks = jax.random.split(key, 7)
        s1 = 1.0 / np.sqrt(DIM).astype(np.float32)
        s2 = 1.0 / np.sqrt(H).astype(np.float32)
        return {'x': jax.random.normal(ks[0], (B, T, DIM), jnp.float32), 'w1': jax.random.uniform(ks[1], (E, DIM, H), jnp.float32, -s1, s1), 'b1': jax.random.uniform(ks[2], (E, H), jnp.float32, -s1, s1), 'w2': jax.random.uniform(ks[3], (E, H, DIM), jnp.float32, -s2, s2), 'b2': jax.random.uniform(ks[4], (E, DIM), jnp.float32, -s2, s2), 'router_w': jax.random.uniform(ks[5], (DIM, E), jnp.float32, -s1, s1), 'router_b': jax.random.uniform(ks[6], (E,), jnp.float32, -s1, s1)}
    _L1_ffn_all = _L1_ffn_setup()
    _L1_ffn_in = {k: v for k, v in _L1_ffn_all.items() if k in ('w1', 'b1', 'w2', 'b2', 'router_w', 'router_b')}
    del _L1_ffn_all
    return {'x': x, 'L0_tok_token_emb': _L0_tok_in['token_emb'], 'L0_tok_time_lin_w': _L0_tok_in['time_lin_w'], 'L0_tok_time_lin_b': _L0_tok_in['time_lin_b'], 'L0_tok_time_w': _L0_tok_in['time_w'], 'L0_tok_time_b': _L0_tok_in['time_b'], 'L0_tok_vel_w1': _L0_tok_in['vel_w1'], 'L0_tok_vel_b1': _L0_tok_in['vel_b1'], 'L0_tok_vel_w2': _L0_tok_in['vel_w2'], 'L0_tok_vel_b2': _L0_tok_in['vel_b2'], 'L0_tok_vel_ln_g': _L0_tok_in['vel_ln_g'], 'L0_tok_vel_ln_b': _L0_tok_in['vel_ln_b'], 'L0_tok_dur_lin_w': _L0_tok_in['dur_lin_w'], 'L0_tok_dur_lin_b': _L0_tok_in['dur_lin_b'], 'L0_tok_dur_w': _L0_tok_in['dur_w'], 'L0_tok_dur_b': _L0_tok_in['dur_b'], 'L0_attn_Wq': _L0_attn_in['Wq'], 'L0_attn_Wk': _L0_attn_in['Wk'], 'L0_attn_Wv': _L0_attn_in['Wv'], 'L0_attn_Wu': _L0_attn_in['Wu'], 'L0_ffn_gfc1_w': _L0_ffn_in['gfc1_w'], 'L0_ffn_gfc1_b': _L0_ffn_in['gfc1_b'], 'L0_ffn_gfc2_w': _L0_ffn_in['gfc2_w'], 'L0_ffn_gfc2_b': _L0_ffn_in['gfc2_b'], 'L0_ffn_W1': _L0_ffn_in['W1'], 'L0_ffn_b1': _L0_ffn_in['b1'], 'L0_ffn_W2': _L0_ffn_in['W2'], 'L0_ffn_b2': _L0_ffn_in['b2'], 'L0_ffn_ln_g': _L0_ffn_in['ln_g'], 'L0_ffn_ln_b': _L0_ffn_in['ln_b'], 'L0_ffn_tv_W1': _L0_ffn_in['tv_W1'], 'L0_ffn_tv_b1': _L0_ffn_in['tv_b1'], 'L0_ffn_tv_W2': _L0_ffn_in['tv_W2'], 'L0_ffn_tv_b2': _L0_ffn_in['tv_b2'], 'L0_ffn_tv_ln_g': _L0_ffn_in['tv_ln_g'], 'L0_ffn_tv_ln_b': _L0_ffn_in['tv_ln_b'], 'L1_attn_w_q': _L1_attn_in['w_q'], 'L1_attn_w_k': _L1_attn_in['w_k'], 'L1_attn_w_v': _L1_attn_in['w_v'], 'L1_attn_w_out': _L1_attn_in['w_out'], 'L1_attn_b_out': _L1_attn_in['b_out'], 'L1_ffn_w1': _L1_ffn_in['w1'], 'L1_ffn_b1': _L1_ffn_in['b1'], 'L1_ffn_w2': _L1_ffn_in['w2'], 'L1_ffn_b2': _L1_ffn_in['b2'], 'L1_ffn_router_w': _L1_ffn_in['router_w'], 'L1_ffn_router_b': _L1_ffn_in['router_b']}

def reference(x, L0_tok_token_emb, L0_tok_time_lin_w, L0_tok_time_lin_b, L0_tok_time_w, L0_tok_time_b, L0_tok_vel_w1, L0_tok_vel_b1, L0_tok_vel_w2, L0_tok_vel_b2, L0_tok_vel_ln_g, L0_tok_vel_ln_b, L0_tok_dur_lin_w, L0_tok_dur_lin_b, L0_tok_dur_w, L0_tok_dur_b, L0_attn_Wq, L0_attn_Wk, L0_attn_Wv, L0_attn_Wu, L0_ffn_gfc1_w, L0_ffn_gfc1_b, L0_ffn_gfc2_w, L0_ffn_gfc2_b, L0_ffn_W1, L0_ffn_b1, L0_ffn_W2, L0_ffn_b2, L0_ffn_ln_g, L0_ffn_ln_b, L0_ffn_tv_W1, L0_ffn_tv_b1, L0_ffn_tv_W2, L0_ffn_tv_b2, L0_ffn_tv_ln_g, L0_ffn_tv_ln_b, L1_attn_w_q, L1_attn_w_k, L1_attn_w_v, L1_attn_w_out, L1_attn_b_out, L1_ffn_w1, L1_ffn_b1, L1_ffn_w2, L1_ffn_b2, L1_ffn_router_w, L1_ffn_router_b):
    import jax
    import jax.numpy as jnp

    def _L0_tok_ref(tokens, token_emb, time_lin_w, time_lin_b, time_w, time_b, vel_w1, vel_b1, vel_w2, vel_b2, vel_ln_g, vel_ln_b, dur_lin_w, dur_lin_b, dur_w, dur_b):
        import jax, jax.numpy as jnp
        import numpy as np
        import math
        D = 128
        CAT_VOCAB = 128
        TIME_START, TIME_STEPS = (128, 250)
        NOTE_START, NOTE_RANGE = (378, 128)
        VEL_START, VEL_BINS = (410, 32)
        DUR_START, DUR_STEPS = (418, 250)
        VOCAB = 668

        def _time2vec(t, max_steps, lin_w, lin_b, w, b):
            tn = t.astype(jnp.float32)[..., None] / max_steps
            linear = tn * lin_w + lin_b
            periodic = jnp.sin(tn * w + b)
            return jnp.concatenate([linear, periodic], axis=-1)

        def _pitch_embed(p):
            pf = p.astype(jnp.float32)
            octave = jnp.floor(pf / 12.0)
            semitone = jnp.mod(pf, 12.0)
            i = jnp.arange(D // 4, dtype=jnp.float32)
            div = 2.0 ** i
            ph_oct = octave[..., None] / div
            ph_sem = semitone[..., None] * (math.pi / 6.0) * (i + 1.0)
            emb = jnp.stack([jnp.sin(ph_oct), jnp.cos(ph_oct), jnp.sin(ph_sem), jnp.cos(ph_sem)], axis=-1)
            return emb.reshape(*p.shape, D)

        def _vel_embed(v, w1, b1, w2, b2, g, beta):
            vn = v.astype(jnp.float32)[..., None] / VEL_BINS
            h = jax.nn.gelu(vn * w1 + b1, approximate=False)
            e = jnp.einsum('bsh,dh->bsd', h, w2) + b2
            mu = e.mean(-1, keepdims=True)
            var = ((e - mu) ** 2).mean(-1, keepdims=True)
            return g * (e - mu) / jnp.sqrt(var + 1e-05) + beta
        cat_mask = tokens < CAT_VOCAB
        time_mask = (tokens >= TIME_START) & (tokens < TIME_START + TIME_STEPS)
        note_mask = (tokens >= NOTE_START) & (tokens < NOTE_START + NOTE_RANGE)
        vel_mask = (tokens >= VEL_START) & (tokens < VEL_START + VEL_BINS)
        dur_mask = (tokens >= DUR_START) & (tokens < DUR_START + DUR_STEPS)
        safe_idx = jnp.clip(tokens, 0, CAT_VOCAB - 1)
        out = jnp.where(cat_mask[..., None], token_emb[safe_idx], 0.0)
        t_emb = _time2vec(tokens - TIME_START, float(TIME_STEPS), time_lin_w, time_lin_b, time_w, time_b)
        p_emb = _pitch_embed(tokens - NOTE_START)
        v_emb = _vel_embed(tokens - VEL_START, vel_w1, vel_b1, vel_w2, vel_b2, vel_ln_g, vel_ln_b)
        d_emb = _time2vec(tokens - DUR_START, float(DUR_STEPS), dur_lin_w, dur_lin_b, dur_w, dur_b)
        out = jnp.where(time_mask[..., None], t_emb, out)
        out = jnp.where(note_mask[..., None], p_emb, out)
        out = jnp.where(vel_mask[..., None], v_emb, out)
        out = jnp.where(dur_mask[..., None], d_emb, out)
        return out

    def _L0_attn_ref(x, Wq, Wk, Wv, Wu):
        import jax, jax.numpy as jnp
        import numpy as np
        K = 128
        H = 8
        b, s, _ = x.shape
        q = jnp.einsum('bsd,hed->bhse', x, Wq.reshape(H, K, K))
        kk = jnp.einsum('bsd,hed->bhse', x, Wk.reshape(H, K, K))
        v = jnp.einsum('bsd,hed->bhse', x, Wv.reshape(H, K, K))
        scale = K ** (-0.25)
        dot = jnp.einsum('bhse,bhte->bhst', q * scale, kk * scale)
        causal = jnp.tril(jnp.ones((s, s), dtype=bool))
        dot = jnp.where(causal[None, None], dot, -jnp.inf)
        weights = jax.nn.softmax(dot, axis=-1)
        heads_out = jnp.einsum('bhst,bhte->bhse', weights, v)
        heads_out = heads_out.transpose(0, 2, 1, 3).reshape(b, s, H * K)
        return heads_out @ Wu.T

    def _L0_ffn_ref(hidden_states, gfc1_w, gfc1_b, gfc2_w, gfc2_b, W1, b1, W2, b2, ln_g, ln_b, tv_W1, tv_b1, tv_W2, tv_b2, tv_ln_g, tv_ln_b):
        import jax, jax.numpy as jnp
        import numpy as np
        B, S, D, F, E = (8, 1024, 128, 512, 8)
        INIT_LAMBDA = 0.2
        LN_EPS = 1e-05
        LN_MERGE = 0.03
        x = hidden_states
        gh = jax.nn.relu(jnp.einsum('bsd,hd->bsh', x, gfc1_w) + gfc1_b)
        g = (jnp.einsum('bsh,eh->bse', gh, gfc2_w) + gfc2_b).mean(axis=1)
        W1m = W1 + jnp.einsum('be,efd->bfd', g, tv_W1)
        b1m = b1 + g @ tv_b1
        W2m = W2 + jnp.einsum('be,edf->bdf', g, tv_W2)
        b2m = b2 + g @ tv_b2
        lng = ln_g + LN_MERGE * (tv_ln_g - ln_g).sum(axis=0)
        lnb = ln_b + LN_MERGE * (tv_ln_b - ln_b).sum(axis=0)
        h = jax.nn.relu(jnp.einsum('bsd,bfd->bsf', x, W1m) + b1m[:, None, :])
        out = jnp.einsum('bsf,bdf->bsd', h, W2m) + b2m[:, None, :]
        res = x + out
        mu = res.mean(axis=-1, keepdims=True)
        var = res.var(axis=-1, keepdims=True)
        return (res - mu) * jax.lax.rsqrt(var + LN_EPS) * lng + lnb

    def _L1_attn_ref(hidden_states, w_q, w_k, w_v, w_out, b_out):
        import jax, jax.numpy as jnp
        import numpy as np
        HIGHEST = jax.lax.Precision.HIGHEST
        KEY_CHUNK_SIZE = 1024 * 4
        HEADS = 8
        DIM_HEAD = 64

        def _query_chunk_size(num_q: int) -> int:
            if num_q % 64 == 0:
                return num_q // 64
            if num_q % 16 == 0:
                return num_q // 16
            if num_q % 4 == 0:
                return num_q // 4
            return num_q

        def _me_attention(q, k, v, q_chunk: int, k_chunk: int):
            S, H, D = q.shape
            num_kv = k.shape[0]
            k_chunk = min(k_chunk, num_kv)
            q = q / jnp.sqrt(jnp.asarray(D, q.dtype))
            kc = k.reshape(-1, k_chunk, H, D)
            vc = v.reshape(-1, k_chunk, H, v.shape[-1])

            def per_qchunk(qch):

                def summarize(args):
                    kch, vch = args
                    s = jnp.einsum('qhd,khd->qhk', qch, kch, precision=HIGHEST)
                    m = jax.lax.stop_gradient(jnp.max(s, axis=-1, keepdims=True))
                    e = jnp.exp(s - m)
                    ev = jnp.einsum('khf,qhk->qhf', vch, e, precision=HIGHEST)
                    return (ev, e.sum(axis=-1), m[..., 0])
                evs, ews, ms = jax.lax.map(summarize, (kc, vc))
                gm = jnp.max(ms, axis=0)
                sc = jnp.exp(ms - gm)
                num = (evs * sc[..., None]).sum(axis=0)
                den = (ews * sc).sum(axis=0)
                return num / den[..., None]
            qs = q.reshape(-1, q_chunk, H, D)
            out = jax.lax.map(per_qchunk, qs)
            return out.reshape(S, H, -1)

        def _forward(hidden_states, w_q, w_k, w_v, w_out, b_out):
            B, S, Dm = hidden_states.shape
            H, dh = (HEADS, DIM_HEAD)
            q = hidden_states @ w_q
            k = hidden_states @ w_k
            v = hidden_states @ w_v

            def to_heads(t):
                return t.reshape(B, S, H, dh).transpose(0, 2, 1, 3).reshape(B * H, S, dh)
            qs, ks, vs = (to_heads(q), to_heads(k), to_heads(v))
            qcs = _query_chunk_size(S)
            attn = _me_attention(qs.transpose(1, 0, 2), ks.transpose(1, 0, 2), vs.transpose(1, 0, 2), qcs, KEY_CHUNK_SIZE)
            attn = attn.transpose(1, 0, 2)
            attn = attn.reshape(B, H, S, dh).transpose(0, 2, 1, 3).reshape(B, S, H * dh)
            return attn @ w_out + b_out
        return _forward(hidden_states, w_q, w_k, w_v, w_out, b_out)

    def _L1_ffn_ref(x, w1, b1, w2, b2, router_w, router_b):
        import jax, jax.numpy as jnp
        import numpy as np
        B, T, DIM = (2, 64, 128)
        E, H, K = (64, 256, 42)
        Bb, Tt, C = x.shape
        N = Bb * Tt
        logits = x @ router_w + router_b
        probs = jax.nn.softmax(logits, axis=-1)
        top_w, top_idx = jax.lax.top_k(probs, K)
        top_w = jax.nn.softmax(top_w, axis=-1)
        xt = x.reshape(N, C)
        top_w = top_w.reshape(N, K)
        top_idx = top_idx.reshape(N, K)
        comb = jnp.zeros((N, E), x.dtype).at[jnp.arange(N)[:, None], top_idx].set(top_w)
        h = jax.nn.gelu(jnp.einsum('td,edh->teh', xt, w1) + b1, approximate=False)
        y = jnp.einsum('teh,ehd->ted', h, w2) + b2
        out = jnp.einsum('ted,te->td', y, comb)
        return out.reshape(Bb, Tt, C)
    h = _L0_tok_ref(x, L0_tok_token_emb, L0_tok_time_lin_w, L0_tok_time_lin_b, L0_tok_time_w, L0_tok_time_b, L0_tok_vel_w1, L0_tok_vel_b1, L0_tok_vel_w2, L0_tok_vel_b2, L0_tok_vel_ln_g, L0_tok_vel_ln_b, L0_tok_dur_lin_w, L0_tok_dur_lin_b, L0_tok_dur_w, L0_tok_dur_b)
    h = h + _L0_attn_ref(_layernorm(h, axis=-1), L0_attn_Wq, L0_attn_Wk, L0_attn_Wv, L0_attn_Wu)
    h = h + _L0_ffn_ref(_layernorm(h, axis=-1), L0_ffn_gfc1_w, L0_ffn_gfc1_b, L0_ffn_gfc2_w, L0_ffn_gfc2_b, L0_ffn_W1, L0_ffn_b1, L0_ffn_W2, L0_ffn_b2, L0_ffn_ln_g, L0_ffn_ln_b, L0_ffn_tv_W1, L0_ffn_tv_b1, L0_ffn_tv_W2, L0_ffn_tv_b2, L0_ffn_tv_ln_g, L0_ffn_tv_ln_b)
    h = h + _L1_attn_ref(_layernorm(h, axis=-1), L1_attn_w_q, L1_attn_w_k, L1_attn_w_v, L1_attn_w_out, L1_attn_b_out)
    h = h + _L1_ffn_ref(_layernorm(h, axis=-1), L1_ffn_w1, L1_ffn_b1, L1_ffn_w2, L1_ffn_b2, L1_ffn_router_w, L1_ffn_router_b)
    return h

_drawn_inputs = setup_inputs


def setup_inputs(seed=0):
    import zlib

    import numpy as np

    out = dict(_drawn_inputs(seed))
    spreads = {'L0_tok_vel_ln_g': (1.0, 0.6),
     'L0_tok_vel_ln_b': (0.0, 0.702),
     'L0_ffn_gfc1_b': (0.0, 0.8),
     'L0_ffn_gfc2_b': (0.20000000298023224, 0.6),
     'L0_ffn_b1': (0.0, 0.471),
     'L0_ffn_b2': (0.0, 0.1),
     'L0_ffn_ln_g': (1.0, 0.2),
     'L0_ffn_ln_b': (0.0, 0.1),
     'L1_attn_b_out': (0.0, 0.1)}
    factors = {'L0_tok_vel_w1': 8.0,
     'L0_attn_Wq': 5.506,
     'L0_attn_Wk': 5.739,
     'L0_ffn_gfc1_w': 8.0,
     'L0_ffn_gfc2_w': 8.0,
     'L0_ffn_tv_W1': 2.892,
     'L0_ffn_tv_b1': 8.0,
     'L0_ffn_tv_b2': 8.0,
     'L0_ffn_tv_ln_g': 27.406,
     'L0_ffn_tv_ln_b': 28.601,
     'L1_attn_w_q': 8.0,
     'L1_attn_w_k': 8.0,
     'L1_ffn_w1': 3.342,
     'L1_ffn_b1': 8.0,
     'L1_ffn_w2': 3.139,
     'L1_ffn_b2': 8.0,
     'L1_ffn_router_w': 5.061,
     'L1_ffn_router_b': 8.0}
    for name, (base, spread) in spreads.items():
        noise = np.random.default_rng([zlib.crc32(name.encode()), seed]).standard_normal(out[name].shape)
        drawn = base * np.exp(spread * noise) if base else spread * noise
        out[name] = jnp.asarray(drawn.astype(out[name].dtype))
    for name, factor in factors.items():
        out[name] = (out[name] * factor).astype(out[name].dtype)
    return out
```

```python
import math

import concourse.bass as bass
from concourse import mybir
from contextlib import ExitStack

F32 = mybir.dt.float32
F32R = mybir.dt.float32r
BF16 = mybir.dt.bfloat16
I32 = mybir.dt.int32
ALU = mybir.AluOpType
ACT = mybir.ActivationFunctionType
AX = mybir.AxisListType

B, S, D = 4, 512, 128
T = B * S
NC = T // 512
H = 8
DH1 = 64
F0 = 512
E0 = 8
E, HF, TOPK = 64, 256, 42
DROP = E - TOPK
PADS = -DROP % 8
VC = 6
LN_EPS = 1e-5
LAG = 3
P0 = 4 * F0 // 2 + 5

C_ID, C_ONES, C_MASK = 0, 128, 256
C_IDX, C_POS, C_POW, C_INC, C_VN, C_TN = 384, 390, 392, 424, 456, 496
C_ALL = 498
R_LW, R_LB, R_W, R_B, R_B2, R_G, R_BETA, R_ALL = 0, 128, 256, 384, 512, 640, 768, 896
K_VW1, K_VB1, K_GB1, K_LNG, K_LNB, K_TVG, K_TVB, K_BOUT, K_ALL = 0, 1, 2, 3, 4, 5, 13, 21, 22


def vocabulary_tower(nc, tok, consts, rows, cols, emb, vel_w2t, a0, gfc1t, gfc2t, gfc2b, ffn, a1, rw, rb, ew, eb2,
                     comb_dram, out):
    ctx = ExitStack()
    with ctx:
        def sb(name, shape, dt):
            return ctx.enter_context(nc.sbuf_tensor(name, shape, dt))

        def sem(name):
            return ctx.enter_context(nc.semaphore(name))

        HT = sb("residual", [128, T], F32)
        XN = sb("normed", [128, T], F32)
        XHI = sb("normed_hi", [128, T], F32R)
        XLO = sb("normed_lo", [128, T], F32R)
        CS = sb("constants", [128, C_ALL], F32)
        RW_ = sb("row_params", [128, R_ALL], F32)
        CP = sb("col_params", [128, K_ALL], F32)
        V2T = sb("vel_w2t", [64, 128], F32)
        IDB = sb("ident_bf16", [128, 128], BF16)
        MKB = sb("mask_bf16", [128, 128], BF16)
        FA = sb("arena_f32", [128, 21568], F32)
        RA = sb("arena_f32r", [128, 17408], F32R)
        SM = sb("small", [128, 256], F32)

        def fa(at, n):
            return FA[:, at:at + n]

        def ra(at, n):
            return RA[:, at:at + n]

        ident = CS[:, C_ID:C_ID + 128]
        mean_w = CS[:, C_ONES:C_ONES + 128]
        mask = CS[:, C_MASK:C_MASK + 128]
        SQ = [fa(512 * i, 512) for i in range(2)]
        STD = [fa(1024 + 512 * i, 512) for i in range(2)]
        TOKI = fa(2048, 2048).bitcast(I32)
        TOKF = fa(4096, 2048)
        TAB = fa(19501, 768)
        PH = fa(20269, 384)
        KQ = fa(20653, 384)
        VE = fa(21037, 128)
        VH = fa(21165, 40)
        VSQ = fa(21205, 128)
        THI, TLO = ra(0, 768), ra(768, 768)
        OH = [ra(11264 + 2048 * i, 2048) for i in range(2)]
        PB = [fa(2048 + 2048 * i, 2048).rearrange("p (i t) -> p i t", i=4) for i in range(2)]
        WL = fa(6144, 4096).rearrange("p (w c) -> p w c", w=4)
        XTM = ra(0, 4096)
        MN = ra(4096, 4096)
        STAT = [ra(8192 + 1536 * i, 1280) for i in range(2)]
        PST = [ra(9472 + 1536 * i, 256) for i in range(2)]
        QHI = [ra(11264 + 1024 * i, 512) for i in range(2)]
        QLO = [ra(11776 + 1024 * i, 512) for i in range(2)]
        PTHI = [ra(13312 + 1024 * i, 512) for i in range(2)]
        PTLO = [ra(13824 + 1024 * i, 512) for i in range(2)]
        OHI = [ra(15360 + 1024 * i, 512) for i in range(2)]
        OLO = [ra(15872 + 1024 * i, 512) for i in range(2)]
        NMAX = SM[:, 0:8]
        DEN = SM[:, 8:16]
        RDEN = SM[:, 16:24]
        TV = fa(10240, 9 * P0).rearrange("p (e c) -> p e c", e=9)
        WM = [fa(2048 + P0 * i, P0) for i in range(2)]
        H1F = [fa(4106 + 512 * i, 512) for i in range(2)]
        RES = [fa(19501 + 512 * i, 512) for i in range(2)]
        GF1 = fa(20525, 128)
        GF2 = fa(20653, 8)
        GF2B = fa(20661, 8)
        GMB = fa(20669, 128)
        G1HI, G1LO = ra(0, 128), ra(128, 128)
        WSP = [ra(11264 + 2048 * i, 2048) for i in range(2)]
        H1HI = [ra(15360 + 1024 * i, 512) for i in range(2)]
        H1LO = [ra(15872 + 1024 * i, 512) for i in range(2)]
        GS = SM[:, 24:28]
        G = SM[:, 32:64].rearrange("p (b e) -> p b e", b=B)
        LNG, LNB = SM[:, 64:65], SM[:, 65:66]
        WRAW = [fa(6144 + 514 * i, 514) for i in range(2)]
        HG = [fa(7172 + 1024 * i, 1024) for i in range(2)]
        CB = [fa(10240 + 2048 * i, 2048) for i in range(2)]
        CT = FA[0:E, 14336:14336 + T]
        LG = fa(16384, 1024).rearrange("p (c e) -> p c e", c=16)
        PR = fa(17408, 1024).rearrange("p (c e) -> p c e", c=16)
        CW = fa(18432, 1024).rearrange("p (c e) -> p c e", c=16)
        KP = fa(19456, 1024).rearrange("p (c e) -> p c e", c=16)
        LW = fa(20480, 16 * (E + PADS)).rearrange("p (c e) -> p c e", c=16)
        RWT = fa(9220, E)
        RBT = fa(9284, E)
        EB2 = FA[0:E, 9348:9348 + 128]
        HHI = [ra(1024 * i, 1024) for i in range(2)]
        HLO = [ra(2048 + 1024 * i, 1024) for i in range(2)]
        WHI = [ra(4096 + 1024 * i, 512) for i in range(2)]
        WLO = [ra(4608 + 1024 * i, 512) for i in range(2)]
        V8 = SM[:, 72:80]
        RS16 = SM[:, 80:96]
        MX16 = SM[:, 96:112]
        RP16 = SM[:, 112:128]
        D16 = SM[:, 128:144]
        EPS = SM[:, 144:145]
        ONE = CS[:, C_POW:C_POW + 1]
        TN = CS[:, C_TN:C_TN + 2]
        O1, O2, SEM_, SEMC = SM[:, 148:149], SM[:, 149:150], SM[:, 150:151], SM[:, 151:152]
        VM, VV, VS, VR = SM[:, 152:153], SM[:, 153:154], SM[:, 154:155], SM[:, 155:156]
        TVS, T8 = SM[:, 156:158], SM[:, 160:168]

        PS = ctx.enter_context(nc.psum_tensor("banks", [128, 8 * 512], F32))

        def bank(i, n=1):
            return PS[:, 512 * i:512 * (i + n)]

        ld = {k: sem("ld_" + k) for k in ("tok", "const", "rows", "a0", "a1", "ffn", "moe")}
        dve_seq = sem("dve_seq")
        names = """tok_split onehot onehot_used tab_phase tab_sin vel_gelu vel_e vel_sq vel_std emb_tab emb_mm emb_out
            bf_ready eps_ready
            ln_mean ln_xc ln_sq ln_var ln_std ln_out ln_src x_hi x_lo
            xt_mm xt_hi xt_lo mn_mm mn_hi mn_lo
            stat_ready proj_ready q_mm q_hi q_lo s_mm nmax exp p_done pt_mm pt_hi pt_lo av o_hi o_lo y_mm y_add
            gate_w gate_mm gate_sum gate_bc gate_g gate_done mod w_hi w_lo h1_mm h1_act h1_hi h1_lo y0_mm res0 lnp
            ffn_out logit_mm router dist probs pair comb comb_t comb_s comb_out seed
            wsplit h_mm gelu scaled hh hl down final out_done""".split()
        s = {k: sem(k) for k in names}
        wld = [sem(f"ld_expert{i}") for i in range(2)]
        cbd = [sem(f"ld_comb{i}") for i in range(2)]
        block = ctx.enter_context(nc.Block())

        def three(pe, o, w_hi, w_lo, x_hi, x_lo, start, stop, **kw):
            pe.matmul(o, w_hi, x_hi, start=start, stop=False, **kw)
            pe.matmul(o, w_hi, x_lo, start=False, stop=False, **kw)
            return pe.matmul(o, w_lo, x_hi, start=False, stop=stop, **kw)

        def bchunk(t, c):
            return t[:, 512 * c:512 * (c + 1)]

        @block.sync
        def _(sp):
            sp.dma_start(TOKI, tok.partition_broadcast(128)).then_inc(ld["tok"], 16)
            sp.dma_start(CS[:, :], consts).then_inc(ld["const"], 16)
            sp.dma_start(CP[:, :], cols).then_inc(ld["rows"], 16)
            sp.dma_start(RW_[:, :], rows.partition_broadcast(128)).then_inc(ld["rows"], 16)
            sp.dma_start(TAB[:, 0:128], emb).then_inc(ld["rows"], 16)
            sp.dma_start(V2T[:, :], vel_w2t).then_inc(ld["rows"], 16)
            sp.dma_start(WL, a0).then_inc(ld["a0"], 16)
            sp.dma_start(TV, ffn.rearrange("e p c -> p e c")).then_inc(ld["ffn"], 16)
            sp.wait_ge(s["emb_out"], 4)
            sp.dma_start(GF1, gfc1t).then_inc(ld["ffn"], 16)
            sp.dma_start(GF2, gfc2t).then_inc(ld["ffn"], 16)
            sp.dma_start(GF2B, gfc2b.partition_broadcast(128)).then_inc(ld["ffn"], 16)
            sp.wait_ge(s["mn_lo"], H)
            sp.wait_ge(s["mn_hi"], H)
            sp.dma_start(WL[0:DH1], a1).then_inc(ld["a1"], 16)
            sp.wait_ge(s["mn_lo"], 2 * H)
            sp.wait_ge(s["mn_hi"], 2 * H)
            sp.dma_start(RWT, rw).then_inc(ld["moe"], 16)
            sp.dma_start(RBT, rb.partition_broadcast(128)).then_inc(ld["moe"], 16)
            sp.dma_start(EB2, eb2).then_inc(ld["moe"], 16)
            sp.wait_ge(s["comb_s"], 4)
            sp.dma_start(comb_dram, CT).then_inc(s["comb_out"], 16)
            sp.wait_ge(s["comb_out"], 16)

            def expert(e, i):
                if not isinstance(e, int):
                    sp.wait_ge(s["gelu"], 4 * (e - 1))
                sp.dma_start(WRAW[i], ew[bass.ds(e, 1), :, :].rearrange("o p c -> (o p) c")).then_inc(wld[i], 16)
                if not isinstance(e, int):
                    sp.wait_ge(s["scaled"], 4 * (e - 1))
                sp.dma_start(CB[i], comb_dram[bass.ds(e, 1), :].rearrange("o t -> (o t)").partition_broadcast(128))\
                    .then_inc(cbd[i], 16)

            expert(0, 0)
            expert(1, 1)
            with sp.Fori(1, E // 2) as pair:
                expert(2 * pair, 0)
                expert(2 * pair + 1, 1)
            sp.wait_ge(s["final"], NC)
            sp.dma_start(out, HT[:, :]).then_inc(s["out_done"], 16)
            sp.wait_ge(s["out_done"], 16)

        @block.gpsimd
        def _(pool):
            def split_x(norm, n):
                for c in range(NC):
                    pool.wait_ge(s["ln_out"], NC * norm + c + 1)
                    nc.gpsimd.tensor_copy(bchunk(XHI, c), bchunk(XN, c)).then_inc(s["x_hi"], 1)
                    pool.wait_ge(s["x_hi"], NC * n + c + 1)
                    nc.gpsimd.tensor_tensor(bchunk(XLO, c), bchunk(XN, c), bchunk(XHI, c).bitcast(F32), ALU.subtract)\
                        .then_inc(s["x_lo"], 1)

            def stationary(layer, u, i):
                N = H * B * layer + u
                if not isinstance(u, int):
                    pool.wait_ge(s["av"], 4 * (N - 1))
                nc.gpsimd.tensor_copy(STAT[i][:, 0:256], MN.bitcast(F32)[:, bass.ds((u % H) * 512, 256)])
                nc.gpsimd.tensor_copy(STAT[i][:, 256:1280], XTM.bitcast(F32)[:, bass.ds((u // H) * 1024, 1024)])\
                    .then_inc(s["stat_ready"], 1)
                if not isinstance(u, int):
                    pool.wait_ge(s["y_mm"], N - 1)
                nc.gpsimd.tensor_copy(PST[i], MN.bitcast(F32)[:, bass.ds((u % H) * 512 + 256, 256)])\
                    .then_inc(s["proj_ready"], 1)

            def attention(layer):
                pool.wait_ge(s["mn_lo"], H * (layer + 1))
                pool.wait_ge(s["xt_lo"], NC * (layer + 1))
                stationary(layer, 0, 0)
                stationary(layer, 1, 1)
                with pool.Fori(1, H * B // 2) as pair:
                    stationary(layer, 2 * pair, 0)
                    stationary(layer, 2 * pair + 1, 1)

            split_x(0, 0)
            attention(0)
            split_x(1, 1)
            for m in range(4 * B):
                pool.wait_ge(s["h1_act"], m + 1)
                if m >= 2:
                    pool.wait_ge(s["y0_mm"], m - 1)
                nc.gpsimd.tensor_copy(H1HI[m % 2], H1F[m % 2]).then_inc(s["h1_hi"], 1)
                pool.wait_ge(s["h1_hi"], m + 1)
                nc.gpsimd.tensor_tensor(H1LO[m % 2], H1F[m % 2], H1HI[m % 2].bitcast(F32), ALU.subtract)\
                    .then_inc(s["h1_lo"], 1)
            split_x(3, 2)
            attention(1)
            split_x(4, 3)

            def split_weights(e, i):
                pool.wait_ge(wld[i], 8 * (e - i) + 16)
                nc.gpsimd.tensor_tensor(WHI[i], WRAW[i][:, 0:512], ONE.to_broadcast([128, 512]), ALU.mult)\
                    .then_inc(s["pair"], 1)
                pool.wait_ge(s["pair"], e + 1)
                nc.gpsimd.tensor_tensor(WLO[i], WRAW[i][:, 0:512], WHI[i].bitcast(F32), ALU.subtract)\
                    .then_inc(s["wsplit"], 1)

            for e in range(2):
                split_weights(e, e)
            with pool.Fori(1, E // 2) as pair:
                for i in range(2):
                    pool.wait_ge(s["down"], 4 * (2 * pair + i) - 4)
                    split_weights(2 * pair + i, i)

        @block.scalar
        def _(act):
            A = nc.scalar.activation
            act.wait_ge(ld["rows"], 64)
            act.wait_ge(ld["const"], 16)
            A(VH[0:64], CS[0:64, C_VN:C_VN + 40], ACT.Gelu, bias=CP[0:64, K_VB1:K_VB1 + 1],
              scale=CP[0:64, K_VW1:K_VW1 + 1]).then_inc(s["vel_gelu"], 1)
            act.wait_ge(s["tab_phase"], 1)
            tab = TAB.rearrange("p (k d) -> p k d", k=VC)
            A(tab[:, 1:5, 64:128], PH[:, 0:256].rearrange("p (k d) -> p k d", k=4), ACT.Sin).then_inc(s["tab_sin"], 1)
            A(tab[:, 5, :], PH[:, 256:384], ACT.Sin).then_inc(s["tab_sin"], 1)
            act.wait_ge(s["vel_sq"], 1)
            act.wait_ge(s["eps_ready"], 1)
            A(VS[0:40], VV[0:40], ACT.Sqrt, bias=EPS[0:40]).then_inc(s["vel_std"], 1)
            for c in range(NC):
                act.wait_ge(s["emb_mm"], c + 1)
                A(bchunk(HT, c), bank(c), ACT.Copy).then_inc(s["emb_out"], 1)

            def norm(n):
                def square(c):
                    g = NC * n + c
                    act.wait_ge(s["ln_xc"], g + 1)
                    if g >= 2:
                        act.wait_ge(s["ln_var"], g - 1)
                    A(SQ[c % 2], bchunk(XN, c), ACT.Square).then_inc(s["ln_sq"], 1)

                def root(c):
                    g = NC * n + c
                    act.wait_ge(s["ln_var"], g + 1)
                    if g >= 2:
                        act.wait_ge(s["ln_out"], g - 1)
                    A(STD[c % 2], bank(2 + c % 2), ACT.Sqrt, bias=EPS).then_inc(s["ln_std"], 1)
                square(0)
                for c in range(NC):
                    if c + 1 < NC:
                        square(c + 1)
                    root(c)

            def tokens_out(layer):
                for c in range(NC):
                    act.wait_ge(s["xt_mm"], NC * layer + c + 1)
                    A(XTM[:, 1024 * c:1024 * c + 512], bank(4 + c), ACT.Copy).then_inc(s["xt_hi"], 1)

            def head_matrices(layer):
                scale = 1 / math.sqrt(D) if layer == 0 else 1 / math.sqrt(DH1)
                for h in range(H):
                    act.wait_ge(s["mn_mm"], H * layer + h + 1)
                    A(MN[:, 512 * h:512 * h + 128], bank(h % 4)[:, 0:128], ACT.Copy, scale=scale)
                    A(MN[:, 512 * h + 256:512 * h + 384], bank(h % 4)[:, 128:256], ACT.Copy).then_inc(s["mn_hi"], 1)

            def attention(layer):
                def step(u, i, first, second, third):
                    N = H * B * layer + u
                    w = [(128 * (c + 1) if layer == 0 else 512) for c in range(4)]
                    lo = [(128 * j if layer == 0 else 0) for j in range(4)]
                    if first:
                        act.wait_ge(s["q_mm"], N + 1)
                        A(QHI[i], bank(5), ACT.Copy).then_inc(s["q_hi"], 1)

                    def part(j):
                        if second:
                            act.wait_ge(s["pt_mm"], 4 * (N - 1) + j + 1)
                            if j >= 2:
                                act.wait_ge(s["av"], 4 * (N - 1) + j - 1)
                            A(PTHI[j % 2][:, lo[j]:512], bank(3 + j % 2)[:, lo[j]:512], ACT.Copy).then_inc(s["pt_hi"], 1)

                    def exps(c):
                        if first:
                            act.wait_ge(s["nmax"], 4 * N + c + 1)
                            A(PB[i][:, c, 0:w[c]], bank(c % 3)[:, 0:w[c]], ACT.Exp,
                              bias=NMAX[:, 4 * i + c:4 * i + c + 1],
                              accum_out=DEN[:, 4 * i + c:4 * i + c + 1]).then_inc(s["exp"], 1)
                    part(0)
                    part(1)
                    exps(0)
                    exps(1)
                    part(2)
                    exps(2)
                    part(3)
                    exps(3)
                    if second:
                        act.wait_ge(s["av"], 4 * (N - 1) + 4)
                        A(OHI[1 - i], bank(6), ACT.Copy).then_inc(s["o_hi"], 1)
                step(0, 0, True, False, False)
                step(1, 1, True, True, False)
                with act.Fori(1, H * B // 2) as pair:
                    step(2 * pair, 0, True, True, True)
                    step(2 * pair + 1, 1, True, True, True)
                step(H * B, 0, False, True, True)

            norm(0)
            head_matrices(0)
            tokens_out(0)
            attention(0)
            norm(1)
            act.wait_ge(ld["ffn"], 64)
            A(G1HI, GF1, ACT.Copy).then_inc(s["gate_w"], 1)
            for b in range(B):
                act.wait_ge(s["gate_mm"], b + 1)
                A(fa(512 * b, 512), bank(4 + b), ACT.Relu, bias=CP[:, K_GB1:K_GB1 + 1], accum_out=GS[:, b:b + 1])\
                    .then_inc(s["gate_sum"], 1)
            for b in range(B):
                act.wait_ge(s["mod"], b + 1)
                if b >= 2:
                    act.wait_ge(s["y0_mm"], 4 * (b - 1))
                A(WSP[b % 2][:, 0:1024], WM[b % 2][:, 0:1024], ACT.Copy).then_inc(s["w_hi"], 1)
                for j in range(4):
                    m = 4 * b + j
                    act.wait_ge(s["h1_mm"], m + 1)
                    if m >= 2:
                        act.wait_ge(s["h1_lo"], m - 1)
                    A(H1F[j % 2], bank(j % 2), ACT.Relu, bias=WM[b % 2][:, 1024 + j:1025 + j]).then_inc(s["h1_act"], 1)
            norm(2)
            norm(3)
            head_matrices(1)
            tokens_out(1)
            attention(1)
            norm(4)
            act.wait_ge(s["router"], 1)
            A(PR, LG, ACT.Exp).then_inc(s["dist"], 1)
            act.wait_ge(s["router"], 2)
            A(CW, PR, ACT.Exp).then_inc(s["dist"], 1)
            for c in range(NC):
                act.wait_ge(s["comb_t"], c + 1)
                A(CT[:, 512 * c:512 * (c + 1)], bank(c)[0:E], ACT.Copy).then_inc(s["comb_s"], 1)

            def hi_part(m, k):
                act.wait_ge(s["scaled"], m + 1)
                if not isinstance(m, int) or m >= 2:
                    act.wait_ge(s["down"], m - 1)
                A(HHI[k % 2], HG[k % 2], ACT.Copy).then_inc(s["hh"], 1)
            for k in range(4):
                act.wait_ge(s["h_mm"], k + 1)
                if k >= 2:
                    act.wait_ge(s["hl"], k - 1)
                A(HG[k % 2], bank(4 + 2 * (k % 2), 2), ACT.Gelu, bias=WRAW[0][:, 512 + k // 2:513 + k // 2])\
                    .then_inc(s["gelu"], 1)
                if k >= 1:
                    hi_part(k - 1, k - 1)

            def expert(e, i):
                for k in range(4):
                    m = 4 * e + k
                    act.wait_ge(s["h_mm"], m + 1)
                    act.wait_ge(s["hl"], m - 1)
                    g = A(HG[k % 2], bank(4 + 2 * (k % 2), 2), ACT.Gelu, bias=WRAW[i][:, 512 + k // 2:513 + k // 2])
                    g.then_inc(s["gelu"], 1)
                    hi_part(m - 1, k + 3)
            expert(1, 1)
            with act.Fori(1, E // 2) as pair:
                expert(2 * pair, 0)
                expert(2 * pair + 1, 1)
            hi_part(4 * E - 1, 3)

        @block.vector
        def _(dve):
            V = nc.vector
            seq = [0]

            def link(ins):
                seq[0] += 1
                ins.then_inc(dve_seq, 1)
                dve.wait_ge(dve_seq, seq[0])

            V.memset(EPS, LN_EPS).then_inc(s["eps_ready"], 1)
            dve.wait_ge(ld["const"], 16)
            dve.wait_ge(ld["tok"], 16)
            V.tensor_copy(IDB[:, :], ident)
            V.tensor_copy(MKB[:, :], mask).then_inc(s["bf_ready"], 1)
            link(V.tensor_copy(TOKF, TOKI))
            link(V.tensor_scalar(TOKF, TOKF, 0.0, None, ALU.max))
            dve.wait_ge(ld["rows"], 64)
            tab = TAB.rearrange("p (k d) -> p k d", k=VC)
            pos = CS[:, C_POS:C_POS + 1]
            for kind in range(2):
                for j in range(2):
                    o = 64 * kind
                    V.scalar_tensor_tensor(tab[:, 1 + 2 * kind + j, 0:64], RW_[:, R_LW + o:R_LW + o + 64], TN[:, j:j + 1],
                                           RW_[:, R_LB + o:R_LB + o + 64], ALU.mult, ALU.add)
                    V.scalar_tensor_tensor(PH[:, 128 * kind + 64 * j:128 * kind + 64 * j + 64],
                                           RW_[:, R_W + o:R_W + o + 64], TN[:, j:j + 1],
                                           RW_[:, R_B + o:R_B + o + 64], ALU.mult, ALU.add)
            p0 = pos[:, 0:1]
            link(V.tensor_scalar(O1, p0, 12.0, None, ALU.is_ge))
            link(V.scalar_tensor_tensor(O2, p0, 24.0, O1, ALU.is_ge, ALU.add))
            link(V.scalar_tensor_tensor(SEM_, O2, -12.0, p0, ALU.mult, ALU.add))
            link(V.tensor_scalar(SEMC, SEM_, math.pi / 6.0, None, ALU.mult))
            pn = PH[:, 256:384].rearrange("p (i a b) -> p i a b", a=2, b=2)
            kn = KQ[:, 256:384].rearrange("p (i a b) -> p i a b", a=2, b=2)
            for b_ in range(2):
                V.tensor_scalar(pn[:, :, 0, b_], CS[:, C_POW:C_POW + 32], O2, None, ALU.mult)
                last = V.tensor_scalar(pn[:, :, 1, b_], CS[:, C_INC:C_INC + 32], SEMC, None, ALU.mult)
            link(last)
            link(V.tensor_scalar(KQ, PH, 1 / (2 * math.pi), None, ALU.mult))
            link(V.tensor_scalar(kn[:, :, :, 1], kn[:, :, :, 1], 0.25, None, ALU.add))
            link(V.tensor_scalar(KQ, KQ, 1.5 * 2 ** 23, None, ALU.add))
            link(V.tensor_scalar(KQ, KQ, 1.5 * 2 ** 23, None, ALU.subtract))
            link(V.scalar_tensor_tensor(PH, KQ, -6.28125, PH, ALU.mult, ALU.add))
            link(V.scalar_tensor_tensor(PH, KQ, -(2 * math.pi - 6.28125), PH, ALU.mult, ALU.add))
            link(V.tensor_scalar(pn[:, :, :, 1], pn[:, :, :, 1], math.pi / 2, None, ALU.add))
            V.tensor_scalar(PH, PH, -3.1415925, 3.1415925, ALU.max, ALU.min).then_inc(s["tab_phase"], 1)
            dve.wait_ge(s["vel_e"], 1)
            ve = VE[0:40]
            link(V.tensor_tensor(ve, bank(7)[0:40, 0:128], RW_[0:40, R_B2:R_B2 + 128], ALU.add))
            link(V.reduce_sum(VM[0:40], ve, AX.X))
            link(V.tensor_scalar(VM[0:40], VM[0:40], 1.0 / D, None, ALU.mult))
            link(V.tensor_scalar(ve, ve, VM[0:40], None, ALU.subtract))
            link(V.tensor_tensor(VSQ[0:40], ve, ve, ALU.mult))
            link(V.reduce_sum(VR[0:40], VSQ[0:40], AX.X))
            V.tensor_scalar(VV[0:40], VR[0:40], 1.0 / D, None, ALU.mult).then_inc(s["vel_sq"], 1)
            dve.wait_ge(s["vel_std"], 1)
            link(V.reciprocal(VS[0:40], VS[0:40]))
            link(V.tensor_scalar(ve, ve, VS[0:40], None, ALU.mult))
            link(V.tensor_tensor(ve, ve, RW_[0:40, R_G:R_G + 128], ALU.mult))
            dve.wait_ge(s["tab_sin"], 2)
            link(V.tensor_tensor(tab[32:40, 5, :], ve[32:40], RW_[32:40, R_BETA:R_BETA + 128], ALU.add))
            link(V.tensor_copy(THI, TAB))
            V.tensor_tensor(TLO, TAB, THI.bitcast(F32), ALU.subtract).then_inc(s["emb_tab"], 1)
            for k in range(VC):
                if k >= 2:
                    dve.wait_ge(s["onehot_used"], k - 1)
                V.tensor_scalar(OH[k % 2], TOKF, CS[:, C_IDX + k:C_IDX + k + 1], None, ALU.is_equal)\
                    .then_inc(s["onehot"], 1)

            def norm(n, src):
                def center(c):
                    g = NC * n + c
                    dve.wait_ge(s["ln_mean"], g + 1)
                    V.tensor_tensor(bchunk(XN, c), bchunk(src, c), bank(c % 2), ALU.subtract).then_inc(s["ln_xc"], 1)

                def scale(c):
                    g = NC * n + c
                    dve.wait_ge(s["ln_std"], g + 1)
                    link(V.reciprocal(STD[c % 2], STD[c % 2]))
                    V.tensor_tensor(bchunk(XN, c), bchunk(XN, c), STD[c % 2], ALU.mult).then_inc(s["ln_out"], 1)
                center(0)
                for c in range(NC):
                    if c + 1 < NC:
                        center(c + 1)
                    scale(c)

            def tokens_out(layer):
                for c in range(NC):
                    dve.wait_ge(s["xt_hi"], NC * layer + c + 1)
                    V.tensor_tensor(XTM[:, 1024 * c + 512:1024 * (c + 1)], bank(4 + c),
                                    XTM[:, 1024 * c:1024 * c + 512].bitcast(F32), ALU.subtract).then_inc(s["xt_lo"], 1)

            def head_matrices(layer):
                scale = 1 / math.sqrt(D) if layer == 0 else 1 / math.sqrt(DH1)
                for h in range(H):
                    dve.wait_ge(s["mn_hi"], H * layer + h + 1)
                    V.scalar_tensor_tensor(MN[:, 512 * h + 128:512 * h + 256], bank(h % 4)[:, 0:128], scale,
                                           MN[:, 512 * h:512 * h + 128].bitcast(F32), ALU.mult, ALU.subtract)
                    V.tensor_tensor(MN[:, 512 * h + 384:512 * h + 512], bank(h % 4)[:, 128:256],
                                    MN[:, 512 * h + 256:512 * h + 384].bitcast(F32), ALU.subtract)\
                        .then_inc(s["mn_lo"], 1)

            rd = sem("rden")

            def attention(layer):
                def step(u, i, first, second, third):
                    N = H * B * layer + u
                    w = [(128 * (c + 1) if layer == 0 else 512) for c in range(4)]
                    lo = [(128 * j if layer == 0 else 0) for j in range(4)]
                    if first:
                        dve.wait_ge(s["q_hi"], N + 1)
                        V.tensor_tensor(QLO[i], bank(5), QHI[i].bitcast(F32), ALU.subtract).then_inc(s["q_lo"], 1)

                    def part(j):
                        if second:
                            dve.wait_ge(s["pt_hi"], 4 * (N - 1) + j + 1)
                            V.tensor_tensor(PTLO[j % 2][:, lo[j]:512], bank(3 + j % 2)[:, lo[j]:512],
                                            PTHI[j % 2][:, lo[j]:512].bitcast(F32), ALU.subtract)\
                                .then_inc(s["pt_lo"], 1)

                    def top(c):
                        if first:
                            dve.wait_ge(s["s_mm"], 4 * N + c + 1)
                            V.tensor_reduce(NMAX[:, 4 * i + c:4 * i + c + 1], bank(c % 3)[:, 0:w[c]], AX.X, ALU.max,
                                            negate=True).then_inc(s["nmax"], 1)

                    def weights(c):
                        if first:
                            dve.wait_ge(s["exp"], 4 * N + c + 1)
                            V.reciprocal(RDEN[:, 4 * i + c:4 * i + c + 1], DEN[:, 4 * i + c:4 * i + c + 1]).then_inc(rd, 1)
                            dve.wait_ge(rd, 4 * N + c + 1)
                            V.tensor_scalar(PB[i][:, c, 0:w[c]], PB[i][:, c, 0:w[c]], RDEN[:, 4 * i + c:4 * i + c + 1],
                                            None, ALU.mult).then_inc(s["p_done"], 1)
                    part(0)
                    part(1)
                    top(0)
                    if third:
                        batch = (u - 2) // H
                        dve.wait_ge(s["y_mm"], N - 1)
                        V.tensor_tensor(HT[:, bass.ds(512 * batch, 512)], bank(7), HT[:, bass.ds(512 * batch, 512)],
                                        ALU.add).then_inc(s["y_add"], 1)
                    top(1)
                    weights(0)
                    part(2)
                    weights(1)
                    top(2)
                    part(3)
                    weights(2)
                    top(3)
                    weights(3)
                    if second:
                        dve.wait_ge(s["o_hi"], N)
                        V.tensor_tensor(OLO[1 - i], bank(6), OHI[1 - i].bitcast(F32), ALU.subtract)\
                            .then_inc(s["o_lo"], 1)
                step(0, 0, True, False, False)
                step(1, 1, True, True, False)
                with dve.Fori(1, H * B // 2) as pair:
                    step(2 * pair, 0, True, True, True)
                    step(2 * pair + 1, 1, True, True, True)
                step(H * B, 0, False, True, True)
                step(H * B + 1, 1, False, False, True)

            norm(0, HT)
            head_matrices(0)
            tokens_out(0)
            attention(0)
            norm(1, HT)
            dve.wait_ge(s["gate_w"], 1)
            V.tensor_tensor(G1LO, GF1, G1HI.bitcast(F32), ALU.subtract).then_inc(s["gate_w"], 1)
            for b in range(B):
                dve.wait_ge(s["gate_sum"], b + 1)
                if b:
                    dve.wait_ge(s["gate_g"], b)
                V.tensor_scalar(GMB, GS[:, b:b + 1].to_broadcast([128, 128]), 1.0 / S, None, ALU.mult)\
                    .then_inc(s["gate_bc"], 1)
                dve.wait_ge(s["gate_g"], b + 1)
                link(V.tensor_tensor(G[:, b, :], bank(0)[:, 8 * b:8 * b + 8], GF2B, ALU.add))
            for col, base, o in ((K_TVG, K_LNG, LNG), (K_TVB, K_LNB, LNB)):
                link(V.tensor_scalar(T8, CP[:, col:col + E0], CP[:, base:base + 1], None, ALU.subtract))
                link(V.reduce_sum(TVS[:, 0:1], T8, AX.X))
                link(V.scalar_tensor_tensor(o, TVS[:, 0:1], 0.03, CP[:, base:base + 1], ALU.mult, ALU.add))

            def modulate(b):
                if b >= 2:
                    dve.wait_ge(s["res0"], b - 1)
                    dve.wait_ge(s["h1_act"], 4 * (b - 1))
                for e in range(E0):
                    ins = V.scalar_tensor_tensor(WM[b % 2], TV[:, 1 + e, :], G[:, b, e:e + 1],
                                                 TV[:, 0, :] if e == 0 else WM[b % 2], ALU.mult, ALU.add)
                    if e < E0 - 1:
                        link(ins)
                ins.then_inc(s["mod"], 1)

            def finish(b):
                dve.wait_ge(s["y0_mm"], 4 * (b + 1))
                V.scalar_tensor_tensor(bchunk(XN, b), bank(2 + b % 2), WM[b % 2][:, 1028:1029], bchunk(XN, b),
                                       ALU.add, ALU.add).then_inc(s["res0"], 1)
            for b in range(B):
                modulate(b)
                dve.wait_ge(s["w_hi"], b + 1)
                V.tensor_tensor(WSP[b % 2][:, 1024:2048], WM[b % 2][:, 0:1024], WSP[b % 2][:, 0:1024].bitcast(F32),
                                ALU.subtract).then_inc(s["w_lo"], 1)
                if b >= 1:
                    finish(b - 1)
            finish(B - 1)
            norm(2, XN)
            for c in range(NC):
                dve.wait_ge(s["ln_out"], NC * 2 + c + 1)
                link(V.tensor_scalar(bchunk(XN, c), bchunk(XN, c), LNG, LNB, ALU.mult, ALU.add))
                ins = V.tensor_tensor(bchunk(HT, c), bchunk(HT, c), bchunk(XN, c), ALU.add)
                ins.then_inc(s["ffn_out"], 1)
            norm(3, HT)
            head_matrices(1)
            tokens_out(1)
            attention(1)
            dve.wait_ge(s["y_add"], 2 * H * B)
            for c in range(NC):
                V.tensor_scalar(bchunk(HT, c), bchunk(HT, c), CP[:, K_BOUT:K_BOUT + 1], None, ALU.add)\
                    .then_inc(s["ln_src"], 1)
            norm(4, HT)
            dve.wait_ge(s["logit_mm"], 1)
            dve.wait_ge(ld["moe"], 48)

            def over(x):
                return x.unsqueeze(2).to_broadcast([128, 16, E])
            V.memset(LW[:, :, E:E + PADS], 1e30)
            link(V.tensor_tensor(LG, bank(4, 2).rearrange("p (c e) -> p c e", c=16),
                                 RBT.unsqueeze(1).to_broadcast([128, 16, E]), ALU.add))
            link(V.tensor_reduce(MX16, LG, AX.X, ALU.max))
            link(V.tensor_tensor(LG, LG, over(MX16), ALU.subtract))
            V.tensor_scalar(LG, LG, -87.33654, None, ALU.max).then_inc(s["router"], 1)
            dve.wait_ge(s["router"], 1)
            link(V.tensor_scalar(LW[:, :, 0:E], LG, -1.0, None, ALU.mult))
            for c in range(16):
                for r in range((DROP + PADS) // 8):
                    link(V.max(V8, LW[:, c, :]))
                    link(V.match_replace(LW[:, c, :], V8, LW[:, c, :], -1.0))
            dve.wait_ge(s["dist"], 1)
            link(V.reduce_sum(RS16, PR, AX.X))
            link(V.reciprocal(RP16, RS16))
            link(V.tensor_tensor(PR, PR, over(RP16), ALU.mult))
            link(V.tensor_reduce(MX16, PR, AX.X, ALU.max))
            V.tensor_tensor(PR, PR, over(MX16), ALU.subtract).then_inc(s["router"], 1)
            link(V.tensor_scalar(KP, LW[:, :, 0:E], 0.0, None, ALU.is_ge))
            dve.wait_ge(s["dist"], 2)
            link(V.tensor_tensor(CW, CW, KP, ALU.mult))
            link(V.reduce_sum(D16, CW, AX.X))
            link(V.reciprocal(D16, D16))
            V.tensor_tensor(CW, CW, over(D16), ALU.mult).then_inc(s["comb"], 1)

            def lo_part(m, k):
                dve.wait_ge(s["hh"], m + 1)
                V.tensor_tensor(HLO[k % 2], HG[k % 2], HHI[k % 2].bitcast(F32), ALU.subtract).then_inc(s["hl"], 1)

            def weigh(m, k, i):
                dve.wait_ge(s["gelu"], m + 1)
                V.tensor_tensor(HG[k % 2], HG[k % 2], CB[i][:, 1024 * (k % 2):1024 * (k % 2) + 1024], ALU.mult)\
                    .then_inc(s["scaled"], 1)

            def expert(e, i, first=False):
                for k in range(4):
                    m = 4 * e + k
                    if k == 0:
                        dve.wait_ge(cbd[i], 8 * (e - i) + 16)
                    weigh(m, k, i)
                    if not (first and k == 0):
                        lo_part(m - 1, k + 3)
            expert(0, 0, True)
            expert(1, 1)
            with dve.Fori(1, E // 2) as pair:
                expert(2 * pair, 0)
                expert(2 * pair + 1, 1)
            lo_part(4 * E - 1, 3)
            dve.wait_ge(s["down"], 4 * E)
            for c in range(NC):
                V.tensor_tensor(bchunk(HT, c), bchunk(HT, c), bank(c), ALU.add).then_inc(s["final"], 1)

        @block.tensor
        def _(pe):
            pe.wait_ge(ld["rows"], 64)
            pe.wait_ge(s["vel_gelu"], 1)
            pe.matmul(bank(7)[0:40, 0:128], VH[0:64], V2T[:, :], start=True, stop=True).then_inc(s["vel_e"], 1)
            pe.wait_ge(s["emb_tab"], 1)
            for k in range(VC):
                pe.wait_ge(s["onehot"], k + 1)
                for c in range(NC):
                    o = bank(c)
                    pe.matmul(o, THI[:, 128 * k:128 * (k + 1)], bchunk(OH[k % 2], c), start=(k == 0), stop=False)
                    ins = pe.matmul(o, TLO[:, 128 * k:128 * (k + 1)], bchunk(OH[k % 2], c), start=False,
                                    stop=(k == VC - 1))
                    if k == VC - 1:
                        ins.then_inc(s["emb_mm"], 1)
                if k < VC - 1:
                    ins.then_inc(s["onehot_used"], 1)

            def norm(n, src, ready):
                def mean(c):
                    g = NC * n + c
                    ready(c)
                    if c >= 2:
                        pe.wait_ge(s["ln_xc"], g - 1)
                    pe.matmul(bank(c % 2), mean_w, bchunk(src, c), start=True, stop=True).then_inc(s["ln_mean"], 1)

                def var(c):
                    g = NC * n + c
                    pe.wait_ge(s["ln_sq"], g + 1)
                    if g >= 2:
                        pe.wait_ge(s["ln_std"], g - 1)
                    pe.matmul(bank(2 + c % 2), mean_w, SQ[c % 2], start=True, stop=True).then_inc(s["ln_var"], 1)
                mean(0)
                for c in range(NC):
                    if c + 1 < NC:
                        mean(c + 1)
                    var(c)

            def tokens_out(layer):
                n = 0 if layer == 0 else 3
                for c in range(NC):
                    pe.wait_ge(s["ln_out"], NC * n + c + 1)
                    for j in range(4):
                        ins = pe.transpose(bank(4 + c)[:, 128 * j:128 * (j + 1)],
                                           XN[:, 512 * c + 128 * j:512 * c + 128 * (j + 1)], ident)
                    ins.then_inc(s["xt_mm"], 1)

            def head_matrices(layer):
                k = 128 if layer == 0 else DH1
                pe.wait_ge(ld["a0" if layer == 0 else "a1"], 16)
                pe.wait_ge(s["ln_std"], NC * (1 if layer == 0 else 4))
                for h in range(H):
                    if h >= 4:
                        pe.wait_ge(s["mn_lo"], H * layer + h - 3)
                    hs = slice(128 * h, 128 * (h + 1))
                    pe.matmul(bank(h % 4)[:, 0:128], WL[0:k, 0, hs], WL[0:k, 1, hs], start=True, stop=True)
                    pe.matmul(bank(h % 4)[:, 128:256], WL[0:k, 2, hs], WL[0:k, 3, hs], start=True, stop=True)\
                        .then_inc(s["mn_mm"], 1)

            def attention(layer):
                n = 0 if layer == 0 else 3
                pe.wait_ge(s["x_lo"], NC * (n + 1) if layer == 0 else NC * 3)
                pe.wait_ge(s["mn_lo"], H * (layer + 1))
                pe.wait_ge(s["xt_lo"], NC * (layer + 1))

                def step(u, i, first, second, third):
                    N = H * B * layer + u
                    if first:
                        batch = u // H
                        st = STAT[i]
                        x_hi = XHI[:, bass.ds(512 * batch, 512)]
                        x_lo = XLO[:, bass.ds(512 * batch, 512)]
                        pe.wait_ge(s["stat_ready"], N + 1)
                        three(pe, bank(5), st[:, 0:128], st[:, 128:256], x_hi, x_lo, True, True)\
                            .then_inc(s["q_mm"], 1)

                    def turn(j):
                        if second:
                            if j == 0:
                                pe.wait_ge(s["p_done"], 4 * N)
                            if j >= 2:
                                pe.wait_ge(s["pt_lo"], 4 * (N - 1) + j - 1)
                            for c in range(j if layer == 0 else 0, 4):
                                ins = pe.transpose(bank(3 + j % 2)[:, 128 * c:128 * (c + 1)],
                                                   PB[1 - i][:, c, 128 * j:128 * (j + 1)], ident)
                            ins.then_inc(s["pt_mm"], 1)

                    def scores(c):
                        if first:
                            w = 128 * (c + 1) if layer == 0 else 512
                            if c == 0:
                                pe.wait_ge(s["q_lo"], N + 1)
                            if c == 3:
                                pe.wait_ge(s["exp"], 4 * N + 1)
                            qs = slice(128 * c, 128 * (c + 1))
                            o = bank(c % 3)[:, 0:w]
                            xh = XHI[:, bass.ds(512 * batch, w)]
                            xl = XLO[:, bass.ds(512 * batch, w)]
                            pe.matmul(o, QHI[i][:, qs], xh, start=True, stop=False)
                            if layer == 0:
                                pe.matmul(o[:, 128 * c:128 * (c + 1)], IDB[:, :], MKB[:, :], start=False, stop=False,
                                          skip_group_check=True)
                            pe.matmul(o, QHI[i][:, qs], xl, start=False, stop=False)
                            ins = pe.matmul(o, QLO[i][:, qs], xh, start=False, stop=True)
                            ins.then_inc(s["s_mm"], 1)

                    def mix(j):
                        if second:
                            st = STAT[1 - i]
                            lo = 128 * j if layer == 0 else 0
                            pe.wait_ge(s["pt_lo"], 4 * (N - 1) + j + 1)
                            three(pe, bank(6)[:, lo:512], st[:, 256 + 128 * j:256 + 128 * (j + 1)],
                                  st[:, 768 + 128 * j:768 + 128 * (j + 1)], PTHI[j % 2][:, lo:512],
                                  PTLO[j % 2][:, lo:512], j == 0, layer == 0 or j == 3, skip_group_check=True)\
                                .then_inc(s["av"], 1)

                    def project():
                        if third:
                            pe.wait_ge(s["o_lo"], N - 1)
                            pe.wait_ge(s["proj_ready"], N - 1)
                            if not second:
                                pe.wait_ge(s["y_add"], N - 2)
                            three(pe, bank(7), PST[i][:, 0:128], PST[i][:, 128:256], OHI[i], OLO[i], True, True)\
                                .then_inc(s["y_mm"], 1)
                    turn(0)
                    turn(1)
                    scores(0)
                    project()
                    scores(1)
                    mix(0)
                    turn(2)
                    scores(2)
                    mix(1)
                    turn(3)
                    scores(3)
                    mix(2)
                    mix(3)
                step(0, 0, True, False, False)
                step(1, 1, True, True, False)
                with pe.Fori(1, H * B // 2) as pair:
                    step(2 * pair, 0, True, True, True)
                    step(2 * pair + 1, 1, True, True, True)
                step(H * B, 0, False, True, True)
                step(H * B + 1, 1, False, False, True)

            norm(0, HT, lambda c: pe.wait_ge(s["emb_out"], NC))
            head_matrices(0)
            tokens_out(0)
            attention(0)
            norm(1, HT, lambda c: pe.wait_ge(s["y_add"], H * B))
            pe.wait_ge(s["x_lo"], 2 * NC)
            pe.wait_ge(s["gate_w"], 2)
            for b in range(B):
                three(pe, bank(4 + b), G1HI, G1LO, bchunk(XHI, b), bchunk(XLO, b), True, True).then_inc(s["gate_mm"], 1)
            for b in range(B):
                pe.wait_ge(s["gate_bc"], b + 1)
                pe.matmul(bank(0)[:, 8 * b:8 * b + 8], GMB, GF2, start=True, stop=True).then_inc(s["gate_g"], 1)

            def up(m):
                b, j = m // 4, m % 4
                if j == 0:
                    pe.wait_ge(s["w_lo"], b + 1)
                if m >= 2:
                    pe.wait_ge(s["h1_act"], m - 1)
                w = WSP[b % 2]
                three(pe, bank(m % 2), w[:, 128 * j:128 * (j + 1)], w[:, 1024 + 128 * j:1024 + 128 * (j + 1)],
                      bchunk(XHI, b), bchunk(XLO, b), True, True).then_inc(s["h1_mm"], 1)

            def down0(m):
                b, j = m // 4, m % 4
                if j == 0 and b >= 2:
                    pe.wait_ge(s["res0"], b - 1)
                pe.wait_ge(s["h1_lo"], m + 1)
                w = WSP[b % 2]
                three(pe, bank(2 + b % 2), w[:, 512 + 128 * j:512 + 128 * (j + 1)],
                      w[:, 1536 + 128 * j:1536 + 128 * (j + 1)], H1HI[m % 2], H1LO[m % 2], j == 0, j == 3)\
                    .then_inc(s["y0_mm"], 1)
            for m in range(4 * B + 2):
                if m < 4 * B:
                    up(m)
                if m >= 2:
                    down0(m - 2)
            norm(2, XN, lambda c: pe.wait_ge(s["res0"], B))
            norm(3, HT, lambda c: pe.wait_ge(s["ffn_out"], c + 1))
            head_matrices(1)
            tokens_out(1)
            attention(1)
            norm(4, HT, lambda c: pe.wait_ge(s["ln_src"], c + 1))
            pe.wait_ge(ld["moe"], 48)
            pe.wait_ge(s["ln_out"], 5 * NC)
            for c in range(16):
                ins = pe.matmul(PS[:, 2048 + E * c:2048 + E * (c + 1)], XN[:, 128 * c:128 * (c + 1)], RWT, start=True,
                                stop=True)
            ins.then_inc(s["logit_mm"], 1)
            pe.wait_ge(s["comb"], 1)
            for c in range(NC):
                for j in range(4):
                    ins = pe.transpose(bank(c)[0:E, 128 * j:128 * (j + 1)], CW[:, 4 * c + j, :], ident)
                ins.then_inc(s["comb_t"], 1)
            pe.wait_ge(s["comb_s"], NC)
            for c in range(NC):
                pe.matmul(bank(c), EB2, CT[:, 512 * c:512 * (c + 1)], start=True, stop=False, skip_group_check=True)

            pe.wait_ge(s["x_lo"], 4 * NC)

            def rise(m, k, i):
                if not isinstance(m, int) or m >= 2:
                    pe.wait_ge(s["gelu"], m - 1)
                f = slice(128 * (k // 2), 128 * (k // 2 + 1))
                for j in range(2):
                    c = 2 * (k % 2) + j
                    ins = three(pe, bank(4 + 2 * (k % 2) + j), WHI[i][:, f], WLO[i][:, f], bchunk(XHI, c), bchunk(XLO, c),
                                True, True)
                ins.then_inc(s["h_mm"], 1)

            def fall(m, k, i, last=False):
                pe.wait_ge(s["hl"], m + 1)
                f = slice(256 + 128 * (k // 2), 256 + 128 * (k // 2 + 1))
                for j in range(2):
                    c = 2 * (k % 2) + j
                    h = slice(512 * j, 512 * (j + 1))
                    ins = three(pe, bank(c), WHI[i][:, f], WLO[i][:, f], HHI[k % 2][:, h], HLO[k % 2][:, h], False, last,
                                skip_group_check=True)
                ins.then_inc(s["down"], 1)

            def expert(e, i):
                pe.wait_ge(s["wsplit"], e + 1)
                for k in range(4):
                    rise(4 * e + k, k, i)
                    if not (isinstance(e, int) and e == 0 and k < LAG):
                        fall(4 * e + k - LAG, (k - LAG) % 4, i if k >= LAG else 1 - i)
            expert(0, 0)
            expert(1, 1)
            with pe.Fori(1, E // 2) as pair:
                expert(2 * pair, 0)
                expert(2 * pair + 1, 1)
            for m in range(4 * E - LAG, 4 * E):
                fall(m, m % 4, 1, last=m >= 4 * E - 2)


def kernel(**inputs):
    import numpy as np
    import concourse.bacc as bacc
    from concourse.bass_utils import run_bass_kernel_spmd

    x = {k: np.asarray(v) for k, v in inputs.items()}
    f = np.float32

    consts = np.zeros((128, C_ALL), f)
    p = np.arange(128)
    consts[:, C_ID:C_ID + 128] = np.eye(128)
    consts[:, C_ONES:C_ONES + 128] = 1.0 / D
    consts[:, C_MASK:C_MASK + 128] = np.where(p[None, :] <= p[:, None], 0.0, -1e30)
    for k, (first, n) in enumerate(((0, 128), (128, 125), (253, 125), (418, 125), (543, 125), (378, 40))):
        consts[:, C_IDX + k] = np.where(p < n, first + p, -1)
    consts[:, C_POS] = p
    consts[:, C_TN] = p / 250
    consts[:, C_TN + 1] = (125 + p) / 250
    consts[:, C_POW:C_POW + 32] = 0.5 ** np.arange(32)
    consts[:, C_INC:C_INC + 32] = np.arange(32) + 1
    consts[:, C_VN:C_VN + 40] = (np.arange(40) - 32) / 32

    t = "L0_tok_"
    rows = np.concatenate([x[t + k] for k in ("time_lin_w", "dur_lin_w", "time_lin_b", "dur_lin_b", "time_w", "dur_w",
                                              "time_b", "dur_b", "vel_b2", "vel_ln_g", "vel_ln_b")])
    cols = np.zeros((128, K_ALL), f)
    cols[0:64, K_VW1] = x[t + "vel_w1"]
    cols[0:64, K_VB1] = x[t + "vel_b1"]
    q = "L0_ffn_"
    cols[:, K_GB1] = x[q + "gfc1_b"]
    cols[:, K_LNG] = x[q + "ln_g"]
    cols[:, K_LNB] = x[q + "ln_b"]
    cols[:, K_TVG:K_TVG + E0] = x[q + "tv_ln_g"].T
    cols[:, K_TVB:K_TVB + E0] = x[q + "tv_ln_b"].T
    cols[:, K_BOUT] = x["L1_attn_b_out"]

    def by_head(w, n):
        return w.reshape(H, n, -1).transpose(1, 0, 2).reshape(n, -1)
    a = "L0_attn_"
    a0 = np.stack([by_head(w, 128) for w in (x[a + "Wq"], x[a + "Wk"], x[a + "Wv"], x[a + "Wu"].T)], 1)
    a = "L1_attn_"
    a1 = np.stack([by_head(w, DH1) for w in (x[a + "w_q"].T, x[a + "w_k"].T, x[a + "w_v"].T, x[a + "w_out"])], 1)

    def modulated(w1, w2, b1, b2):
        return np.concatenate([w1.T, w2.T.reshape(4, 128, D).transpose(1, 0, 2).reshape(128, -1),
                               b1.reshape(4, 128).T, b2[:, None]], 1)
    ffn = np.stack([modulated(x[q + "W1"], x[q + "W2"], x[q + "b1"], x[q + "b2"])]
                   + [modulated(x[q + "tv_W1"][e], x[q + "tv_W2"][e], x[q + "tv_b1"][e], x[q + "tv_b2"][e])
                      for e in range(E0)])
    m = "L1_ffn_"
    ew = np.concatenate([x[m + "w1"], x[m + "w2"].reshape(E, 2, 128, D).transpose(0, 2, 1, 3).reshape(E, 128, 256),
                         x[m + "b1"].reshape(E, 2, 128).transpose(0, 2, 1)], 2)[::-1]
    given = {
        "tok": x["x"].reshape(T), "consts": consts, "rows": rows, "cols": cols, "emb": x[t + "token_emb"],
        "vel_w2t": x[t + "vel_w2"].T, "a0": a0, "gfc1t": x[q + "gfc1_w"].T, "gfc2t": x[q + "gfc2_w"].T,
        "gfc2b": x[q + "gfc2_b"], "ffn": ffn, "a1": a1, "rw": x[m + "router_w"][:, ::-1],
        "rb": x[m + "router_b"][::-1], "ew": ew, "eb2": x[m + "b2"][::-1],
    }
    given = {k: np.ascontiguousarray(v) for k, v in given.items()}
    nc = bacc.Bacc("TRN2", target_bir_lowering=False, num_devices=1)
    args = [nc.dram_tensor("in_" + k, v.shape, mybir.dt.from_np(v.dtype), kind="ExternalInput").ap()
            for k, v in given.items()]
    comb = nc.dram_tensor("comb", (E, T), F32, kind="Internal").ap()
    out = nc.dram_tensor("out", (D, T), F32, kind="ExternalOutput").ap()
    vocabulary_tower(nc, *args, comb, out)
    r = run_bass_kernel_spmd(nc, [{"in_" + k: v for k, v in given.items()}], core_ids=[0])
    return np.ascontiguousarray(r.results[0]["out"].T).reshape(B, S, D)
```

```python
import math

import concourse.bass as bass
from concourse import mybir
from contextlib import ExitStack

F32 = mybir.dt.float32
F32R = mybir.dt.float32r
BF16 = mybir.dt.bfloat16
I32 = mybir.dt.int32
ALU = mybir.AluOpType
ACT = mybir.ActivationFunctionType
AX = mybir.AxisListType

B, S, D = 4, 512, 128
T = B * S
NC = T // 512
H = 8
DH1 = 64
F0 = 512
E0 = 8
E, HF, TOPK = 64, 256, 42
DROP = E - TOPK
PADS = -DROP % 8
VC = 6
LN_EPS = 1e-5
LAG = 3
P0 = 4 * F0 // 2 + 5

C_ID, C_ONES, C_MASK = 0, 128, 256
C_IDX, C_POS, C_POW, C_INC, C_VN, C_TN = 384, 390, 392, 424, 456, 496
C_ALL = 498
R_LW, R_LB, R_W, R_B, R_B2, R_G, R_BETA, R_ALL = 0, 128, 256, 384, 512, 640, 768, 896
K_VW1, K_VB1, K_GB1, K_LNG, K_LNB, K_TVG, K_TVB, K_BOUT, K_ALL = 0, 1, 2, 3, 4, 5, 13, 21, 22


def vocabulary_tower(nc, tok, consts, rows, cols, emb, vel_w2t, a0, gfc1t, gfc2t, gfc2b, ffn, a1, rw, rb, ew, eb2,
                     comb_dram, out):
    ctx = ExitStack()
    with ctx:
        def sb(name, shape, dt):
            return ctx.enter_context(nc.sbuf_tensor(name, shape, dt))

        def sem(name):
            return ctx.enter_context(nc.semaphore(name))

        HT = sb("residual", [128, T], F32)
        XN = sb("normed", [128, T], F32)
        XHI = sb("normed_hi", [128, T], F32R)
        XLO = sb("normed_lo", [128, T], F32R)
        CS = sb("constants", [128, C_ALL], F32)
        RW_ = sb("row_params", [128, R_ALL], F32)
        CP = sb("col_params", [128, K_ALL], F32)
        V2T = sb("vel_w2t", [64, 128], F32)
        IDB = sb("ident_bf16", [128, 128], BF16)
        MKB = sb("mask_bf16", [128, 128], BF16)
        FA = sb("arena_f32", [128, 21568], F32)
        RA = sb("arena_f32r", [128, 17408], F32R)
        SM = sb("small", [128, 256], F32)

        def fa(at, n):
            return FA[:, at:at + n]

        def ra(at, n):
            return RA[:, at:at + n]

        ident = CS[:, C_ID:C_ID + 128]
        mean_w = CS[:, C_ONES:C_ONES + 128]
        mask = CS[:, C_MASK:C_MASK + 128]
        SQ = [fa(512 * i, 512) for i in range(NC)]
        TOKI = fa(2048, 2048).bitcast(I32)
        TOKF = fa(4096, 2048)
        TAB = fa(19501, 768)
        PH = fa(20269, 384)
        KQ = fa(20653, 384)
        VE = fa(21037, 128)
        VH = fa(21165, 40)
        VSQ = fa(21205, 128)
        THI, TLO = ra(0, 768), ra(768, 768)
        OH = [ra(11264 + 2048 * i, 2048) for i in range(2)]
        PB = [fa(2048 + 2048 * i, 2048).rearrange("p (i t) -> p i t", i=4) for i in range(2)]
        WL = fa(6144, 4096).rearrange("p (w c) -> p w c", w=4)
        XTM = ra(0, 4096)
        MN = ra(4096, 4096)
        XTB = ra(8192, 1024)
        QHI = [ra(11264 + 1024 * i, 512) for i in range(2)]
        QLO = [ra(11776 + 1024 * i, 512) for i in range(2)]
        PTHI = [ra(13312 + 1024 * i, 512) for i in range(2)]
        PTLO = [ra(13824 + 1024 * i, 512) for i in range(2)]
        OHI = [ra(15360 + 1024 * i, 512) for i in range(2)]
        OLO = [ra(15872 + 1024 * i, 512) for i in range(2)]
        NMAX = SM[:, 0:8]
        DEN = SM[:, 8:16]
        RDEN = SM[:, 16:24]
        TV = fa(10240, 9 * P0).rearrange("p (e c) -> p e c", e=9)
        WM = [fa(2048 + P0 * i, P0) for i in range(2)]
        H1F = [fa(4106 + 512 * i, 512) for i in range(2)]
        RES = [fa(19501 + 512 * i, 512) for i in range(2)]
        GF1 = fa(20525, 128)
        GF2 = fa(20653, 8)
        GF2B = fa(20661, 8)
        GMB = fa(20669, 128)
        G1HI, G1LO = ra(0, 128), ra(128, 128)
        WSP = [ra(11264 + 2048 * i, 2048) for i in range(2)]
        H1HI = [ra(15360 + 1024 * i, 512) for i in range(2)]
        H1LO = [ra(15872 + 1024 * i, 512) for i in range(2)]
        GS = SM[:, 24:28]
        G = SM[:, 32:64].rearrange("p (b e) -> p b e", b=B)
        LNG, LNB = SM[:, 64:65], SM[:, 65:66]
        WRAW = [fa(6144 + 514 * i, 514) for i in range(2)]
        HG = [fa(2048 + 1024 * i, 1024) for i in range(4)]
        CB = [fa(10240 + 2048 * i, 2048) for i in range(2)]
        CT = FA[0:E, 14336:14336 + T]
        LG = fa(16384, 1024).rearrange("p (c e) -> p c e", c=16)
        PR = fa(17408, 1024).rearrange("p (c e) -> p c e", c=16)
        CW = fa(18432, 1024).rearrange("p (c e) -> p c e", c=16)
        KP = fa(19456, 1024).rearrange("p (c e) -> p c e", c=16)
        LW = fa(20480, 16 * (E + PADS)).rearrange("p (c e) -> p c e", c=16)
        RWT = fa(9220, E)
        RBT = fa(9284, E)
        EB2 = FA[0:E, 9348:9348 + 128]
        HHI = [ra(1024 * i, 1024) for i in range(2)]
        HLO = [ra(2048 + 1024 * i, 1024) for i in range(2)]
        WHI = [ra(4096 + 1024 * i, 512) for i in range(2)]
        WLO = [ra(4608 + 1024 * i, 512) for i in range(2)]
        V8 = SM[:, 72:80]
        RS16 = SM[:, 80:96]
        MX16 = SM[:, 96:112]
        RP16 = SM[:, 112:128]
        D16 = SM[:, 128:144]
        EPS = SM[:, 144:145]
        ONE = CS[:, C_POW:C_POW + 1]
        TN = CS[:, C_TN:C_TN + 2]
        O1, O2, SEM_, SEMC = SM[:, 148:149], SM[:, 149:150], SM[:, 150:151], SM[:, 151:152]
        VM, VV, VS, VR = SM[:, 152:153], SM[:, 153:154], SM[:, 154:155], SM[:, 155:156]
        RSTD = SM[:, 168:184]
        TVS, T8 = SM[:, 156:158], SM[:, 160:168]

        PS = ctx.enter_context(nc.psum_tensor("banks", [128, 8 * 512], F32))

        def bank(i, n=1):
            return PS[:, 512 * i:512 * (i + n)]

        ld = {k: sem("ld_" + k) for k in ("tok", "const", "rows", "a0", "a1", "ffn", "moe")}
        dve_seq = sem("dve_seq")
        names = """tok_split onehot onehot_used tab_phase tab_sin vel_gelu vel_e vel_sq vel_std emb_tab emb_mm emb_out
            bf_ready eps_ready
            ln_mean ln_xc ln_sq ln_var ln_std ln_rstd ln_bc ln_out ln_src x_hi x_lo
            xt_mm xt_hi xt_lo mn_mm mn_hi mn_lo
            rden p_pool zero_banks xtb_hi xtb_lo q_mm q_hi q_lo s_mm nmax exp p_done pt_mm pt_hi pt_lo av o_hi o_lo y_mm y_add
            gate_w gate_mm gate_sum gate_bc gate_g gate_done mod w_hi w_lo h1_mm h1_act h1_lo y0_mm res0 lnp
            ffn_out logit_mm router dist probs pair comb comb_t comb_s comb_out seed
            wsplit h_mm gelu scaled hh hl down final out_done""".split()
        s = {k: sem(k) for k in names}
        wld = [sem(f"ld_expert{i}") for i in range(2)]
        cbd = [sem(f"ld_comb{i}") for i in range(2)]
        block = ctx.enter_context(nc.Block())

        def three(pe, o, w_hi, w_lo, x_hi, x_lo, start, stop, **kw):
            pe.matmul(o, w_hi, x_hi, start=start, stop=False, **kw)
            pe.matmul(o, w_hi, x_lo, start=False, stop=False, **kw)
            return pe.matmul(o, w_lo, x_hi, start=False, stop=stop, **kw)

        def bchunk(t, c):
            return t[:, 512 * c:512 * (c + 1)]

        ORDER = [[3, 2, 1, 0], [0, 1, 2, 3]]
        SBANK = [0, 1, 2, 5]

        def seen(layer, c):
            return 128 * (c + 1) if layer == 0 else 512

        def first_query(layer, j):
            return 128 * j if layer == 0 else 0

        @block.sync
        def _(sp):
            sp.dma_start(TOKI, tok.partition_broadcast(128)).then_inc(ld["tok"], 16)
            sp.dma_start(CS[:, :], consts).then_inc(ld["const"], 16)
            sp.dma_start(CP[:, :], cols).then_inc(ld["rows"], 16)
            sp.dma_start(RW_[:, :], rows.partition_broadcast(128)).then_inc(ld["rows"], 16)
            sp.dma_start(TAB[:, 0:128], emb).then_inc(ld["rows"], 16)
            sp.dma_start(V2T[:, :], vel_w2t).then_inc(ld["rows"], 16)
            sp.dma_start(WL, a0).then_inc(ld["a0"], 16)
            sp.dma_start(TV, ffn.rearrange("e p c -> p e c")).then_inc(ld["ffn"], 16)
            sp.wait_ge(s["emb_out"], 4)
            sp.dma_start(GF1, gfc1t).then_inc(ld["ffn"], 16)
            sp.dma_start(GF2, gfc2t).then_inc(ld["ffn"], 16)
            sp.dma_start(GF2B, gfc2b.partition_broadcast(128)).then_inc(ld["ffn"], 16)
            sp.wait_ge(s["mn_lo"], H)
            sp.wait_ge(s["mn_hi"], H)
            sp.dma_start(WL[0:DH1], a1).then_inc(ld["a1"], 16)
            sp.wait_ge(s["mn_lo"], 2 * H)
            sp.wait_ge(s["mn_hi"], 2 * H)
            sp.dma_start(RWT, rw).then_inc(ld["moe"], 16)
            sp.dma_start(RBT, rb.partition_broadcast(128)).then_inc(ld["moe"], 16)
            sp.dma_start(EB2, eb2).then_inc(ld["moe"], 16)
            sp.wait_ge(s["comb_s"], 4)
            sp.dma_start(comb_dram, CT).then_inc(s["comb_out"], 16)
            sp.wait_ge(s["comb_out"], 16)

            def expert(e, i):
                if not isinstance(e, int):
                    sp.wait_ge(s["gelu"], 4 * (e - 1))
                sp.dma_start(WRAW[i], ew[bass.ds(e, 1), :, :].rearrange("o p c -> (o p) c")).then_inc(wld[i], 16)
                if not isinstance(e, int):
                    sp.wait_ge(s["scaled"], 4 * (e - 1))
                sp.dma_start(CB[i], comb_dram[bass.ds(e, 1), :].rearrange("o t -> (o t)").partition_broadcast(128))\
                    .then_inc(cbd[i], 16)

            expert(0, 0)
            expert(1, 1)
            with sp.Fori(1, E // 2) as pair:
                expert(2 * pair, 0)
                expert(2 * pair + 1, 1)
            sp.wait_ge(s["final"], NC)
            sp.dma_start(out, HT[:, :]).then_inc(s["out_done"], 16)
            sp.wait_ge(s["out_done"], 16)

        @block.gpsimd
        def _(pool):
            def split_x(n):
                for c in range(NC):
                    pool.wait_ge(s["x_hi"], NC * n + c + 1)
                    nc.gpsimd.tensor_tensor(bchunk(XLO, c), bchunk(XN, c), bchunk(XHI, c).bitcast(F32), ALU.subtract)\
                        .then_inc(s["x_lo"], 1)

            def attention(layer):
                w = [seen(layer, c) for c in ORDER[layer]]
                with pool.Fori(0, B) as b:
                    for h in range(H):
                        for c in range(3):
                            i = h % 2
                            pool.wait_ge(s["rden"], 4 * (H * B * layer + H * b + h) + c + 1)
                            nc.gpsimd.tensor_tensor(PB[i][:, c, 0:w[c]], PB[i][:, c, 0:w[c]],
                                                    RDEN[:, 4 * i + c:4 * i + c + 1].to_broadcast([128, w[c]]),
                                                    ALU.mult).then_inc(s["p_pool"], 1)

            split_x(0)
            attention(0)
            split_x(1)
            for m in range(4 * B):
                pool.wait_ge(s["h1_act"], m + 1)
                nc.gpsimd.tensor_tensor(H1LO[m % 2], H1F[m % 2], H1HI[m % 2].bitcast(F32), ALU.subtract)\
                    .then_inc(s["h1_lo"], 1)
            split_x(2)
            attention(1)
            split_x(3)

            def split_weights(e, i):
                pool.wait_ge(wld[i], 8 * (e - i) + 16)
                nc.gpsimd.tensor_tensor(WHI[i], WRAW[i][:, 0:512], ONE.to_broadcast([128, 512]), ALU.mult)\
                    .then_inc(s["pair"], 1)
                pool.wait_ge(s["pair"], e + 1)
                nc.gpsimd.tensor_tensor(WLO[i], WRAW[i][:, 0:512], WHI[i].bitcast(F32), ALU.subtract)\
                    .then_inc(s["wsplit"], 1)

            for e in range(2):
                split_weights(e, e)
            with pool.Fori(1, E // 2) as pair:
                for i in range(2):
                    pool.wait_ge(s["down"], 4 * (2 * pair + i) - 4)
                    split_weights(2 * pair + i, i)

        @block.scalar
        def _(act):
            A = nc.scalar.activation
            act.wait_ge(ld["rows"], 64)
            act.wait_ge(ld["const"], 16)
            A(VH[0:64], CS[0:64, C_VN:C_VN + 40], ACT.Gelu, bias=CP[0:64, K_VB1:K_VB1 + 1],
              scale=CP[0:64, K_VW1:K_VW1 + 1]).then_inc(s["vel_gelu"], 1)
            act.wait_ge(s["tab_phase"], 1)
            tab = TAB.rearrange("p (k d) -> p k d", k=VC)
            A(tab[:, 1:5, 64:128], PH[:, 0:256].rearrange("p (k d) -> p k d", k=4), ACT.Sin).then_inc(s["tab_sin"], 1)
            A(tab[:, 5, :], PH[:, 256:384], ACT.Sin).then_inc(s["tab_sin"], 1)
            act.wait_ge(s["vel_sq"], 1)
            act.wait_ge(s["eps_ready"], 1)
            A(VS[0:40], VV[0:40], ACT.Sqrt, bias=EPS[0:40]).then_inc(s["vel_std"], 1)
            for c in range(NC):
                act.wait_ge(s["emb_mm"], c + 1)
                A(bchunk(HT, c), bank(c), ACT.Copy).then_inc(s["emb_out"], 1)

            def norm(n, split=None):
                def square(c):
                    act.wait_ge(s["ln_xc"], NC * n + c + 1)
                    A(SQ[c], bchunk(XN, c), ACT.Square).then_inc(s["ln_sq"], 1)

                def root(c):
                    act.wait_ge(s["ln_var"], NC * n + c + 1)
                    A(RSTD[:, 4 * c:4 * c + 4], bank(4 + c)[:, 0:4], ACT.Sqrt, bias=EPS)\
                        .then_inc(s["ln_std"], 1)
                for c in range(NC):
                    square(c)
                    if c >= 1:
                        root(c - 1)
                root(NC - 1)
                if split is not None:
                    for c in range(NC):
                        act.wait_ge(s["ln_out"], NC * n + c + 1)
                        A(bchunk(XHI, c), bchunk(XN, c), ACT.Copy).then_inc(s["x_hi"], 1)

            def tokens_out(layer):
                for c in range(NC):
                    act.wait_ge(s["xt_mm"], NC * layer + c + 1)
                    A(XTM[:, 1024 * c:1024 * c + 512], bank(4 + c), ACT.Copy).then_inc(s["xt_hi"], 1)

            def head_matrices(layer):
                scale = 1 / math.sqrt(D) if layer == 0 else 1 / math.sqrt(DH1)
                for h in range(H):
                    act.wait_ge(s["mn_mm"], H * layer + h + 1)
                    A(MN[:, 512 * h:512 * h + 128], bank(h % 4)[:, 0:128], ACT.Copy, scale=scale)
                    A(MN[:, 512 * h + 256:512 * h + 384], bank(h % 4)[:, 128:256], ACT.Copy).then_inc(s["mn_hi"], 1)

            def attention(layer):
                w = [seen(layer, c) for c in ORDER[layer]]
                lo = [first_query(layer, j) for j in ORDER[layer]]

                def query(n, i):
                    act.wait_ge(s["q_mm"], n)
                    A(QHI[i], bank(0), ACT.Copy).then_inc(s["q_hi"], 1)
                query((H * B + 1) * layer + 1, 0)

                def step(b, h, first, second):
                    i, v = h % 2, H * b + h
                    one, two = H * B * layer + v, (H * B + 1) * layer + v

                    def part(j):
                        act.wait_ge(s["pt_mm"], 4 * two + j + 1)
                        if j >= 2:
                            act.wait_ge(s["av"], 4 * two + j - 1)
                        A(PTHI[j % 2][:, lo[j]:512], bank(3 + j % 2)[:, lo[j]:512], ACT.Copy).then_inc(s["pt_hi"], 1)

                    def exps(c):
                        act.wait_ge(s["nmax"], 4 * one + c + 1)
                        A(PB[i][:, c, 0:w[c]], bank(SBANK[c])[:, 0:w[c]], ACT.Exp, bias=NMAX[:, 4 * i + c:4 * i + c + 1],
                          accum_out=DEN[:, 4 * i + c:4 * i + c + 1]).then_inc(s["exp"], 1)
                    if second:
                        part(0)
                        part(1)
                    if first:
                        exps(0)
                        exps(1)
                    if second:
                        part(2)
                    if first:
                        exps(2)
                    if second:
                        part(3)
                    if first:
                        query(two + 2, 1 - i)
                        exps(3)
                    if second:
                        act.wait_ge(s["av"], 4 * two + 4)
                        A(OHI[1 - i], bank(6), ACT.Copy).then_inc(s["o_hi"], 1)
                    if first and h == 0:
                        A(XTB[:, 0:512], XTM.bitcast(F32)[:, bass.ds(1024 * b, 512)], ACT.Copy).then_inc(s["xtb_hi"], 1)

                with act.Fori(0, B) as b:
                    for h in range(H):
                        step(b, h, True, True)
                step(B, 0, False, True)
                step(B, 1, False, False)

            norm(0, 0)
            head_matrices(0)
            tokens_out(0)
            attention(0)
            norm(1, 1)
            act.wait_ge(ld["ffn"], 64)
            A(G1HI, GF1, ACT.Copy).then_inc(s["gate_w"], 1)
            for b in range(B):
                act.wait_ge(s["gate_mm"], b + 1)
                A(fa(512 * b, 512), bank(4 + b), ACT.Relu, bias=CP[:, K_GB1:K_GB1 + 1], accum_out=GS[:, b:b + 1])\
                    .then_inc(s["gate_sum"], 1)
            for b in range(B):
                act.wait_ge(s["mod"], b + 1)
                if b >= 2:
                    act.wait_ge(s["y0_mm"], 4 * (b - 1))
                A(WSP[b % 2][:, 0:1024], WM[b % 2][:, 0:1024], ACT.Copy).then_inc(s["w_hi"], 1)
                for j in range(4):
                    m = 4 * b + j
                    act.wait_ge(s["h1_mm"], m + 1)
                    if m >= 2:
                        act.wait_ge(s["h1_lo"], m - 1)
                        act.wait_ge(s["y0_mm"], m - 1)
                    b1 = WM[b % 2][:, 1024 + j:1025 + j]
                    A(H1F[j % 2], bank(j % 2), ACT.Relu, bias=b1)
                    A(H1HI[j % 2], bank(j % 2), ACT.Relu, bias=b1).then_inc(s["h1_act"], 1)
            norm(2)
            norm(3, 2)
            head_matrices(1)
            tokens_out(1)
            attention(1)
            norm(4, 3)
            act.wait_ge(s["router"], 1)
            A(PR, LG, ACT.Exp).then_inc(s["dist"], 1)
            act.wait_ge(s["router"], 2)
            A(CW, PR, ACT.Exp).then_inc(s["dist"], 1)
            for c in range(NC):
                act.wait_ge(s["comb_t"], c + 1)
                A(CT[:, 512 * c:512 * (c + 1)], bank(c)[0:E], ACT.Copy).then_inc(s["comb_s"], 1)

            def hi_part(m, k):
                act.wait_ge(s["scaled"], m + 1)
                if not isinstance(m, int) or m >= 2:
                    act.wait_ge(s["down"], m - 1)
                A(HHI[k % 2], HG[k % 4], ACT.Copy).then_inc(s["hh"], 1)
            for k in range(4):
                act.wait_ge(s["h_mm"], k + 1)
                A(HG[k % 4], bank(4 + 2 * (k % 2), 2), ACT.Gelu, bias=WRAW[0][:, 512 + k // 2:513 + k // 2])\
                    .then_inc(s["gelu"], 1)
                if k >= 1:
                    hi_part(k - 1, k - 1)

            def expert(e, i):
                for k in range(4):
                    m = 4 * e + k
                    act.wait_ge(s["h_mm"], m + 1)
                    act.wait_ge(s["hl"], m - 3)
                    g = A(HG[k % 4], bank(4 + 2 * (k % 2), 2), ACT.Gelu, bias=WRAW[i][:, 512 + k // 2:513 + k // 2])
                    g.then_inc(s["gelu"], 1)
                    hi_part(m - 1, k + 3)
            expert(1, 1)
            with act.Fori(1, E // 2) as pair:
                expert(2 * pair, 0)
                expert(2 * pair + 1, 1)
            hi_part(4 * E - 1, 3)

        @block.vector
        def _(dve):
            V = nc.vector
            seq = [0]

            def link(ins):
                seq[0] += 1
                ins.then_inc(dve_seq, 1)
                dve.wait_ge(dve_seq, seq[0])

            V.memset(EPS, LN_EPS).then_inc(s["eps_ready"], 1)
            dve.wait_ge(ld["const"], 16)
            dve.wait_ge(ld["tok"], 16)
            V.tensor_copy(IDB[:, :], ident)
            V.tensor_copy(MKB[:, :], mask).then_inc(s["bf_ready"], 1)
            link(V.tensor_copy(TOKF, TOKI))
            link(V.tensor_scalar(TOKF, TOKF, 0.0, None, ALU.max))
            dve.wait_ge(ld["rows"], 64)
            tab = TAB.rearrange("p (k d) -> p k d", k=VC)
            pos = CS[:, C_POS:C_POS + 1]
            for kind in range(2):
                for j in range(2):
                    o = 64 * kind
                    V.scalar_tensor_tensor(tab[:, 1 + 2 * kind + j, 0:64], RW_[:, R_LW + o:R_LW + o + 64], TN[:, j:j + 1],
                                           RW_[:, R_LB + o:R_LB + o + 64], ALU.mult, ALU.add)
                    V.scalar_tensor_tensor(PH[:, 128 * kind + 64 * j:128 * kind + 64 * j + 64],
                                           RW_[:, R_W + o:R_W + o + 64], TN[:, j:j + 1],
                                           RW_[:, R_B + o:R_B + o + 64], ALU.mult, ALU.add)
            p0 = pos[:, 0:1]
            link(V.tensor_scalar(O1, p0, 12.0, None, ALU.is_ge))
            link(V.scalar_tensor_tensor(O2, p0, 24.0, O1, ALU.is_ge, ALU.add))
            link(V.scalar_tensor_tensor(SEM_, O2, -12.0, p0, ALU.mult, ALU.add))
            link(V.tensor_scalar(SEMC, SEM_, math.pi / 6.0, None, ALU.mult))
            pn = PH[:, 256:384].rearrange("p (i a b) -> p i a b", a=2, b=2)
            kn = KQ[:, 256:384].rearrange("p (i a b) -> p i a b", a=2, b=2)
            for b_ in range(2):
                V.tensor_scalar(pn[:, :, 0, b_], CS[:, C_POW:C_POW + 32], O2, None, ALU.mult)
                last = V.tensor_scalar(pn[:, :, 1, b_], CS[:, C_INC:C_INC + 32], SEMC, None, ALU.mult)
            link(last)
            link(V.tensor_scalar(KQ, PH, 1 / (2 * math.pi), None, ALU.mult))
            link(V.tensor_scalar(kn[:, :, :, 1], kn[:, :, :, 1], 0.25, None, ALU.add))
            link(V.tensor_scalar(KQ, KQ, 1.5 * 2 ** 23, None, ALU.add))
            link(V.tensor_scalar(KQ, KQ, 1.5 * 2 ** 23, None, ALU.subtract))
            link(V.scalar_tensor_tensor(PH, KQ, -6.28125, PH, ALU.mult, ALU.add))
            link(V.scalar_tensor_tensor(PH, KQ, -(2 * math.pi - 6.28125), PH, ALU.mult, ALU.add))
            link(V.tensor_scalar(pn[:, :, :, 1], pn[:, :, :, 1], math.pi / 2, None, ALU.add))
            V.tensor_scalar(PH, PH, -3.1415925, 3.1415925, ALU.max, ALU.min).then_inc(s["tab_phase"], 1)
            dve.wait_ge(s["vel_e"], 1)
            ve = VE[0:40]
            link(V.tensor_tensor(ve, bank(7)[0:40, 0:128], RW_[0:40, R_B2:R_B2 + 128], ALU.add))
            link(V.reduce_sum(VM[0:40], ve, AX.X))
            link(V.tensor_scalar(VM[0:40], VM[0:40], 1.0 / D, None, ALU.mult))
            link(V.tensor_scalar(ve, ve, VM[0:40], None, ALU.subtract))
            link(V.tensor_tensor(VSQ[0:40], ve, ve, ALU.mult))
            link(V.reduce_sum(VR[0:40], VSQ[0:40], AX.X))
            V.tensor_scalar(VV[0:40], VR[0:40], 1.0 / D, None, ALU.mult).then_inc(s["vel_sq"], 1)
            dve.wait_ge(s["vel_std"], 1)
            link(V.reciprocal(VS[0:40], VS[0:40]))
            link(V.tensor_scalar(ve, ve, VS[0:40], None, ALU.mult))
            link(V.tensor_tensor(ve, ve, RW_[0:40, R_G:R_G + 128], ALU.mult))
            dve.wait_ge(s["tab_sin"], 2)
            link(V.tensor_tensor(tab[32:40, 5, :], ve[32:40], RW_[32:40, R_BETA:R_BETA + 128], ALU.add))
            link(V.tensor_copy(THI, TAB))
            V.tensor_tensor(TLO, TAB, THI.bitcast(F32), ALU.subtract).then_inc(s["emb_tab"], 1)
            for k in range(VC):
                if k >= 2:
                    dve.wait_ge(s["onehot_used"], k - 1)
                V.tensor_scalar(OH[k % 2], TOKF, CS[:, C_IDX + k:C_IDX + k + 1], None, ALU.is_equal)\
                    .then_inc(s["onehot"], 1)

            def norm(n, src):
                def center(c):
                    dve.wait_ge(s["ln_mean"], NC * n + c + 1)
                    V.tensor_tensor(bchunk(XN, c), bchunk(src, c), bank(c), ALU.subtract).then_inc(s["ln_xc"], 1)

                def invert(c):
                    dve.wait_ge(s["ln_std"], NC * n + c + 1)
                    V.reciprocal(RSTD[:, 4 * c:4 * c + 4], RSTD[:, 4 * c:4 * c + 4]).then_inc(s["ln_rstd"], 1)

                def scale(c):
                    dve.wait_ge(s["ln_bc"], NC * n + c + 1)
                    V.tensor_tensor(bchunk(XN, c), bchunk(XN, c), bank(c), ALU.mult).then_inc(s["ln_out"], 1)
                for c in range(NC):
                    center(c)
                invert(0)
                for c in range(NC):
                    if c + 1 < NC:
                        invert(c + 1)
                    scale(c)

            def tokens_out(layer):
                for c in range(NC):
                    dve.wait_ge(s["xt_hi"], NC * layer + c + 1)
                    V.tensor_tensor(XTM[:, 1024 * c + 512:1024 * (c + 1)], bank(4 + c),
                                    XTM[:, 1024 * c:1024 * c + 512].bitcast(F32), ALU.subtract).then_inc(s["xt_lo"], 1)

            def head_matrices(layer):
                scale = 1 / math.sqrt(D) if layer == 0 else 1 / math.sqrt(DH1)
                for h in range(H):
                    dve.wait_ge(s["mn_hi"], H * layer + h + 1)
                    V.scalar_tensor_tensor(MN[:, 512 * h + 128:512 * h + 256], bank(h % 4)[:, 0:128], scale,
                                           MN[:, 512 * h:512 * h + 128].bitcast(F32), ALU.mult, ALU.subtract)
                    V.tensor_tensor(MN[:, 512 * h + 384:512 * h + 512], bank(h % 4)[:, 128:256],
                                    MN[:, 512 * h + 256:512 * h + 384].bitcast(F32), ALU.subtract)\
                        .then_inc(s["mn_lo"], 1)

            def attention(layer):
                w = [seen(layer, c) for c in ORDER[layer]]
                lo = [first_query(layer, j) for j in ORDER[layer]]
                V.memset(XTB.bitcast(F32), 0.0)
                V.memset(OHI[0].bitcast(F32), 0.0).then_inc(s["o_hi"], 1)
                V.memset(PB[1][:, 0:3, :], 0.0).then_inc(s["p_pool"], 3)
                V.memset(PB[1][:, 3, :], 0.0).then_inc(s["p_done"], 1)

                def query(n, i):
                    dve.wait_ge(s["q_hi"], n)
                    V.tensor_tensor(QLO[i], bank(0), QHI[i].bitcast(F32), ALU.subtract).then_inc(s["q_lo"], 1)
                query((H * B + 1) * layer + 1, 0)
                dve.wait_ge(s["zero_banks"], layer + 1)

                def step(b, h, first, second):
                    i, v = h % 2, H * b + h
                    one, two = H * B * layer + v, (H * B + 1) * layer + v

                    def part(j):
                        dve.wait_ge(s["pt_hi"], 4 * two + j + 1)
                        V.tensor_tensor(PTLO[j % 2][:, lo[j]:512], bank(3 + j % 2)[:, lo[j]:512],
                                        PTHI[j % 2][:, lo[j]:512].bitcast(F32), ALU.subtract).then_inc(s["pt_lo"], 1)

                    def top(c):
                        dve.wait_ge(s["s_mm"], 4 * one + c + 1)
                        V.tensor_reduce(NMAX[:, 4 * i + c:4 * i + c + 1], bank(SBANK[c])[:, 0:w[c]], AX.X, ALU.max,
                                        negate=True).then_inc(s["nmax"], 1)

                    def over(c):
                        col = slice(4 * i + c, 4 * i + c + 1)
                        dve.wait_ge(s["exp"], 4 * one + c + 1)
                        V.reciprocal(RDEN[:, col], DEN[:, col]).then_inc(s["rden"], 1)
                    if first:
                        top(0)
                    dve.wait_ge(s["o_hi"], (H * B + 2) * layer + v + 1)
                    V.tensor_tensor(OLO[i], bank(6), OHI[i].bitcast(F32), ALU.subtract).then_inc(s["o_lo"], 1)
                    if first:
                        top(1)
                    if second:
                        part(0)
                        part(1)
                    if h == 1:
                        at = bass.ds(512 * ((b + B - 1) % B), 512) if not isinstance(b, int) else slice(1536, 2048)
                        dve.wait_ge(s["y_mm"], (B + 1) * layer + b + 1)
                        V.tensor_tensor(HT[:, at], bank(7), HT[:, at], ALU.add).then_inc(s["y_add"], 1)
                    if first:
                        over(0)
                        top(2)
                        over(1)
                    if second:
                        part(2)
                    if first:
                        over(2)
                    if second:
                        part(3)
                    if first:
                        query(two + 2, 1 - i)
                        top(3)
                        over(3)
                        dve.wait_ge(s["rden"], 4 * one + 4)
                        V.tensor_scalar(PB[i][:, 3, 0:w[3]], PB[i][:, 3, 0:w[3]], RDEN[:, 4 * i + 3:4 * i + 4], None,
                                        ALU.mult).then_inc(s["p_done"], 1)
                    if first and h == 0:
                        dve.wait_ge(s["av"], 4 * two + 4)
                        V.tensor_copy(XTB[:, 512:1024], XTM.bitcast(F32)[:, bass.ds(1024 * b + 512, 512)])\
                            .then_inc(s["xtb_lo"], 1)

                with dve.Fori(0, B) as b:
                    for h in range(H):
                        step(b, h, True, True)
                step(B, 0, False, True)
                step(B, 1, False, False)

            norm(0, HT)
            head_matrices(0)
            tokens_out(0)
            attention(0)
            norm(1, HT)
            dve.wait_ge(s["gate_w"], 1)
            V.tensor_tensor(G1LO, GF1, G1HI.bitcast(F32), ALU.subtract).then_inc(s["gate_w"], 1)
            for b in range(B):
                dve.wait_ge(s["gate_sum"], b + 1)
                if b:
                    dve.wait_ge(s["gate_g"], b)
                V.tensor_scalar(GMB, GS[:, b:b + 1].to_broadcast([128, 128]), 1.0 / S, None, ALU.mult)\
                    .then_inc(s["gate_bc"], 1)
                dve.wait_ge(s["gate_g"], b + 1)
                link(V.tensor_tensor(G[:, b, :], bank(0)[:, 8 * b:8 * b + 8], GF2B, ALU.add))
            for col, base, o in ((K_TVG, K_LNG, LNG), (K_TVB, K_LNB, LNB)):
                link(V.tensor_scalar(T8, CP[:, col:col + E0], CP[:, base:base + 1], None, ALU.subtract))
                link(V.reduce_sum(TVS[:, 0:1], T8, AX.X))
                link(V.scalar_tensor_tensor(o, TVS[:, 0:1], 0.03, CP[:, base:base + 1], ALU.mult, ALU.add))

            def modulate(b):
                if b >= 2:
                    dve.wait_ge(s["res0"], b - 1)
                    dve.wait_ge(s["h1_act"], 4 * (b - 1))
                for e in range(E0):
                    ins = V.scalar_tensor_tensor(WM[b % 2], TV[:, 1 + e, :], G[:, b, e:e + 1],
                                                 TV[:, 0, :] if e == 0 else WM[b % 2], ALU.mult, ALU.add)
                    if e < E0 - 1:
                        link(ins)
                ins.then_inc(s["mod"], 1)

            def finish(b):
                dve.wait_ge(s["y0_mm"], 4 * (b + 1))
                V.scalar_tensor_tensor(bchunk(XN, b), bank(2 + b % 2), WM[b % 2][:, 1028:1029], bchunk(XN, b),
                                       ALU.add, ALU.add).then_inc(s["res0"], 1)
            for b in range(B):
                modulate(b)
                dve.wait_ge(s["w_hi"], b + 1)
                V.tensor_tensor(WSP[b % 2][:, 1024:2048], WM[b % 2][:, 0:1024], WSP[b % 2][:, 0:1024].bitcast(F32),
                                ALU.subtract).then_inc(s["w_lo"], 1)
                if b >= 1:
                    finish(b - 1)
            finish(B - 1)
            norm(2, XN)
            for c in range(NC):
                dve.wait_ge(s["ln_out"], NC * 2 + c + 1)
                link(V.tensor_scalar(bchunk(XN, c), bchunk(XN, c), LNG, LNB, ALU.mult, ALU.add))
                ins = V.tensor_tensor(bchunk(HT, c), bchunk(HT, c), bchunk(XN, c), ALU.add)
                ins.then_inc(s["ffn_out"], 1)
            norm(3, HT)
            head_matrices(1)
            tokens_out(1)
            attention(1)
            dve.wait_ge(s["y_add"], 2 * (B + 1))
            for c in range(NC):
                V.tensor_scalar(bchunk(HT, c), bchunk(HT, c), CP[:, K_BOUT:K_BOUT + 1], None, ALU.add)\
                    .then_inc(s["ln_src"], 1)
            norm(4, HT)
            dve.wait_ge(s["logit_mm"], 1)
            dve.wait_ge(ld["moe"], 48)

            def over(x):
                return x.unsqueeze(2).to_broadcast([128, 16, E])
            V.memset(LW[:, :, E:E + PADS], 1e30)
            link(V.tensor_tensor(LG, bank(4, 2).rearrange("p (c e) -> p c e", c=16),
                                 RBT.unsqueeze(1).to_broadcast([128, 16, E]), ALU.add))
            link(V.tensor_reduce(MX16, LG, AX.X, ALU.max))
            link(V.tensor_tensor(LG, LG, over(MX16), ALU.subtract))
            V.tensor_scalar(LG, LG, -87.33654, None, ALU.max).then_inc(s["router"], 1)
            dve.wait_ge(s["router"], 1)
            link(V.tensor_scalar(LW[:, :, 0:E], LG, -1.0, None, ALU.mult))
            for c in range(16):
                for r in range((DROP + PADS) // 8):
                    link(V.max(V8, LW[:, c, :]))
                    link(V.match_replace(LW[:, c, :], V8, LW[:, c, :], -1.0))
            dve.wait_ge(s["dist"], 1)
            link(V.reduce_sum(RS16, PR, AX.X))
            link(V.reciprocal(RP16, RS16))
            link(V.tensor_tensor(PR, PR, over(RP16), ALU.mult))
            link(V.tensor_reduce(MX16, PR, AX.X, ALU.max))
            V.tensor_tensor(PR, PR, over(MX16), ALU.subtract).then_inc(s["router"], 1)
            link(V.tensor_scalar(KP, LW[:, :, 0:E], 0.0, None, ALU.is_ge))
            dve.wait_ge(s["dist"], 2)
            link(V.tensor_tensor(CW, CW, KP, ALU.mult))
            link(V.reduce_sum(D16, CW, AX.X))
            link(V.reciprocal(D16, D16))
            V.tensor_tensor(CW, CW, over(D16), ALU.mult).then_inc(s["comb"], 1)

            def lo_part(m, k):
                dve.wait_ge(s["hh"], m + 1)
                V.tensor_tensor(HLO[k % 2], HG[k % 4], HHI[k % 2].bitcast(F32), ALU.subtract).then_inc(s["hl"], 1)

            def weigh(m, k, i):
                dve.wait_ge(s["gelu"], m + 1)
                V.tensor_tensor(HG[k % 4], HG[k % 4], CB[i][:, 1024 * (k % 2):1024 * (k % 2) + 1024], ALU.mult)\
                    .then_inc(s["scaled"], 1)

            def expert(e, i, first=False):
                for k in range(4):
                    m = 4 * e + k
                    if k == 0:
                        dve.wait_ge(cbd[i], 8 * (e - i) + 16)
                    weigh(m, k, i)
                    if not (first and k == 0):
                        lo_part(m - 1, k + 3)
            expert(0, 0, True)
            expert(1, 1)
            with dve.Fori(1, E // 2) as pair:
                expert(2 * pair, 0)
                expert(2 * pair + 1, 1)
            lo_part(4 * E - 1, 3)
            dve.wait_ge(s["down"], 4 * E)
            for c in range(NC):
                V.tensor_tensor(bchunk(HT, c), bchunk(HT, c), bank(c), ALU.add).then_inc(s["final"], 1)

        @block.tensor
        def _(pe):
            pe.wait_ge(ld["rows"], 64)
            pe.wait_ge(s["vel_gelu"], 1)
            pe.matmul(bank(7)[0:40, 0:128], VH[0:64], V2T[:, :], start=True, stop=True).then_inc(s["vel_e"], 1)
            pe.wait_ge(s["emb_tab"], 1)
            for k in range(VC):
                pe.wait_ge(s["onehot"], k + 1)
                for c in range(NC):
                    o = bank(c)
                    pe.matmul(o, THI[:, 128 * k:128 * (k + 1)], bchunk(OH[k % 2], c), start=(k == 0), stop=False)
                    ins = pe.matmul(o, TLO[:, 128 * k:128 * (k + 1)], bchunk(OH[k % 2], c), start=False,
                                    stop=(k == VC - 1))
                    if k == VC - 1:
                        ins.then_inc(s["emb_mm"], 1)
                if k < VC - 1:
                    ins.then_inc(s["onehot_used"], 1)

            def norm(n, src, ready):
                def var(c):
                    pe.wait_ge(s["ln_sq"], NC * n + c + 1)
                    for j in range(4):
                        ins = pe.matmul(bank(4 + c)[:, j:j + 1], SQ[c][:, 128 * j:128 * (j + 1)], mean_w[:, 0:1],
                                        start=True, stop=True)
                    ins.then_inc(s["ln_var"], 1)

                def spread(c):
                    pe.wait_ge(s["ln_rstd"], NC * n + c + 1)
                    for j in range(4):
                        ins = pe.matmul(bank(c)[:, 128 * j:128 * (j + 1)],
                                        RSTD[:, 4 * c + j:4 * c + j + 1].to_broadcast([128, 128]), ident, start=True,
                                        stop=True)
                    ins.then_inc(s["ln_bc"], 1)
                for c in range(NC):
                    ready(c)
                    pe.matmul(bank(c), mean_w, bchunk(src, c), start=True, stop=True).then_inc(s["ln_mean"], 1)
                for c in range(NC):
                    var(c)
                    if c >= 1:
                        spread(c - 1)
                spread(NC - 1)

            def tokens_out(layer):
                n = 0 if layer == 0 else 3
                for c in range(NC):
                    pe.wait_ge(s["ln_out"], NC * n + c + 1)
                    for j in range(4):
                        ins = pe.transpose(bank(4 + c)[:, 128 * j:128 * (j + 1)],
                                           XN[:, 512 * c + 128 * j:512 * c + 128 * (j + 1)], ident)
                    ins.then_inc(s["xt_mm"], 1)

            def head_matrices(layer):
                k = 128 if layer == 0 else DH1
                pe.wait_ge(ld["a0" if layer == 0 else "a1"], 16)
                pe.wait_ge(s["ln_out"], NC * (1 if layer == 0 else 4))
                for h in range(H):
                    if h >= 4:
                        pe.wait_ge(s["mn_lo"], H * layer + h - 3)
                    hs = slice(128 * h, 128 * (h + 1))
                    pe.matmul(bank(h % 4)[:, 0:128], WL[0:k, 0, hs], WL[0:k, 1, hs], start=True, stop=True)
                    pe.matmul(bank(h % 4)[:, 128:256], WL[0:k, 2, hs], WL[0:k, 3, hs], start=True, stop=True)\
                        .then_inc(s["mn_mm"], 1)

            def attention(layer):
                pe.wait_ge(s["x_lo"], NC * (1 if layer == 0 else 3))
                pe.wait_ge(s["mn_lo"], H * (layer + 1))
                pe.wait_ge(s["xt_lo"], NC * (layer + 1))

                def query(b, h):
                    m = MN[:, 512 * h:512 * h + 256]
                    at = bass.ds(512 * b, 512)
                    three(pe, bank(0), m[:, 0:128], m[:, 128:256], XHI[:, at], XLO[:, at], True, True)\
                        .then_inc(s["q_mm"], 1)
                query(0, 0)
                pe.wait_ge(s["p_done"], (H * B + 1) * layer + 1)
                pe.matmul(bank(7), XTB[:, 0:128], XTB[:, 0:512], start=True, stop=False, skip_group_check=True)
                pe.matmul(bank(6), XTB[:, 0:128], XTB[:, 0:512], start=True, stop=True).then_inc(s["zero_banks"], 1)

                def step(b, h, first, second):
                    i, v = h % 2, H * b + h
                    one, two = H * B * layer + v, (H * B + 1) * layer + v

                    def turn(k):
                        j = ORDER[layer][k]
                        if layer == 0:
                            pe.wait_ge(s["p_pool"], 3 * (one + layer) + min(k + 1, 3))
                        elif k == 0:
                            pe.wait_ge(s["p_pool"], 3 * (one + layer + 1))
                        if k == (3 if layer == 0 else 0):
                            pe.wait_ge(s["p_done"], one + layer + 1)
                        if k >= 2:
                            pe.wait_ge(s["pt_lo"], 4 * two + k - 1)
                        for c in range(j if layer == 0 else 0, 4):
                            ins = pe.transpose(bank(3 + k % 2)[:, 128 * c:128 * (c + 1)],
                                               PB[1 - i][:, ORDER[layer].index(c), 128 * j:128 * (j + 1)], ident)
                        ins.then_inc(s["pt_mm"], 1)

                    def scores(k):
                        c = ORDER[layer][k]
                        w = seen(layer, c)
                        if k == 0:
                            pe.wait_ge(s["q_lo"], two + 1)
                        elif h == 0:
                            pe.wait_ge(s["p_done"], one + layer + 1)
                        else:
                            pe.wait_ge(s["exp"], 4 * (one - 1) + k + 1)
                        qs = slice(128 * c, 128 * (c + 1))
                        o = bank(SBANK[k])[:, 0:w]
                        xh = XHI[:, bass.ds(512 * b, w)]
                        xl = XLO[:, bass.ds(512 * b, w)]
                        pe.matmul(o, QHI[i][:, qs], xh, start=True, stop=False)
                        if layer == 0:
                            pe.matmul(o[:, 128 * c:128 * (c + 1)], IDB[:, :], MKB[:, :], start=False, stop=False,
                                      skip_group_check=True)
                        pe.matmul(o, QHI[i][:, qs], xl, start=False, stop=False)
                        pe.matmul(o, QLO[i][:, qs], xh, start=False, stop=True).then_inc(s["s_mm"], 1)

                    def mix(k):
                        j = ORDER[layer][k]
                        at = first_query(layer, j)
                        if k == 0 and h == 1 and not isinstance(b, int):
                            pe.wait_ge(s["xtb_hi"], B * layer + b + 1)
                            pe.wait_ge(s["xtb_lo"], B * layer + b + 1)
                        if k == 0:
                            pe.wait_ge(s["o_lo"], (H * B + 2) * layer + v + 1)
                        pe.wait_ge(s["pt_lo"], 4 * two + k + 1)
                        three(pe, bank(6)[:, at:512], XTB[:, 128 * j:128 * (j + 1)],
                              XTB[:, 512 + 128 * j:512 + 128 * (j + 1)], PTHI[k % 2][:, at:512],
                              PTLO[k % 2][:, at:512], k == 0, k == 3, skip_group_check=True)\
                            .then_inc(s["av"], 1)

                    def project():
                        g = (h - 2) % H
                        pe.wait_ge(s["o_lo"], (H * B + 2) * layer + v + 1)
                        if g == 0:
                            pe.wait_ge(s["y_add"], (B + 1) * layer + b + 1)
                        n = MN[:, 512 * g + 256:512 * g + 512]
                        ins = three(pe, bank(7), n[:, 0:128], n[:, 128:256], OHI[i], OLO[i], g == 0, g == H - 1,
                                    skip_group_check=True)
                        if g == H - 1:
                            ins.then_inc(s["y_mm"], 1)
                    if first:
                        scores(0)
                        scores(1)
                    if second:
                        turn(0)
                        turn(1)
                    project()
                    if first:
                        scores(2)
                    if second:
                        mix(0)
                        turn(2)
                        mix(1)
                        turn(3)
                    if first:
                        pe.wait_ge(s["exp"], 4 * one + 1)
                        query((b + 1) % B if h == H - 1 else b, (h + 1) % H)
                        scores(3)
                    if second:
                        mix(2)
                        mix(3)

                with pe.Fori(0, B) as b:
                    for h in range(H):
                        step(b, h, True, True)
                step(B, 0, False, True)
                step(B, 1, False, False)

            norm(0, HT, lambda c: pe.wait_ge(s["emb_out"], NC))
            head_matrices(0)
            tokens_out(0)
            attention(0)
            norm(1, HT, lambda c: pe.wait_ge(s["y_add"], B + 1))
            pe.wait_ge(s["x_lo"], 2 * NC)
            pe.wait_ge(s["gate_w"], 2)
            for b in range(B):
                three(pe, bank(4 + b), G1HI, G1LO, bchunk(XHI, b), bchunk(XLO, b), True, True).then_inc(s["gate_mm"], 1)
            for b in range(B):
                pe.wait_ge(s["gate_bc"], b + 1)
                pe.matmul(bank(0)[:, 8 * b:8 * b + 8], GMB, GF2, start=True, stop=True).then_inc(s["gate_g"], 1)

            def up(m):
                b, j = m // 4, m % 4
                if j == 0:
                    pe.wait_ge(s["w_lo"], b + 1)
                if m >= 2:
                    pe.wait_ge(s["h1_act"], m - 1)
                w = WSP[b % 2]
                three(pe, bank(m % 2), w[:, 128 * j:128 * (j + 1)], w[:, 1024 + 128 * j:1024 + 128 * (j + 1)],
                      bchunk(XHI, b), bchunk(XLO, b), True, True).then_inc(s["h1_mm"], 1)

            def down0(m):
                b, j = m // 4, m % 4
                if j == 0 and b >= 2:
                    pe.wait_ge(s["res0"], b - 1)
                pe.wait_ge(s["h1_lo"], m + 1)
                w = WSP[b % 2]
                three(pe, bank(2 + b % 2), w[:, 512 + 128 * j:512 + 128 * (j + 1)],
                      w[:, 1536 + 128 * j:1536 + 128 * (j + 1)], H1HI[m % 2], H1LO[m % 2], j == 0, j == 3)\
                    .then_inc(s["y0_mm"], 1)
            for m in range(4 * B + 2):
                if m < 4 * B:
                    up(m)
                if m >= 2:
                    down0(m - 2)
            norm(2, XN, lambda c: pe.wait_ge(s["res0"], B))
            norm(3, HT, lambda c: pe.wait_ge(s["ffn_out"], c + 1))
            head_matrices(1)
            tokens_out(1)
            attention(1)
            norm(4, HT, lambda c: pe.wait_ge(s["ln_src"], c + 1))
            pe.wait_ge(ld["moe"], 48)
            pe.wait_ge(s["ln_out"], 5 * NC)
            for c in range(16):
                ins = pe.matmul(PS[:, 2048 + E * c:2048 + E * (c + 1)], XN[:, 128 * c:128 * (c + 1)], RWT, start=True,
                                stop=True)
            ins.then_inc(s["logit_mm"], 1)
            pe.wait_ge(s["comb"], 1)
            for c in range(NC):
                for j in range(4):
                    ins = pe.transpose(bank(c)[0:E, 128 * j:128 * (j + 1)], CW[:, 4 * c + j, :], ident)
                ins.then_inc(s["comb_t"], 1)
            pe.wait_ge(s["comb_s"], NC)
            for c in range(NC):
                pe.matmul(bank(c), EB2, CT[:, 512 * c:512 * (c + 1)], start=True, stop=False, skip_group_check=True)

            pe.wait_ge(s["x_lo"], 4 * NC)

            def rise(m, k, i):
                if not isinstance(m, int) or m >= 2:
                    pe.wait_ge(s["gelu"], m - 1)
                f = slice(128 * (k // 2), 128 * (k // 2 + 1))
                for j in range(2):
                    c = 2 * (k % 2) + j
                    ins = three(pe, bank(4 + 2 * (k % 2) + j), WHI[i][:, f], WLO[i][:, f], bchunk(XHI, c), bchunk(XLO, c),
                                True, True)
                ins.then_inc(s["h_mm"], 1)

            def fall(m, k, i, last=False):
                pe.wait_ge(s["hl"], m + 1)
                f = slice(256 + 128 * (k // 2), 256 + 128 * (k // 2 + 1))
                for j in range(2):
                    c = 2 * (k % 2) + j
                    h = slice(512 * j, 512 * (j + 1))
                    ins = three(pe, bank(c), WHI[i][:, f], WLO[i][:, f], HHI[k % 2][:, h], HLO[k % 2][:, h], False, last,
                                skip_group_check=True)
                ins.then_inc(s["down"], 1)

            def expert(e, i):
                pe.wait_ge(s["wsplit"], e + 1)
                for k in range(4):
                    rise(4 * e + k, k, i)
                    if not (isinstance(e, int) and e == 0 and k < LAG):
                        fall(4 * e + k - LAG, (k - LAG) % 4, i if k >= LAG else 1 - i)
            expert(0, 0)
            expert(1, 1)
            with pe.Fori(1, E // 2) as pair:
                expert(2 * pair, 0)
                expert(2 * pair + 1, 1)
            for m in range(4 * E - LAG, 4 * E):
                fall(m, m % 4, 1, last=m >= 4 * E - 2)


def kernel(**inputs):
    import numpy as np
    import concourse.bacc as bacc
    from concourse.bass_utils import run_bass_kernel_spmd

    x = {k: np.asarray(v) for k, v in inputs.items()}
    f = np.float32

    consts = np.zeros((128, C_ALL), f)
    p = np.arange(128)
    consts[:, C_ID:C_ID + 128] = np.eye(128)
    consts[:, C_ONES:C_ONES + 128] = 1.0 / D
    consts[:, C_MASK:C_MASK + 128] = np.where(p[None, :] <= p[:, None], 0.0, -1e30)
    for k, (first, n) in enumerate(((0, 128), (128, 125), (253, 125), (418, 125), (543, 125), (378, 40))):
        consts[:, C_IDX + k] = np.where(p < n, first + p, -1)
    consts[:, C_POS] = p
    consts[:, C_TN] = p / 250
    consts[:, C_TN + 1] = (125 + p) / 250
    consts[:, C_POW:C_POW + 32] = 0.5 ** np.arange(32)
    consts[:, C_INC:C_INC + 32] = np.arange(32) + 1
    consts[:, C_VN:C_VN + 40] = (np.arange(40) - 32) / 32

    t = "L0_tok_"
    rows = np.concatenate([x[t + k] for k in ("time_lin_w", "dur_lin_w", "time_lin_b", "dur_lin_b", "time_w", "dur_w",
                                              "time_b", "dur_b", "vel_b2", "vel_ln_g", "vel_ln_b")])
    cols = np.zeros((128, K_ALL), f)
    cols[0:64, K_VW1] = x[t + "vel_w1"]
    cols[0:64, K_VB1] = x[t + "vel_b1"]
    q = "L0_ffn_"
    cols[:, K_GB1] = x[q + "gfc1_b"]
    cols[:, K_LNG] = x[q + "ln_g"]
    cols[:, K_LNB] = x[q + "ln_b"]
    cols[:, K_TVG:K_TVG + E0] = x[q + "tv_ln_g"].T
    cols[:, K_TVB:K_TVB + E0] = x[q + "tv_ln_b"].T
    cols[:, K_BOUT] = x["L1_attn_b_out"]

    def by_head(w, n):
        return w.reshape(H, n, -1).transpose(1, 0, 2).reshape(n, -1)
    a = "L0_attn_"
    a0 = np.stack([by_head(w, 128) for w in (x[a + "Wq"], x[a + "Wk"], x[a + "Wv"], x[a + "Wu"].T)], 1)
    a = "L1_attn_"
    a1 = np.stack([by_head(w, DH1) for w in (x[a + "w_q"].T, x[a + "w_k"].T, x[a + "w_v"].T, x[a + "w_out"])], 1)

    def modulated(w1, w2, b1, b2):
        return np.concatenate([w1.T, w2.T.reshape(4, 128, D).transpose(1, 0, 2).reshape(128, -1),
                               b1.reshape(4, 128).T, b2[:, None]], 1)
    ffn = np.stack([modulated(x[q + "W1"], x[q + "W2"], x[q + "b1"], x[q + "b2"])]
                   + [modulated(x[q + "tv_W1"][e], x[q + "tv_W2"][e], x[q + "tv_b1"][e], x[q + "tv_b2"][e])
                      for e in range(E0)])
    m = "L1_ffn_"
    ew = np.concatenate([x[m + "w1"], x[m + "w2"].reshape(E, 2, 128, D).transpose(0, 2, 1, 3).reshape(E, 128, 256),
                         x[m + "b1"].reshape(E, 2, 128).transpose(0, 2, 1)], 2)[::-1]
    given = {
        "tok": x["x"].reshape(T), "consts": consts, "rows": rows, "cols": cols, "emb": x[t + "token_emb"],
        "vel_w2t": x[t + "vel_w2"].T, "a0": a0, "gfc1t": x[q + "gfc1_w"].T, "gfc2t": x[q + "gfc2_w"].T,
        "gfc2b": x[q + "gfc2_b"], "ffn": ffn, "a1": a1, "rw": x[m + "router_w"][:, ::-1],
        "rb": x[m + "router_b"][::-1], "ew": ew, "eb2": x[m + "b2"][::-1],
    }
    given = {k: np.ascontiguousarray(v) for k, v in given.items()}
    nc = bacc.Bacc("TRN2", target_bir_lowering=False, num_devices=1)
    args = [nc.dram_tensor("in_" + k, v.shape, mybir.dt.from_np(v.dtype), kind="ExternalInput").ap()
            for k, v in given.items()]
    comb = nc.dram_tensor("comb", (E, T), F32, kind="Internal").ap()
    out = nc.dram_tensor("out", (D, T), F32, kind="ExternalOutput").ap()
    vocabulary_tower(nc, *args, comb, out)
    r = run_bass_kernel_spmd(nc, [{"in_" + k: v for k, v in given.items()}], core_ids=[0])
    return np.ascontiguousarray(r.results[0]["out"].T).reshape(B, S, D)
```

```python
import math

import concourse.bass as bass
from concourse import mybir
from contextlib import ExitStack

F32 = mybir.dt.float32
F32R = mybir.dt.float32r
BF16 = mybir.dt.bfloat16
I32 = mybir.dt.int32
ALU = mybir.AluOpType
ACT = mybir.ActivationFunctionType
AX = mybir.AxisListType

B, S, D = 4, 512, 128
T = B * S
NC = T // 512
H = 8
DH1 = 64
F0 = 512
E0 = 8
E, TOPK = 64, 42
DROP = E - TOPK
PADS = -DROP % 8
VC = 6
LN_EPS = 1e-5
LAG = 3
PW = 256
P0 = 4 * F0 // 2 + 5

C_ID, C_ONES, C_MASK = 0, 128, 256
C_IDX, C_POS, C_POW, C_INC, C_VN, C_TN = 384, 390, 392, 424, 456, 496
C_ALL = 498
R_LW, R_LB, R_W, R_B, R_B2, R_G, R_BETA, R_ALL = 0, 128, 256, 384, 512, 640, 768, 896
K_VW1, K_VB1, K_GB1, K_LNG, K_LNB, K_TVG, K_TVB, K_BOUT, K_ALL = 0, 1, 2, 3, 4, 5, 13, 21, 22


def vocabulary_tower(nc, tok, consts, rows, cols, emb, vel_w2t, a0, gfc1t, gfc2t, gfc2b, ffn, a1, rw, rb, ew, eb2,
                     comb_dram, out):
    ctx = ExitStack()
    with ctx:
        def sb(name, shape, dt):
            return ctx.enter_context(nc.sbuf_tensor(name, shape, dt))

        def sem(name):
            return ctx.enter_context(nc.semaphore(name))

        HT = sb("residual", [128, T], F32)
        XN = sb("normed", [128, T], F32)
        XHI = sb("normed_hi", [128, T], F32R)
        XLO = sb("normed_lo", [128, T], F32R)
        CS = sb("constants", [128, C_ALL], F32)
        RW_ = sb("row_params", [128, R_ALL], F32)
        CP = sb("col_params", [128, K_ALL], F32)
        V2T = sb("vel_w2t", [64, 128], F32)
        IDB = sb("ident_bf16", [128, 128], BF16)
        MKB = sb("mask_bf16", [128, 128], BF16)
        FA = sb("arena_f32", [128, 21568], F32)
        RA = sb("arena_f32r", [128, 17408], F32R)
        SM = sb("small", [128, 256], F32)

        def fa(at, n):
            return FA[:, at:at + n]

        def ra(at, n):
            return RA[:, at:at + n]

        ident = CS[:, C_ID:C_ID + 128]
        mean_w = CS[:, C_ONES:C_ONES + 128]
        mask = CS[:, C_MASK:C_MASK + 128]
        SQ = [fa(512 * i, 512) for i in range(NC)]
        TOKI = fa(2048, 2048).bitcast(I32)
        DIST = fa(2048, 2048)
        TOKF = fa(4096, 2048)
        TAB = fa(19501, 768)
        PH = fa(20269, 384)
        KQ = fa(20653, 384)
        VE = fa(21037, 128)
        VH = fa(21165, 40)
        VSQ = fa(21205, 128)
        THI, TLO = ra(0, 768), ra(768, 768)
        OH = [ra(at, 2048) for at in (11264, 13312, 11264, 13312, 9216, 15360)]
        PB = [fa(2048 + 2048 * i, 2048).rearrange("p (i t) -> p i t", i=4) for i in range(2)]
        WL = fa(6144, 4096).rearrange("p (w c) -> p w c", w=4)
        XTM = ra(0, 4096)
        MN = ra(4096, 4096)
        XTB = ra(8192, 1024)
        QHI = [ra(11264 + 1024 * i, 512) for i in range(2)]
        QLO = [ra(11776 + 1024 * i, 512) for i in range(2)]
        PTHI = [ra(13312 + 1024 * i, 512) for i in range(2)]
        PTLO = [ra(13824 + 1024 * i, 512) for i in range(2)]
        OHI = [ra(15360 + 1024 * i, 512) for i in range(2)]
        OLO = [ra(15872 + 1024 * i, 512) for i in range(2)]
        NMAX = SM[:, 0:8]
        DEN = SM[:, 8:16]
        RDEN = SM[:, 16:24]
        TV = fa(10240, 9 * P0).rearrange("p (e c) -> p e c", e=9)
        WM = [fa(2048 + P0 * i, P0) for i in range(2)]
        H1F = [fa(at, 512) for at in (4106, 4618, 19501, 20013)]
        GF1 = fa(20525, 128)
        GF2 = fa(20653, 8)
        GF2B = fa(20661, 8)
        GMB = fa(20669, 128)
        G1HI, G1LO = ra(0, 128), ra(128, 128)
        WSP = [ra(11264 + 2048 * i, 2048) for i in range(2)]
        H1HI = [ra(at, 512) for at in (15360, 16384, 1024, 2048)]
        H1LO = [ra(at, 512) for at in (15872, 16896, 1536, 2560)]
        UP = [0, 1, 6, 7]
        DG = [fa(7172 + 1024 * i, 1024) for i in range(2)]
        GS = SM[:, 24:28]
        G = SM[:, 32:64].rearrange("p (b e) -> p b e", b=B)
        LNG, LNB = SM[:, 64:65], SM[:, 65:66]
        WRAW = [fa(6144 + 514 * i, 514) for i in range(2)]
        HG = [fa(2048 + 1024 * i, 1024) for i in range(4)]
        CB = [fa(10240 + 2048 * i, 2048) for i in range(2)]
        CT = FA[0:E, 14336:14336 + T]
        LG = fa(16384, 1024).rearrange("p (c e) -> p c e", c=16)
        PR = fa(17408, 1024).rearrange("p (c e) -> p c e", c=16)
        CW = fa(18432, 1024).rearrange("p (c e) -> p c e", c=16)
        LW = fa(20480, 16 * (E + PADS)).rearrange("p (c e) -> p c e", c=16)
        RWT = fa(9220, E)
        RBT = fa(9284, E)
        EB2 = FA[0:E, 9348:9348 + 128]
        HHI = [ra(1024 * i, 1024) for i in range(2)]
        HLO = [ra(2048 + 1024 * i, 1024) for i in range(2)]
        WHI = [ra(4096 + 1024 * i, 512) for i in range(2)]
        WLO = [ra(4608 + 1024 * i, 512) for i in range(2)]
        V8 = [SM[:, 184 + 8 * j:192 + 8 * j] for j in range(4)]
        RS16 = SM[:, 80:96]
        MX16 = SM[:, 96:112]
        RP16 = SM[:, 112:128]
        NRP16 = SM[:, 216:232]
        D16 = SM[:, 128:144]
        EPS = SM[:, 144:145]
        ONE = CS[:, C_POW:C_POW + 1]
        TN = CS[:, C_TN:C_TN + 2]
        O1, O2, SEM_, SEMC = SM[:, 148:149], SM[:, 149:150], SM[:, 150:151], SM[:, 151:152]
        VM, VV, VS, VR = SM[:, 152:153], SM[:, 153:154], SM[:, 154:155], SM[:, 155:156]
        RSTD = SM[:, 168:184]
        TVS, T16 = SM[:, 156:158], SM[:, 232:248]

        PS = ctx.enter_context(nc.psum_tensor("banks", [128, 8 * 512], F32))

        def bank(i, n=1):
            return PS[:, 512 * i:512 * (i + n)]

        ld = {k: sem("ld_" + k) for k in ("tok", "const", "rows", "a0", "a1", "ffn", "moe")}
        dve_seq = sem("dve_seq")
        names = """tokens onehot onehot_sq onehot_late onehot_used tab_phase tab_sin vel_gelu vel_e vel_sq vel_std emb_tab emb_mm emb_out
            bf_ready eps_ready
            ln_mean ln_xc ln_sq ln_var ln_std ln_rstd ln_bc ln_out x_hi x_lo
            xt_mm xt_hi xt_lo mn_mm mn_hi mn_lo
            rden p_pool zero_banks xtb_hi xtb_lo q_mm q_hi q_lo s_mm nmax exp p_done pt_mm pt_hi pt_lo av o_hi o_lo y_mm y_add
            gate_w gate_mm gate_sum gate_bc gate_g gates diag mod_pe mod w_hi w_lo h1_mm h1_act h1_lo y0_mm res0 ln_gain offset
            ffn_out logit_mm router dist inv_sum shares pair comb comb_t comb_s comb_bc comb_b comb_out
            wsplit1 wsplit2 h_mm gelu scaled hh hl down final out_done""".split()
        s = {k: sem(k) for k in names}
        wld = [sem(f"ld_expert{i}") for i in range(2)]
        cbd = [sem(f"ld_comb{i}") for i in range(2)]
        block = ctx.enter_context(nc.Block())

        def three(pe, o, w_hi, w_lo, x_hi, x_lo, start, stop, **kw):
            pe.matmul(o, w_hi, x_hi, start=start, stop=False, **kw)
            pe.matmul(o, w_hi, x_lo, start=False, stop=False, **kw)
            return pe.matmul(o, w_lo, x_hi, start=False, stop=stop, **kw)

        def bchunk(t, c):
            return t[:, 512 * c:512 * (c + 1)]

        ORDER = [[3, 2, 1, 0], [0, 1, 2, 3]]
        SBANK = [0, 1, 2, 5]

        def seen(layer, c):
            return 128 * (c + 1) if layer == 0 else 512

        AFTER = [1, 4]

        def early(n):
            return NC - 1 if n in AFTER else 0

        def first_query(layer, j):
            return 128 * j if layer == 0 else 0

        def pair_bank(layer, h):
            return bank((4 if layer == 0 else 0) + h // 2)[:, 256 * (h % 2):256 * (h % 2) + 256]

        @block.sync
        def _(sp):
            sp.dma_start(TOKI, tok.partition_broadcast(128)).then_inc(ld["tok"], 16)
            sp.dma_start(CS[:, :], consts).then_inc(ld["const"], 16)
            sp.dma_start(CP[:, :], cols).then_inc(ld["rows"], 16)
            sp.dma_start(RW_[:, :], rows.partition_broadcast(128)).then_inc(ld["rows"], 16)
            sp.dma_start(TAB[:, 0:128], emb).then_inc(ld["rows"], 16)
            sp.dma_start(V2T[:, :], vel_w2t).then_inc(ld["rows"], 16)
            sp.dma_start(WL, a0).then_inc(ld["a0"], 16)
            sp.dma_start(TV, ffn.rearrange("e p c -> p e c")).then_inc(ld["ffn"], 16)
            sp.wait_ge(s["emb_out"], 4)
            sp.dma_start(GF1, gfc1t).then_inc(ld["ffn"], 16)
            sp.dma_start(GF2, gfc2t).then_inc(ld["ffn"], 16)
            sp.dma_start(GF2B, gfc2b.partition_broadcast(128)).then_inc(ld["ffn"], 16)
            sp.wait_ge(s["mn_lo"], H)
            sp.wait_ge(s["mn_hi"], H)
            sp.dma_start(WL[0:DH1], a1).then_inc(ld["a1"], 16)
            sp.wait_ge(s["mn_lo"], 2 * H)
            sp.wait_ge(s["mn_hi"], 2 * H)
            sp.dma_start(RWT, rw).then_inc(ld["moe"], 16)
            sp.dma_start(RBT, rb.partition_broadcast(128)).then_inc(ld["moe"], 16)
            sp.dma_start(EB2, eb2).then_inc(ld["moe"], 16)

            def weights(e, i):
                sp.dma_start(WRAW[i], ew[bass.ds(e, 1), :, :].rearrange("o p c -> (o p) c")).then_inc(wld[i], 16)

            def shares(e, i):
                sp.dma_start(CB[i], comb_dram[bass.ds(e, 1), :].rearrange("o t -> (o t)").partition_broadcast(128))\
                    .then_inc(cbd[i], 16)
            weights(0, 0)
            weights(1, 1)
            sp.wait_ge(s["comb_s"], 4)
            sp.dma_start(comb_dram, CT).then_inc(s["comb_out"], 16)
            sp.wait_ge(s["comb_out"], 16)

            shares(1, 1)

            def expert(e, i):
                sp.wait_ge(s["down"], 4 * e - 5)
                weights(e, i)
                sp.wait_ge(s["scaled"], 4 * (e - 1))
                shares(e, i)

            with sp.Fori(1, E // 2) as pair:
                expert(2 * pair, 0)
                expert(2 * pair + 1, 1)
            for half in range(2):
                sp.wait_ge(s["final"], 2 * half + 2)
                sp.dma_start(out[:, T // 2 * half:T // 2 * (half + 1)], HT[:, T // 2 * half:T // 2 * (half + 1)])\
                    .then_inc(s["out_done"], 16)
            sp.wait_ge(s["out_done"], 32)

        @block.gpsimd
        def _(pool):
            def split_x(n):
                for c in range(NC):
                    pool.wait_ge(s["x_hi"], NC * n + c + 1)
                    nc.gpsimd.tensor_tensor(bchunk(XLO, c), bchunk(XN, c), bchunk(XHI, c).bitcast(F32), ALU.subtract)\
                        .then_inc(s["x_lo"], 1)

            def attention(layer):
                w = [seen(layer, c) for c in ORDER[layer]]
                with pool.Fori(0, B) as b:
                    for h in range(H):
                        for c in range(3):
                            i = h % 2
                            pool.wait_ge(s["rden"], 4 * (H * B * layer + H * b + h) + c + 1)
                            nc.gpsimd.tensor_tensor(PB[i][:, c, 0:w[c]], PB[i][:, c, 0:w[c]],
                                                    RDEN[:, 4 * i + c:4 * i + c + 1].to_broadcast([128, w[c]]),
                                                    ALU.mult).then_inc(s["p_pool"], 1)

            def zero_heads():
                nc.gpsimd.memset(XTB.bitcast(F32), 0.0)
                nc.gpsimd.memset(OHI[0].bitcast(F32), 0.0).then_inc(s["o_hi"], 1)
                nc.gpsimd.memset(PB[1][:, 0:3, :], 0.0).then_inc(s["p_pool"], 3)
                nc.gpsimd.memset(PB[1][:, 3, :], 0.0).then_inc(s["p_done"], 1)
            pool.wait_ge(s["emb_mm"], NC)
            nc.gpsimd.memset(NMAX, 0.0).then_inc(s["exp"], 4)
            zero_heads()
            split_x(0)
            attention(0)
            split_x(1)
            pool.wait_ge(s["ln_gain"], 2)
            for c in range(NC):
                nc.gpsimd.tensor_tensor(bchunk(HT, c), bchunk(HT, c), LNB.to_broadcast([128, 512]), ALU.add)\
                    .then_inc(s["offset"], 1)

            for m in range(4 * B):
                pool.wait_ge(s["h1_act"], m + 1)
                nc.gpsimd.tensor_tensor(H1LO[m % 4], H1F[m % 4], H1HI[m % 4].bitcast(F32), ALU.subtract)\
                    .then_inc(s["h1_lo"], 1)
            pool.wait_ge(s["res0"], B)
            zero_heads()
            split_x(2)
            for c in range(NC):
                nc.gpsimd.tensor_tensor(bchunk(HT, c), bchunk(HT, c),
                                        CP[:, K_BOUT:K_BOUT + 1].to_broadcast([128, 512]), ALU.add)\
                    .then_inc(s["offset"], 1)
            attention(1)
            split_x(3)

            def split_weights(e, i, w):
                c = slice(256 * w, 256 * w + 256)
                nc.gpsimd.tensor_tensor(WHI[i][:, c], WRAW[i][:, c], ONE.to_broadcast([128, 256]), ALU.mult)\
                    .then_inc(s["pair"], 1)
                pool.wait_ge(s["pair"], 2 * e + w + 1)
                nc.gpsimd.tensor_tensor(WLO[i][:, c], WRAW[i][:, c], WHI[i][:, c].bitcast(F32), ALU.subtract)\
                    .then_inc(s["wsplit2" if w else "wsplit1"], 1)

            for e in range(2):
                pool.wait_ge(wld[e], 16)
                split_weights(e, e, 0)
                split_weights(e, e, 1)
            with pool.Fori(1, E // 2) as pair:
                for i in range(2):
                    e = 2 * pair + i
                    pool.wait_ge(wld[i], 8 * (e - i) + 16)
                    pool.wait_ge(s["h_mm"], 4 * e - 4)
                    split_weights(e, i, 0)
                    pool.wait_ge(s["down"], 4 * e - 4)
                    split_weights(e, i, 1)

        @block.scalar
        def _(act):
            A = nc.scalar.activation
            def head_matrices(layer):
                scale = 1 / math.sqrt(D) if layer == 0 else 1 / math.sqrt(DH1)
                for h in range(0, H, 2):
                    act.wait_ge(s["mn_mm"], H * layer + h + 2)
                    for g in (h, h + 1):
                        m = pair_bank(layer, g)
                        A(MN[:, 512 * g:512 * g + 128], m[:, 0:128], ACT.Copy, scale=scale)
                        A(MN[:, 512 * g + 256:512 * g + 384], m[:, 128:256], ACT.Copy).then_inc(s["mn_hi"], 1)

            act.wait_ge(ld["tok"], 16)
            A(TOKF, TOKI, ACT.Relu).then_inc(s["tokens"], 1)
            act.wait_ge(ld["rows"], 64)
            act.wait_ge(ld["const"], 16)
            A(VH[0:64], CS[0:64, C_VN:C_VN + 40], ACT.Gelu, bias=CP[0:64, K_VB1:K_VB1 + 1],
              scale=CP[0:64, K_VW1:K_VW1 + 1]).then_inc(s["vel_gelu"], 1)

            def onehot(k):
                if k > 4:
                    act.wait_ge(s["onehot_late"], k - 4)
                A(DIST, TOKF, ACT.Square, bias=CS[:, C_IDX + k:C_IDX + k + 1], scale=-1.0).then_inc(s["onehot_sq"], 1)
                act.wait_ge(s["onehot_sq"], k - 3)
                A(OH[k], DIST, ACT.Relu, bias=ONE, scale=-1.0).then_inc(s["onehot_late"], 1)
            act.wait_ge(s["tokens"], 1)
            onehot(4)
            act.wait_ge(s["tab_phase"], 1)
            tab = TAB.rearrange("p (k d) -> p k d", k=VC)
            A(tab[:, 1:5, 64:128], PH[:, 0:256].rearrange("p (k d) -> p k d", k=4), ACT.Sin).then_inc(s["tab_sin"], 1)
            A(tab[:, 5, :], PH[:, 256:384], ACT.Sin).then_inc(s["tab_sin"], 1)
            act.wait_ge(s["vel_sq"], 1)
            act.wait_ge(s["eps_ready"], 1)
            A(VS[0:40], VV[0:40], ACT.Sqrt, bias=EPS[0:40]).then_inc(s["vel_std"], 1)
            head_matrices(0)
            onehot(5)
            for c in range(NC):
                act.wait_ge(s["emb_mm"], c + 1)
                A(bchunk(HT, c), bank(c), ACT.Copy).then_inc(s["emb_out"], 1)

            def square(n, c):
                act.wait_ge(s["ln_xc"], NC * n + c + 1)
                A(SQ[c], bchunk(XN, c), ACT.Square).then_inc(s["ln_sq"], 1)

            def norm(n, split=None):

                def root(c):
                    act.wait_ge(s["ln_var"], NC * n + c + 1)
                    A(RSTD[:, 4 * c:4 * c + 4], bank(4 + c)[:, 0:4], ACT.Sqrt, bias=EPS)\
                        .then_inc(s["ln_std"], 1)
                for c in range(NC):
                    if c >= early(n):
                        square(n, c)
                    if c >= 1:
                        root(c - 1)
                root(NC - 1)
                if split is not None:
                    for c in range(NC):
                        act.wait_ge(s["ln_out"], NC * n + c + 1)
                        A(bchunk(XHI, c), bchunk(XN, c), ACT.Copy).then_inc(s["x_hi"], 1)

            def tokens_out(layer):
                for c in range(NC):
                    act.wait_ge(s["xt_mm"], NC * layer + c + 1)
                    A(XTM[:, 1024 * c:1024 * c + 512], bank(4 + c), ACT.Copy).then_inc(s["xt_hi"], 1)

            def attention(layer):
                w = [seen(layer, c) for c in ORDER[layer]]
                lo = [first_query(layer, j) for j in ORDER[layer]]

                def query(n, i):
                    act.wait_ge(s["q_mm"], n)
                    A(QHI[i], bank(0), ACT.Copy).then_inc(s["q_hi"], 1)
                query((H * B + 1) * layer + 1, 0)
                tokens_out(layer)

                def step(b, h, first, second):
                    i, v = h % 2, H * b + h
                    one, two = H * B * layer + v, (H * B + 1) * layer + v

                    def part(j):
                        act.wait_ge(s["pt_mm"], 4 * two + j + 1)
                        if j >= 2:
                            act.wait_ge(s["av"], 4 * two + j - 1)
                        A(PTHI[j % 2][:, lo[j]:512], bank(3 + j % 2)[:, lo[j]:512], ACT.Copy).then_inc(s["pt_hi"], 1)

                    def exps(c):
                        act.wait_ge(s["nmax"], 4 * one + c + 1)
                        A(PB[i][:, c, 0:w[c]], bank(SBANK[c])[:, 0:w[c]], ACT.Exp, bias=NMAX[:, 4 * i + c:4 * i + c + 1],
                          accum_out=DEN[:, 4 * i + c:4 * i + c + 1]).then_inc(s["exp"], 1)
                    if second:
                        part(0)
                        part(1)
                    if first:
                        exps(0)
                        exps(1)
                    if second:
                        part(2)
                    if first:
                        exps(2)
                    if second:
                        part(3)
                    if first:
                        query(two + 2, 1 - i)
                    if first:
                        exps(3)
                    if second:
                        act.wait_ge(s["av"], 4 * two + 4)
                        A(OHI[1 - i], bank(6), ACT.Copy).then_inc(s["o_hi"], 1)
                    if first and h == 0:
                        A(XTB[:, 0:512], XTM.bitcast(F32)[:, bass.ds(1024 * b, 512)], ACT.Copy).then_inc(s["xtb_hi"], 1)

                A(SM[:, 146:147], EPS, ACT.Exp)
                with act.Fori(0, B) as b:
                    for h in range(H):
                        step(b, h, True, True)
                step(B, 0, False, True)
                step(B, 1, False, False)
                for c in range(early(AFTER[layer])):
                    square(AFTER[layer], c)

            norm(0, 0)
            attention(0)
            norm(1, 1)
            head_matrices(1)
            act.wait_ge(ld["ffn"], 64)
            A(G1HI, GF1, ACT.Copy).then_inc(s["gate_w"], 1)
            for b in range(B):
                act.wait_ge(s["gate_mm"], b + 1)
                A(fa(512 * b, 512), bank(4 + b), ACT.Relu, bias=CP[:, K_GB1:K_GB1 + 1], accum_out=GS[:, b:b + 1])\
                    .then_inc(s["gate_sum"], 1)

            def diagonals(b):
                act.wait_ge(s["gates"], b + 1)
                for e in range(E0):
                    ins = A(DG[b % 2][:, 128 * e:128 * (e + 1)], ident, ACT.Identity, scale=G[:, b, e:e + 1])
                ins.then_inc(s["diag"], 1)
            diagonals(0)
            for b in range(B):
                act.wait_ge(s["mod_pe"], b + 1)
                if b >= 2:
                    act.wait_ge(s["y0_mm"], 4 * (b - 1))
                A(WSP[b % 2][:, 0:PW], bank(4 + b % 2)[:, 0:PW], ACT.Copy)
                act.wait_ge(s["mod"], b + 1)
                A(WSP[b % 2][:, PW:1024], WM[b % 2][:, PW:1024], ACT.Copy).then_inc(s["w_hi"], 1)
                if b == 0:
                    diagonals(1)
                for j in range(4):
                    m = 4 * b + j
                    act.wait_ge(s["h1_mm"], m + 1)
                    if m >= 4:
                        act.wait_ge(s["h1_lo"], m - 3)
                        act.wait_ge(s["y0_mm"], m - 3)
                    b1 = WM[b % 2][:, 1024 + j:1025 + j]
                    A(H1F[j], bank(UP[j]), ACT.Relu, bias=b1)
                    A(H1HI[j], bank(UP[j]), ACT.Relu, bias=b1).then_inc(s["h1_act"], 1)
                if b + 2 < B:
                    diagonals(b + 2)
            norm(2)
            norm(3, 2)
            attention(1)
            norm(4, 3)
            for c in range(16):
                if c % 4 == 0:
                    act.wait_ge(s["router"], c // 4 + 1)
                ins = A(PR[:, c, :], LG[:, c, :], ACT.Exp, accum_out=RS16[:, c:c + 1])
                if c % 4 == 3:
                    ins.then_inc(s["dist"], 1)
            for k in range(4):
                act.wait_ge(s["h_mm"], k + 1)
                A(HG[k % 4], bank(4 + 2 * (k % 2), 2), ACT.Gelu, bias=WRAW[0][:, 512 + k // 2:513 + k // 2])\
                    .then_inc(s["gelu"], 1)
            act.wait_ge(s["dist"], NC)
            for c in range(16):
                if c % 4 == 0:
                    act.wait_ge(s["inv_sum"], c // 4 + 1)
                ins = A(CW[:, c, :], PR[:, c, :], ACT.Exp, bias=NRP16[:, c:c + 1], scale=RP16[:, c:c + 1])
                if c % 4 == 3:
                    ins.then_inc(s["shares"], 1)

            def hi_part(m, k):
                act.wait_ge(s["scaled"], m + 1)
                if not isinstance(m, int) or m >= 2:
                    act.wait_ge(s["down"], m - 1)
                A(HHI[k % 2], HG[k % 4], ACT.Copy).then_inc(s["hh"], 1)
            for c in range(NC):
                act.wait_ge(s["comb_t"], c + 1)
                A(CT[:, 512 * c:512 * (c + 1)], bank(c)[0:E], ACT.Copy).then_inc(s["comb_s"], 1)
            for c in range(NC):
                act.wait_ge(s["comb_bc"], c + 1)
                A(bchunk(CB[0], c), bank(4 + c), ACT.Copy).then_inc(s["comb_b"], 1)
            for k in range(3):
                hi_part(k, k)

            def expert(e, i):
                for k in range(4):
                    m = 4 * e + k
                    act.wait_ge(s["h_mm"], m + 1)
                    act.wait_ge(s["hl"], m - 3)
                    g = A(HG[k % 4], bank(4 + 2 * (k % 2), 2), ACT.Gelu, bias=WRAW[i][:, 512 + k // 2:513 + k // 2])
                    g.then_inc(s["gelu"], 1)
                    hi_part(m - 1, k + 3)
            expert(1, 1)
            with act.Fori(1, E // 2) as pair:
                expert(2 * pair, 0)
                expert(2 * pair + 1, 1)
            hi_part(4 * E - 1, 3)

        @block.vector
        def _(dve):
            V = nc.vector
            seq = [0]

            def link(ins):
                seq[0] += 1
                ins.then_inc(dve_seq, 1)
                dve.wait_ge(dve_seq, seq[0])

            def head_matrices(layer):
                scale = 1 / math.sqrt(D) if layer == 0 else 1 / math.sqrt(DH1)
                for h in range(0, H, 2):
                    dve.wait_ge(s["mn_hi"], H * layer + h + 2)
                    for g in (h, h + 1):
                        m = pair_bank(layer, g)
                        V.scalar_tensor_tensor(MN[:, 512 * g + 128:512 * g + 256], m[:, 0:128], scale,
                                               MN[:, 512 * g:512 * g + 128].bitcast(F32), ALU.mult, ALU.subtract)
                        V.tensor_tensor(MN[:, 512 * g + 384:512 * g + 512], m[:, 128:256],
                                        MN[:, 512 * g + 256:512 * g + 384].bitcast(F32), ALU.subtract)\
                            .then_inc(s["mn_lo"], 1)

            V.memset(EPS, LN_EPS).then_inc(s["eps_ready"], 1)
            dve.wait_ge(ld["const"], 16)
            V.tensor_copy(IDB[:, :], ident)
            V.tensor_copy(MKB[:, :], mask).then_inc(s["bf_ready"], 1)

            def onehot(k):
                if k >= 2:
                    dve.wait_ge(s["onehot_used"], k - 1)
                V.tensor_scalar(OH[k], TOKF, CS[:, C_IDX + k:C_IDX + k + 1], None, ALU.is_equal)\
                    .then_inc(s["onehot"], 1)
            dve.wait_ge(s["tokens"], 1)
            onehot(0)
            onehot(1)
            dve.wait_ge(ld["rows"], 64)
            tab = TAB.rearrange("p (k d) -> p k d", k=VC)
            pos = CS[:, C_POS:C_POS + 1]
            for kind in range(2):
                for j in range(2):
                    o = 64 * kind
                    V.scalar_tensor_tensor(tab[:, 1 + 2 * kind + j, 0:64], RW_[:, R_LW + o:R_LW + o + 64], TN[:, j:j + 1],
                                           RW_[:, R_LB + o:R_LB + o + 64], ALU.mult, ALU.add)
                    V.scalar_tensor_tensor(PH[:, 128 * kind + 64 * j:128 * kind + 64 * j + 64],
                                           RW_[:, R_W + o:R_W + o + 64], TN[:, j:j + 1],
                                           RW_[:, R_B + o:R_B + o + 64], ALU.mult, ALU.add)
            p0 = pos[:, 0:1]
            link(V.tensor_scalar(O1, p0, 12.0, None, ALU.is_ge))
            link(V.scalar_tensor_tensor(O2, p0, 24.0, O1, ALU.is_ge, ALU.add))
            link(V.scalar_tensor_tensor(SEM_, O2, -12.0, p0, ALU.mult, ALU.add))
            link(V.tensor_scalar(SEMC, SEM_, math.pi / 6.0, None, ALU.mult))
            pn = PH[:, 256:384].rearrange("p (i a b) -> p i a b", a=2, b=2)
            kn = KQ[:, 256:384].rearrange("p (i a b) -> p i a b", a=2, b=2)
            for b_ in range(2):
                V.tensor_scalar(pn[:, :, 0, b_], CS[:, C_POW:C_POW + 32], O2, None, ALU.mult)
                last = V.tensor_scalar(pn[:, :, 1, b_], CS[:, C_INC:C_INC + 32], SEMC, None, ALU.mult)
            link(last)
            link(V.tensor_scalar(KQ, PH, 1 / (2 * math.pi), None, ALU.mult))
            link(V.tensor_scalar(kn[:, :, :, 1], kn[:, :, :, 1], 0.25, None, ALU.add))
            link(V.tensor_scalar(KQ, KQ, 1.5 * 2 ** 23, None, ALU.add))
            link(V.tensor_scalar(KQ, KQ, 1.5 * 2 ** 23, None, ALU.subtract))
            link(V.scalar_tensor_tensor(PH, KQ, -6.28125, PH, ALU.mult, ALU.add))
            link(V.scalar_tensor_tensor(PH, KQ, -(2 * math.pi - 6.28125), PH, ALU.mult, ALU.add))
            link(V.tensor_scalar(pn[:, :, :, 1], pn[:, :, :, 1], math.pi / 2, None, ALU.add))
            V.tensor_scalar(PH, PH, -3.1415925, 3.1415925, ALU.max, ALU.min).then_inc(s["tab_phase"], 1)
            dve.wait_ge(s["vel_e"], 1)
            ve = VE[0:40]
            link(V.tensor_tensor(ve, bank(0)[0:40, 0:128], RW_[0:40, R_B2:R_B2 + 128], ALU.add))
            link(V.reduce_sum(VM[0:40], ve, AX.X))
            link(V.tensor_scalar(VM[0:40], VM[0:40], 1.0 / D, None, ALU.mult))
            link(V.tensor_scalar(ve, ve, VM[0:40], None, ALU.subtract))
            link(V.tensor_tensor(VSQ[0:40], ve, ve, ALU.mult))
            link(V.reduce_sum(VR[0:40], VSQ[0:40], AX.X))
            V.tensor_scalar(VV[0:40], VR[0:40], 1.0 / D, None, ALU.mult).then_inc(s["vel_sq"], 1)
            dve.wait_ge(s["vel_std"], 1)
            link(V.reciprocal(VS[0:40], VS[0:40]))
            link(V.tensor_scalar(ve, ve, VS[0:40], None, ALU.mult))
            link(V.tensor_tensor(ve, ve, RW_[0:40, R_G:R_G + 128], ALU.mult))
            dve.wait_ge(s["tab_sin"], 2)
            link(V.tensor_tensor(tab[32:40, 5, :], ve[32:40], RW_[32:40, R_BETA:R_BETA + 128], ALU.add))
            link(V.tensor_copy(THI, TAB))
            V.tensor_tensor(TLO, TAB, THI.bitcast(F32), ALU.subtract).then_inc(s["emb_tab"], 1)
            onehot(2)
            onehot(3)
            head_matrices(0)

            def center(n, src, c):
                dve.wait_ge(s["ln_mean"], NC * n + c + 1)
                V.tensor_tensor(bchunk(XN, c), bchunk(src, c), bank(c), ALU.subtract).then_inc(s["ln_xc"], 1)

            def norm(n, src, gain=None):

                def invert(c):
                    dve.wait_ge(s["ln_std"], NC * n + c + 1)
                    V.reciprocal(RSTD[:, 4 * c:4 * c + 4], RSTD[:, 4 * c:4 * c + 4]).then_inc(s["ln_rstd"], 1)

                def scale(c):
                    dve.wait_ge(s["ln_bc"], NC * n + c + 1)
                    if gain is None:
                        ins = V.tensor_tensor(bchunk(XN, c), bchunk(XN, c), bank(c), ALU.mult)
                    else:
                        ins = V.scalar_tensor_tensor(bchunk(XN, c), bchunk(XN, c), gain, bank(c), ALU.mult, ALU.mult)
                    ins.then_inc(s["ln_out"], 1)
                for c in range(early(n), NC):
                    center(n, src, c)
                invert(0)
                for c in range(NC):
                    if c + 1 < NC:
                        invert(c + 1)
                    scale(c)

            def tokens_out(layer):
                for c in range(NC):
                    dve.wait_ge(s["xt_hi"], NC * layer + c + 1)
                    V.tensor_tensor(XTM[:, 1024 * c + 512:1024 * (c + 1)], bank(4 + c),
                                    XTM[:, 1024 * c:1024 * c + 512].bitcast(F32), ALU.subtract).then_inc(s["xt_lo"], 1)

            def attention(layer):
                w = [seen(layer, c) for c in ORDER[layer]]
                lo = [first_query(layer, j) for j in ORDER[layer]]

                def query(n, i):
                    dve.wait_ge(s["q_hi"], n)
                    V.tensor_tensor(QLO[i], bank(0), QHI[i].bitcast(F32), ALU.subtract).then_inc(s["q_lo"], 1)
                query((H * B + 1) * layer + 1, 0)
                tokens_out(layer)
                dve.wait_ge(s["zero_banks"], layer + 1)

                def step(b, h, first, second):
                    i, v = h % 2, H * b + h
                    one, two = H * B * layer + v, (H * B + 1) * layer + v

                    def part(j):
                        dve.wait_ge(s["pt_hi"], 4 * two + j + 1)
                        V.tensor_tensor(PTLO[j % 2][:, lo[j]:512], bank(3 + j % 2)[:, lo[j]:512],
                                        PTHI[j % 2][:, lo[j]:512].bitcast(F32), ALU.subtract).then_inc(s["pt_lo"], 1)

                    def top(c):
                        dve.wait_ge(s["s_mm"], 4 * one + c + 1)
                        V.tensor_reduce(NMAX[:, 4 * i + c:4 * i + c + 1], bank(SBANK[c])[:, 0:w[c]], AX.X, ALU.max,
                                        negate=True).then_inc(s["nmax"], 1)

                    def over(c):
                        col = slice(4 * i + c, 4 * i + c + 1)
                        dve.wait_ge(s["exp"], 4 * one + c + 5)
                        V.reciprocal(RDEN[:, col], DEN[:, col]).then_inc(s["rden"], 1)
                    dve.wait_ge(s["o_hi"], (H * B + 2) * layer + v + 1)
                    V.tensor_tensor(OLO[i], bank(6), OHI[i].bitcast(F32), ALU.subtract).then_inc(s["o_lo"], 1)
                    if first:
                        top(0)
                    if second and layer == 0:
                        part(0)
                    if first:
                        top(1)
                    if second:
                        if layer == 1:
                            part(0)
                        part(1)
                    if isinstance(b, int) and h == 1:
                        for c in range(early(AFTER[layer])):
                            center(AFTER[layer], HT, c)
                    if h == 1:
                        at = bass.ds(512 * ((b + B - 1) % B), 512) if not isinstance(b, int) else slice(1536, 2048)
                        dve.wait_ge(s["y_mm"], (B + 1) * layer + b + 1)
                        if layer == 1:
                            dve.wait_ge(s["offset"], 2 * NC)
                        V.tensor_tensor(HT[:, at], bank(7), HT[:, at], ALU.add).then_inc(s["y_add"], 1)
                    if first:
                        over(0)
                        top(2)
                        over(1)
                    if second:
                        part(2)
                    if first:
                        over(2)
                    if second:
                        part(3)
                    if first:
                        top(3)
                        query(two + 2, 1 - i)
                        over(3)
                        dve.wait_ge(s["rden"], 4 * one + 4)
                        V.tensor_scalar(PB[i][:, 3, 0:w[3]], PB[i][:, 3, 0:w[3]], RDEN[:, 4 * i + 3:4 * i + 4], None,
                                        ALU.mult).then_inc(s["p_done"], 1)
                    if first and h == 0:
                        dve.wait_ge(s["av"], 4 * two + 4)
                        V.tensor_copy(XTB[:, 512:1024], XTM.bitcast(F32)[:, bass.ds(1024 * b + 512, 512)])\
                            .then_inc(s["xtb_lo"], 1)

                with dve.Fori(0, B) as b:
                    for h in range(H):
                        step(b, h, True, True)
                step(B, 0, False, True)
                step(B, 1, False, False)

            norm(0, HT)
            attention(0)
            norm(1, HT)
            head_matrices(1)
            for k, (col, base, o) in enumerate(((K_TVG, K_LNG, LNG), (K_TVB, K_LNB, LNB))):
                T8 = T16[:, 8 * k:8 * k + 8]
                link(V.tensor_scalar(T8, CP[:, col:col + E0], CP[:, base:base + 1], None, ALU.subtract))
                link(V.reduce_sum(TVS[:, k:k + 1], T8, AX.X))
                V.scalar_tensor_tensor(o, TVS[:, k:k + 1], 0.03, CP[:, base:base + 1], ALU.mult, ALU.add)\
                    .then_inc(s["ln_gain"], 1)
            dve.wait_ge(s["gate_w"], 1)
            V.tensor_tensor(G1LO, GF1, G1HI.bitcast(F32), ALU.subtract).then_inc(s["gate_w"], 1)

            def gates(b):
                dve.wait_ge(s["gate_sum"], b + 1)
                if b:
                    dve.wait_ge(s["gate_g"], b)
                V.tensor_scalar(GMB, GS[:, b:b + 1].to_broadcast([128, 128]), 1.0 / S, None, ALU.mult)\
                    .then_inc(s["gate_bc"], 1)
                dve.wait_ge(s["gate_g"], b + 1)
                V.tensor_tensor(G[:, b, :], bank(0)[:, 8 * b:8 * b + 8], GF2B, ALU.add).then_inc(s["gates"], 1)
            def modulate(b):
                if b >= 2:
                    dve.wait_ge(s["res0"], b - 1)
                    dve.wait_ge(s["h1_act"], 4 * (b - 1))
                dve.wait_ge(s["gates"], b + 1)
                w = WM[b % 2][:, PW:P0]
                for e in range(E0):
                    ins = V.scalar_tensor_tensor(w, TV[:, 1 + e, PW:P0], G[:, b, e:e + 1],
                                                 TV[:, 0, PW:P0] if e == 0 else w, ALU.mult, ALU.add)
                    if e < E0 - 1:
                        link(ins)
                ins.then_inc(s["mod"], 1)

            def finish(b):
                dve.wait_ge(s["y0_mm"], 4 * (b + 1))
                V.scalar_tensor_tensor(bchunk(XN, b), bank(2 + b % 2), WM[b % 2][:, 1028:1029], bchunk(XN, b),
                                       ALU.add, ALU.add).then_inc(s["res0"], 1)
            gates(0)
            for b in range(B):
                modulate(b)
                if b == 0:
                    for c in range(1, B):
                        gates(c)
                dve.wait_ge(s["w_hi"], b + 1)
                V.tensor_tensor(WSP[b % 2][:, 1024:1024 + PW], bank(4 + b % 2)[:, 0:PW], WSP[b % 2][:, 0:PW].bitcast(F32),
                                ALU.subtract)
                V.tensor_tensor(WSP[b % 2][:, 1024 + PW:2048], WM[b % 2][:, PW:1024],
                                WSP[b % 2][:, PW:1024].bitcast(F32), ALU.subtract).then_inc(s["w_lo"], 1)
                if b >= 1:
                    finish(b - 1)
            finish(B - 1)
            norm(2, XN, LNG)
            for c in range(NC):
                dve.wait_ge(s["ln_out"], NC * 2 + c + 1)
                dve.wait_ge(s["offset"], c + 1)
                ins = V.tensor_tensor(bchunk(HT, c), bchunk(HT, c), bchunk(XN, c), ALU.add)
                ins.then_inc(s["ffn_out"], 1)
            norm(3, HT)
            attention(1)
            norm(4, HT)
            V.memset(LW[:, :, E:E + PADS], 1e30)
            dve.wait_ge(ld["moe"], 48)

            def quarter(x, q):
                return x[:, 4 * q:4 * q + 4]

            def over(x):
                return x.unsqueeze(2).to_broadcast([128, 4, E])

            def prepare(q):
                x = bank(4 + q)[:, 0:4 * E].rearrange("p (c e) -> p c e", c=4)
                dve.wait_ge(s["logit_mm"], q + 1)
                lg = quarter(LG, q)
                link(V.tensor_tensor(lg, x, RBT.unsqueeze(1).to_broadcast([128, 4, E]), ALU.add))
                link(V.tensor_reduce(quarter(MX16, q), lg, AX.X, ALU.max))
                V.tensor_tensor(lg, lg, over(quarter(MX16, q)), ALU.subtract).then_inc(s["router"], 1)
                dve.wait_ge(s["router"], q + 1)
                link(V.tensor_scalar(quarter(LW, q)[:, :, 0:E], quarter(LG, q), -1.0, 87.33654, ALU.mult, ALU.min))

            def invert_sum(q):
                dve.wait_ge(s["dist"], q + 1)
                link(V.reciprocal(quarter(RP16, q), quarter(RS16, q)))
                V.tensor_scalar(quarter(NRP16, q), quarter(RP16, q), -1.0, None, ALU.mult).then_inc(s["inv_sum"], 1)
            free = [0]

            def drop(q):
                for r in range((DROP + PADS) // 8):
                    for j in range(4):
                        x = LW[:, 4 * q + j, :]
                        if q or r:
                            dve.wait_ge(dve_seq, free[0] + j)
                        V.max(V8[j], x).then_inc(dve_seq, 1)
                    for j in range(4):
                        x = LW[:, 4 * q + j, :]
                        dve.wait_ge(dve_seq, seq[0] + 1 + j)
                        V.match_replace(x, V8[j], x, -1.0).then_inc(dve_seq, 1)
                    free[0] = seq[0] + 5
                    seq[0] += 8

            def share(q):
                cw, d = quarter(CW, q), quarter(D16, q)
                dve.wait_ge(dve_seq, seq[0])
                dve.wait_ge(s["shares"], q + 1)
                link(V.scalar_tensor_tensor(cw, quarter(LW, q)[:, :, 0:E], 0.0, cw, ALU.is_ge, ALU.mult))
                link(V.reduce_sum(d, cw, AX.X))
                link(V.reciprocal(d, d))
                V.tensor_tensor(cw, cw, over(d), ALU.mult).then_inc(s["comb"], 1)
            for q in range(NC):
                prepare(q)
            drop(0)
            for q in range(NC):
                invert_sum(q)
            drop(1)
            drop(2)
            share(0)
            share(1)
            drop(3)
            share(2)
            share(3)

            def lo_part(m, k):
                dve.wait_ge(s["hh"], m + 1)
                V.tensor_tensor(HLO[k % 2], HG[k % 4], HHI[k % 2].bitcast(F32), ALU.subtract).then_inc(s["hl"], 1)

            def weigh(m, k, i):
                dve.wait_ge(s["gelu"], m + 1)
                V.tensor_tensor(HG[k % 4], HG[k % 4], CB[i][:, 1024 * (k % 2):1024 * (k % 2) + 1024], ALU.mult)\
                    .then_inc(s["scaled"], 1)

            def expert(e, i, first=False):
                for k in range(4):
                    m = 4 * e + k
                    if first and k == 0:
                        dve.wait_ge(s["comb_b"], NC)
                    elif k == 0:
                        dve.wait_ge(cbd[i], 8 * (e + i))
                    weigh(m, k, i)
                    if not (first and k == 0):
                        lo_part(m - 1, k + 3)
            expert(0, 0, True)
            expert(1, 1)
            with dve.Fori(1, E // 2) as pair:
                expert(2 * pair, 0)
                expert(2 * pair + 1, 1)
            lo_part(4 * E - 1, 3)
            for c in range(NC):
                dve.wait_ge(s["down"], 4 * E - 1 + c // 2)
                V.tensor_tensor(bchunk(HT, c), bchunk(HT, c), bank(c), ALU.add).then_inc(s["final"], 1)

        @block.tensor
        def _(pe):
            def head_matrices(layer):
                k = 128 if layer == 0 else DH1
                pe.wait_ge(ld["a0" if layer == 0 else "a1"], 16)
                if layer == 1:
                    pe.wait_ge(s["ln_out"], 2 * NC)
                for h in range(H):
                    hs = slice(128 * h, 128 * (h + 1))
                    m = pair_bank(layer, h)
                    pe.matmul(m[:, 0:128], WL[0:k, 0, hs], WL[0:k, 1, hs], start=True, stop=True)
                    pe.matmul(m[:, 128:256], WL[0:k, 2, hs], WL[0:k, 3, hs], start=True, stop=True)\
                        .then_inc(s["mn_mm"], 1)

            pe.wait_ge(ld["rows"], 64)
            pe.wait_ge(s["vel_gelu"], 1)
            pe.matmul(bank(0)[0:40, 0:128], VH[0:64], V2T[:, :], start=True, stop=True).then_inc(s["vel_e"], 1)
            head_matrices(0)
            pe.wait_ge(s["emb_tab"], 1)
            for k in range(VC):
                if k < 4:
                    pe.wait_ge(s["onehot"], k + 1)
                else:
                    pe.wait_ge(s["onehot_late"], k - 3)
                for c in range(NC):
                    o = bank(c)
                    pe.matmul(o, THI[:, 128 * k:128 * (k + 1)], bchunk(OH[k], c), start=(k == 0), stop=False)
                    ins = pe.matmul(o, TLO[:, 128 * k:128 * (k + 1)], bchunk(OH[k], c), start=False,
                                    stop=(k == VC - 1))
                    if k == VC - 1:
                        ins.then_inc(s["emb_mm"], 1)
                if k < VC - 1:
                    ins.then_inc(s["onehot_used"], 1)

            def mean(src, c):
                pe.matmul(bank(c), mean_w, bchunk(src, c), start=True, stop=True).then_inc(s["ln_mean"], 1)

            def norm(n, src, ready, after=None):
                def var(c):
                    pe.wait_ge(s["ln_sq"], NC * n + c + 1)
                    for j in range(4):
                        ins = pe.matmul(bank(4 + c)[:, j:j + 1], SQ[c][:, 128 * j:128 * (j + 1)], mean_w[:, 0:1],
                                        start=True, stop=True)
                    ins.then_inc(s["ln_var"], 1)

                def spread(c):
                    pe.wait_ge(s["ln_rstd"], NC * n + c + 1)
                    for j in range(4):
                        ins = pe.transpose(bank(c)[:, 128 * j:128 * (j + 1)],
                                           RSTD[:, 4 * c + j:4 * c + j + 1].to_broadcast([128, 128]), ident)
                    ins.then_inc(s["ln_bc"], 1)
                if n == 0:
                    pe.wait_ge(s["mn_lo"], H)
                for c in range(early(n), NC):
                    ready(c)
                    mean(src, c)
                for c in range(NC):
                    var(c)
                    if c >= 1:
                        spread(c - 1)
                if after:
                    after(0)
                spread(NC - 1)
                if after:
                    for c in range(1, NC):
                        after(c)

            def tokens_out(layer):
                n = 0 if layer == 0 else 3
                for c in range(NC):
                    pe.wait_ge(s["ln_out"], NC * n + c + 1)
                    for j in range(4):
                        ins = pe.transpose(bank(4 + c)[:, 128 * j:128 * (j + 1)],
                                           XN[:, 512 * c + 128 * j:512 * c + 128 * (j + 1)], ident)
                    ins.then_inc(s["xt_mm"], 1)

            def attention(layer):
                if layer == 0:
                    pe.wait_ge(s["bf_ready"], 1)
                x_lo = NC * (0 if layer == 0 else 2)
                pe.wait_ge(s["x_lo"], x_lo + 1)
                pe.wait_ge(s["mn_lo"], H * (layer + 1))

                def query(b, h):
                    m = MN[:, 512 * h:512 * h + 256]
                    at = bass.ds(512 * b, 512)
                    three(pe, bank(0), m[:, 0:128], m[:, 128:256], XHI[:, at], XLO[:, at], True, True)\
                        .then_inc(s["q_mm"], 1)
                query(0, 0)
                pe.wait_ge(s["xt_lo"], NC * (layer + 1))
                pe.wait_ge(s["p_done"], (H * B + 1) * layer + 1)
                pe.matmul(bank(7), XTB[:, 0:128], XTB[:, 0:512], start=True, stop=False, skip_group_check=True)
                pe.matmul(bank(6), XTB[:, 0:128], XTB[:, 0:512], start=True, stop=True).then_inc(s["zero_banks"], 1)

                def step(b, h, first, second):
                    i, v = h % 2, H * b + h
                    one, two = H * B * layer + v, (H * B + 1) * layer + v

                    def turn(k):
                        j = ORDER[layer][k]
                        if layer == 0:
                            pe.wait_ge(s["p_pool"], 3 * (one + layer) + min(k + 1, 3))
                        elif k == 0:
                            pe.wait_ge(s["p_pool"], 3 * (one + layer + 1))
                        if k == (3 if layer == 0 else 0):
                            pe.wait_ge(s["p_done"], one + layer + 1)
                        if k >= 2:
                            pe.wait_ge(s["pt_lo"], 4 * two + k - 1)
                        for c in range(j if layer == 0 else 0, 4):
                            ins = pe.transpose(bank(3 + k % 2)[:, 128 * c:128 * (c + 1)],
                                               PB[1 - i][:, ORDER[layer].index(c), 128 * j:128 * (j + 1)], ident)
                        ins.then_inc(s["pt_mm"], 1)

                    def scores(k, hi=True, lo=True):
                        c = ORDER[layer][k]
                        w = seen(layer, c)
                        if k == 0:
                            pe.wait_ge(s["q_lo"], two + 1)
                        elif hi:
                            pe.wait_ge(s["exp"], 4 * one + k + 1)
                        if k == 1 and hi:
                            pe.wait_ge(s["q_hi"], two + 1)
                        qs = slice(128 * c, 128 * (c + 1))
                        o = bank(SBANK[k])[:, 0:w]
                        xh = XHI[:, bass.ds(512 * b, w)]
                        xl = XLO[:, bass.ds(512 * b, w)]
                        if hi:
                            pe.matmul(o, QHI[i][:, qs], xh, start=True, stop=False)
                            if layer == 0:
                                pe.matmul(o[:, 128 * c:128 * (c + 1)], IDB[:, :], MKB[:, :], start=False, stop=False,
                                          skip_group_check=True)
                            pe.matmul(o, QHI[i][:, qs], xl, start=False, stop=False)
                        if lo:
                            pe.matmul(o, QLO[i][:, qs], xh, start=False, stop=True).then_inc(s["s_mm"], 1)

                    def mix(k):
                        j = ORDER[layer][k]
                        at = first_query(layer, j)
                        if k == 0 and h == 1 and not isinstance(b, int):
                            pe.wait_ge(s["xtb_hi"], B * layer + b + 1)
                            pe.wait_ge(s["xtb_lo"], B * layer + b + 1)
                        if k == 0:
                            pe.wait_ge(s["o_lo"], (H * B + 2) * layer + v + 1)
                        pe.wait_ge(s["pt_lo"], 4 * two + k + 1)
                        three(pe, bank(6)[:, at:512], XTB[:, 128 * j:128 * (j + 1)],
                              XTB[:, 512 + 128 * j:512 + 128 * (j + 1)], PTHI[k % 2][:, at:512],
                              PTLO[k % 2][:, at:512], k == 0, k == 3, skip_group_check=True)\
                            .then_inc(s["av"], 1)

                    def project():
                        g = (h - 2) % H
                        pe.wait_ge(s["o_lo"], (H * B + 2) * layer + v + 1)
                        if g == 0:
                            pe.wait_ge(s["y_add"], (B + 1) * layer + b + 1)
                        n = MN[:, 512 * g + 256:512 * g + 512]
                        ins = three(pe, bank(7), n[:, 0:128], n[:, 128:256], OHI[i], OLO[i], g == 0, g == H - 1,
                                    skip_group_check=True)
                        if g == H - 1:
                            ins.then_inc(s["y_mm"], 1)
                    if first:
                        scores(1, lo=False)
                        scores(0)
                        scores(1, hi=False)
                    if second:
                        turn(0)
                        turn(1)
                    project()
                    if first:
                        scores(2)
                    if second:
                        mix(0)
                        turn(2)
                        mix(1)
                        turn(3)
                    if first:
                        scores(3)
                        if h == H - 1:
                            pe.wait_ge(s["x_lo"], x_lo + NC)
                        pe.wait_ge(s["exp"], 4 * one + 5)
                        query((b + 1) % B if h == H - 1 else b, (h + 1) % H)
                    if second:
                        mix(2)
                        mix(3)

                with pe.Fori(0, B) as b:
                    for h in range(H):
                        step(b, h, True, True)
                step(B, 0, False, True)
                pe.wait_ge(s["q_lo"], (H * B + 1) * (layer + 1))
                pe.wait_ge(s["exp"], 4 * (H * B * (layer + 1) + 1))
                pe.wait_ge(s["y_add"], (B + 1) * layer + B)
                for c in range(early(AFTER[layer])):
                    mean(HT, c)
                step(B, 1, False, False)

            norm(0, HT, lambda c: pe.wait_ge(s["emb_out"], NC))
            tokens_out(0)
            attention(0)
            norm(1, HT, lambda c: pe.wait_ge(s["y_add"], B + 1))
            head_matrices(1)
            pe.wait_ge(s["gate_w"], 2)
            for b in range(B):
                pe.wait_ge(s["x_lo"], NC + b + 1)
                three(pe, bank(4 + b), G1HI, G1LO, bchunk(XHI, b), bchunk(XLO, b), True, True).then_inc(s["gate_mm"], 1)

            def gates(b):
                pe.wait_ge(s["gate_bc"], b + 1)
                pe.matmul(bank(0)[:, 8 * b:8 * b + 8], GMB, GF2, start=True, stop=True).then_inc(s["gate_g"], 1)
            gates(0)

            def up(m):
                b, j = m // 4, m % 4
                if j == 0:
                    pe.wait_ge(s["w_lo"], b + 1)
                if m >= 4:
                    pe.wait_ge(s["h1_act"], m - 3)
                w = WSP[b % 2]
                three(pe, bank(UP[j]), w[:, 128 * j:128 * (j + 1)], w[:, 1024 + 128 * j:1024 + 128 * (j + 1)],
                      bchunk(XHI, b), bchunk(XLO, b), True, True).then_inc(s["h1_mm"], 1)

            def down0(m):
                b, j = m // 4, m % 4
                if j == 0 and b >= 2:
                    pe.wait_ge(s["res0"], b - 1)
                pe.wait_ge(s["h1_lo"], m + 1)
                w = WSP[b % 2]
                three(pe, bank(2 + b % 2), w[:, 512 + 128 * j:512 + 128 * (j + 1)],
                      w[:, 1536 + 128 * j:1536 + 128 * (j + 1)], H1HI[j], H1LO[j], j == 0, j == 3)\
                    .then_inc(s["y0_mm"], 1)

            def modulate(b):
                o = bank(4 + b % 2)[:, 0:PW]
                if b < 2:
                    pe.wait_ge(s["gate_sum"], NC)
                else:
                    pe.wait_ge(s["w_lo"], b - 1)
                pe.matmul(o, ident, TV[:, 0, 0:PW], start=True, stop=False)
                pe.wait_ge(s["diag"], b + 1)
                for e in range(E0):
                    ins = pe.matmul(o, DG[b % 2][:, 128 * e:128 * (e + 1)], TV[:, 1 + e, 0:PW], start=False,
                                    stop=e == E0 - 1)
                ins.then_inc(s["mod_pe"], 1)
            modulate(0)
            for b in range(1, B):
                gates(b)
            for b in range(B):
                for m in range(4 * b, 4 * b + 4):
                    up(m)
                if b < B - 1:
                    modulate(b + 1)
                for m in range(4 * b, 4 * b + 4):
                    down0(m)
            pe.wait_ge(s["h1_act"], 4 * B)
            norm(2, XN, lambda c: pe.wait_ge(s["res0"], c + 1))
            norm(3, HT, lambda c: pe.wait_ge(s["ffn_out"], c + 1))
            tokens_out(1)
            attention(1)

            def logits(c):
                if c == 0:
                    pe.wait_ge(ld["moe"], 48)
                o = bank(4 + c)[:, 0:4 * E]
                pe.wait_ge(s["ln_out"], 4 * NC + c + 1)
                for j in range(4):
                    ins = pe.matmul(o[:, E * j:E * (j + 1)], XN[:, 512 * c + 128 * j:512 * c + 128 * (j + 1)], RWT,
                                    start=True, stop=True)
                ins.then_inc(s["logit_mm"], 1)
            norm(4, HT, lambda c: pe.wait_ge(s["y_add"], 2 * (B + 1)), logits)

            def rise(m, k, i):
                if not isinstance(m, int) or m >= 2:
                    pe.wait_ge(s["gelu"], m - 1)
                f = slice(128 * (k // 2), 128 * (k // 2 + 1))
                for j in range(2):
                    c = 2 * (k % 2) + j
                    ins = three(pe, bank(4 + 2 * (k % 2) + j), WHI[i][:, f], WLO[i][:, f], bchunk(XHI, c), bchunk(XLO, c),
                                True, True)
                ins.then_inc(s["h_mm"], 1)

            def fall(m, k, i, last=False):
                pe.wait_ge(s["hl"], m + 1)
                f = slice(256 + 128 * (k // 2), 256 + 128 * (k // 2 + 1))
                for j in range(2):
                    c = 2 * (k % 2) + j
                    h = slice(512 * j, 512 * (j + 1))
                    ins = three(pe, bank(c), WHI[i][:, f], WLO[i][:, f], HHI[k % 2][:, h], HLO[k % 2][:, h], False, last,
                                skip_group_check=True)
                ins.then_inc(s["down"], 1)

            def expert(e, i):
                pe.wait_ge(s["wsplit1"], e + 1)
                for k in range(4):
                    if k == LAG:
                        pe.wait_ge(s["wsplit2"], e + 1)
                    rise(4 * e + k, k, i)
                    fall(4 * e + k - LAG, (k - LAG) % 4, i if k >= LAG else 1 - i)
            pe.wait_ge(s["x_lo"], 4 * NC)
            pe.wait_ge(s["wsplit1"], 1)
            pe.wait_ge(s["router"], NC)
            for k in range(4):
                rise(k, k, 0)
            for c in range(NC):
                pe.wait_ge(s["comb"], c + 1)
                for j in range(4):
                    ins = pe.transpose(bank(c)[0:E, 128 * j:128 * (j + 1)], CW[:, 4 * c + j, :], ident)
                ins.then_inc(s["comb_t"], 1)
                pe.wait_ge(s["gelu"], 3 if c < 2 else 4)
                for j in range(4):
                    ins = pe.transpose(bank(4 + c)[:, 128 * j:128 * (j + 1)],
                                       CW[:, 4 * c + j, 0:1].to_broadcast([128, 128]), ident)
                ins.then_inc(s["comb_bc"], 1)
            for c in range(NC):
                pe.wait_ge(s["comb_s"], c + 1)
                pe.matmul(bank(c), EB2, CT[:, 512 * c:512 * (c + 1)], start=True, stop=False, skip_group_check=True)
            pe.wait_ge(s["wsplit2"], 1)
            fall(0, 0, 0)
            pe.wait_ge(s["comb_b"], NC)
            expert(1, 1)
            with pe.Fori(1, E // 2) as pair:
                expert(2 * pair, 0)
                expert(2 * pair + 1, 1)
            for m in range(4 * E - LAG, 4 * E):
                fall(m, m % 4, 1, last=m >= 4 * E - 2)


def kernel(**inputs):
    import numpy as np
    import concourse.bacc as bacc
    from concourse.bass_utils import run_bass_kernel_spmd

    x = {k: np.asarray(v) for k, v in inputs.items()}
    f = np.float32

    consts = np.zeros((128, C_ALL), f)
    p = np.arange(128)
    consts[:, C_ID:C_ID + 128] = np.eye(128)
    consts[:, C_ONES:C_ONES + 128] = 1.0 / D
    consts[:, C_MASK:C_MASK + 128] = np.where(p[None, :] <= p[:, None], 0.0, -1e30)
    for k, (first, n) in enumerate(((0, 128), (128, 125), (253, 125), (418, 125), (543, 125), (378, 40))):
        consts[:, C_IDX + k] = np.where(p < n, first + p, -1)
    consts[:, C_POS] = p
    consts[:, C_TN] = p / 250
    consts[:, C_TN + 1] = (125 + p) / 250
    consts[:, C_POW:C_POW + 32] = 0.5 ** np.arange(32)
    consts[:, C_INC:C_INC + 32] = np.arange(32) + 1
    consts[:, C_VN:C_VN + 40] = (np.arange(40) - 32) / 32

    t = "L0_tok_"
    rows = np.concatenate([x[t + k] for k in ("time_lin_w", "dur_lin_w", "time_lin_b", "dur_lin_b", "time_w", "dur_w",
                                              "time_b", "dur_b", "vel_b2", "vel_ln_g", "vel_ln_b")])
    cols = np.zeros((128, K_ALL), f)
    cols[0:64, K_VW1] = x[t + "vel_w1"]
    cols[0:64, K_VB1] = x[t + "vel_b1"]
    q = "L0_ffn_"
    cols[:, K_GB1] = x[q + "gfc1_b"]
    cols[:, K_LNG] = x[q + "ln_g"]
    cols[:, K_LNB] = x[q + "ln_b"]
    cols[:, K_TVG:K_TVG + E0] = x[q + "tv_ln_g"].T
    cols[:, K_TVB:K_TVB + E0] = x[q + "tv_ln_b"].T
    cols[:, K_BOUT] = x["L1_attn_b_out"]

    def by_head(w, n):
        return w.reshape(H, n, -1).transpose(1, 0, 2).reshape(n, -1)
    a = "L0_attn_"
    a0 = np.stack([by_head(w, 128) for w in (x[a + "Wq"], x[a + "Wk"], x[a + "Wv"], x[a + "Wu"].T)], 1)
    a = "L1_attn_"
    a1 = np.stack([by_head(w, DH1) for w in (x[a + "w_q"].T, x[a + "w_k"].T, x[a + "w_v"].T, x[a + "w_out"])], 1)

    def modulated(w1, w2, b1, b2):
        return np.concatenate([w1.T, w2.T.reshape(4, 128, D).transpose(1, 0, 2).reshape(128, -1),
                               b1.reshape(4, 128).T, b2[:, None]], 1)
    ffn = np.stack([modulated(x[q + "W1"], x[q + "W2"], x[q + "b1"], x[q + "b2"])]
                   + [modulated(x[q + "tv_W1"][e], x[q + "tv_W2"][e], x[q + "tv_b1"][e], x[q + "tv_b2"][e])
                      for e in range(E0)])
    m = "L1_ffn_"
    ew = np.concatenate([x[m + "w1"], x[m + "w2"].reshape(E, 2, 128, D).transpose(0, 2, 1, 3).reshape(E, 128, 256),
                         x[m + "b1"].reshape(E, 2, 128).transpose(0, 2, 1)], 2)[::-1]
    given = {
        "tok": x["x"].reshape(T), "consts": consts, "rows": rows, "cols": cols, "emb": x[t + "token_emb"],
        "vel_w2t": x[t + "vel_w2"].T, "a0": a0, "gfc1t": x[q + "gfc1_w"].T, "gfc2t": x[q + "gfc2_w"].T,
        "gfc2b": x[q + "gfc2_b"], "ffn": ffn, "a1": a1, "rw": x[m + "router_w"][:, ::-1],
        "rb": x[m + "router_b"][::-1], "ew": ew, "eb2": x[m + "b2"][::-1],
    }
    given = {k: np.ascontiguousarray(v) for k, v in given.items()}
    nc = bacc.Bacc("TRN2", target_bir_lowering=False, num_devices=1)
    args = [nc.dram_tensor("in_" + k, v.shape, mybir.dt.from_np(v.dtype), kind="ExternalInput").ap()
            for k, v in given.items()]
    comb = nc.dram_tensor("comb", (E, T), F32, kind="Internal").ap()
    out = nc.dram_tensor("out", (D, T), F32, kind="ExternalOutput").ap()
    vocabulary_tower(nc, *args, comb, out)
    r = run_bass_kernel_spmd(nc, [{"in_" + k: v for k, v in given.items()}], core_ids=[0])
    return np.ascontiguousarray(r.results[0]["out"].T).reshape(B, S, D)
```
